# Optimizing a Trainium2 kernel written in Bass

```python
import numpy as np
import jax
import jax.numpy as jnp

def _softmax(x, axis=-1):
    return jax.nn.softmax(x, axis=axis)

def _gelu(x):
    return jax.nn.gelu(x, approximate=True)

def _silu(x):
    return jax.nn.silu(x)

def _sigmoid(x):
    return jax.nn.sigmoid(x)

def _layernorm(x, axis=-1, eps=1e-05):
    m = jnp.mean(x, axis=axis, keepdims=True)
    v = jnp.var(x, axis=axis, keepdims=True)
    return (x - m) / jnp.sqrt(v + eps)

def _scatter_add(tgt, idx, src, axis=0):
    return tgt.at[idx].add(src)

def _segment_sum(src, seg, n):
    return jax.ops.segment_sum(src, seg, n)
kernel_name = 'mk_audio_tower_d1_tok_audfeat1024_r4_648c46'

def setup_inputs(seed: int=0):
    np.random.seed(seed)
    _w = jnp.asarray

    def _rec_inputs():
        import jax
        import jax.numpy as jnp
        _rk = jax.random.key(seed)
        x = -0.000392918 + 0.999932 * jax.random.normal(jax.random.fold_in(_rk, 1), (8, 375, 128), jnp.float32)
        return x
    x = _rec_inputs()

    def _L0_tok_setup():
        import jax, jax.numpy as jnp
        import numpy as np
        CONTEXT = 5
        DILATION = 1
        EPS = 1e-05
        key = jax.random.key(seed)
        ks = jax.random.split(key, 6)
        B, T, D, O = (32, 1024, 128, 256)
        K = D * CONTEXT
        x = jax.random.normal(ks[0], (B, T, D), dtype=jnp.float32)
        W = jax.random.normal(ks[1], (O, K), dtype=jnp.float32) * 0.02
        b = jnp.zeros((O,), dtype=jnp.float32)
        gamma = jnp.ones((O,), dtype=jnp.float32)
        beta = jnp.zeros((O,), dtype=jnp.float32)
        running_mean = jax.random.normal(ks[2], (O,), dtype=jnp.float32) * 0.1
        running_var = jax.random.uniform(ks[3], (O,), dtype=jnp.float32, minval=0.5, maxval=1.5)
        return {'x': x, 'W': W, 'b': b, 'gamma': gamma, 'beta': beta, 'running_mean': running_mean, 'running_var': running_var}
    _L0_tok_all = _L0_tok_setup()
    _L0_tok_in = {k: v for k, v in _L0_tok_all.items() if k in ('W', 'b', 'gamma', 'beta', 'running_mean', 'running_var')}
    del _L0_tok_all

    def _L0_attn_setup():
        import jax, jax.numpy as jnp
        import numpy as np
        import math
        B, N, D, H = (1, 1024, 256, 16)
        HS = D // H
        NEG_INF = -10000.0
        key = jax.random.key(seed)
        k1, k2, k3, k4, k5 = jax.random.split(key, 5)
        return {'encodings': jax.random.normal(k1, (B, N, D), dtype=jnp.float32), 'attn_W': jax.random.normal(k2, (D, 3 * D), dtype=jnp.float32) * 0.02, 'attn_b': jax.random.normal(k3, (3 * D,), dtype=jnp.float32) * 0.02, 'out_W': jax.random.normal(k4, (D, D), dtype=jnp.float32) * 0.02, 'out_b': jax.random.normal(k5, (D,), dtype=jnp.float32) * 0.02}
    _L0_attn_all = _L0_attn_setup()
    _L0_attn_in = {k: v for k, v in _L0_attn_all.items() if k in ('attn_W', 'attn_b', 'out_W', 'out_b')}
    del _L0_attn_all

    def _L0_ffn_setup():
        import jax, jax.numpy as jnp
        import numpy as np
        DIM = 256
        HID = 128
        N_EXPERTS = 16
        TOP_K = 4
        key = jax.random.key(seed)
        ks = jax.random.split(key, 8)
        s = 0.02
        x = jax.random.normal(ks[0], (2, 256, DIM), dtype=jnp.float32)
        gate_w = jax.random.normal(ks[1], (N_EXPERTS, DIM), dtype=jnp.float32) * s
        w1 = jax.random.normal(ks[2], (N_EXPERTS, HID, DIM), dtype=jnp.float32) * s
        w3 = jax.random.normal(ks[3], (N_EXPERTS, HID, DIM), dtype=jnp.float32) * s
        w2 = jax.random.normal(ks[4], (N_EXPERTS, DIM, HID), dtype=jnp.float32) * s
        sw1 = jax.random.normal(ks[5], (HID, DIM), dtype=jnp.float32) * s
        sw3 = jax.random.normal(ks[6], (HID, DIM), dtype=jnp.float32) * s
        sw2 = jax.random.normal(ks[7], (DIM, HID), dtype=jnp.float32) * s
        return {'x': x, 'gate_w': gate_w, 'w1': w1, 'w3': w3, 'w2': w2, 'sw1': sw1, 'sw3': sw3, 'sw2': sw2}
    _L0_ffn_all = _L0_ffn_setup()
    _L0_ffn_in = {k: v for k, v in _L0_ffn_all.items() if k in ('gate_w', 'w1', 'w3', 'w2', 'sw1', 'sw3', 'sw2')}
    del _L0_ffn_all
    return {'x': x, 'L0_tok_W': _L0_tok_in['W'], 'L0_tok_b': _L0_tok_in['b'], 'L0_tok_gamma': _L0_tok_in['gamma'], 'L0_tok_beta': _L0_tok_in['beta'], 'L0_tok_running_mean': _L0_tok_in['running_mean'], 'L0_tok_running_var': _L0_tok_in['running_var'], 'L0_attn_attn_W': _L0_attn_in['attn_W'], 'L0_attn_attn_b': _L0_attn_in['attn_b'], 'L0_attn_out_W': _L0_attn_in['out_W'], 'L0_attn_out_b': _L0_attn_in['out_b'], 'L0_ffn_gate_w': _L0_ffn_in['gate_w'], 'L0_ffn_w1': _L0_ffn_in['w1'], 'L0_ffn_w3': _L0_ffn_in['w3'], 'L0_ffn_w2': _L0_ffn_in['w2'], 'L0_ffn_sw1': _L0_ffn_in['sw1'], 'L0_ffn_sw3': _L0_ffn_in['sw3'], 'L0_ffn_sw2': _L0_ffn_in['sw2']}

def reference(x, L0_tok_W, L0_tok_b, L0_tok_gamma, L0_tok_beta, L0_tok_running_mean, L0_tok_running_var, L0_attn_attn_W, L0_attn_attn_b, L0_attn_out_W, L0_attn_out_b, L0_ffn_gate_w, L0_ffn_w1, L0_ffn_w3, L0_ffn_w2, L0_ffn_sw1, L0_ffn_sw3, L0_ffn_sw2):
    import jax
    import jax.numpy as jnp

    def _L0_tok_ref(x, W, b, gamma, beta, running_mean, running_var):
        import jax, jax.numpy as jnp
        import numpy as np
        CONTEXT = 5
        DILATION = 1
        EPS = 1e-05
        B, T, D = x.shape
        Tp = T - DILATION * (CONTEXT - 1)
        idx = jnp.arange(Tp)[:, None] + jnp.arange(CONTEXT)[None, :] * DILATION
        win = x[:, idx, :].reshape(B, Tp, CONTEXT * D)
        h = jnp.einsum('btk,ok->bto', win, W) + b
        h = jax.nn.relu(h)
        h = gamma * (h - running_mean) * jax.lax.rsqrt(running_var + EPS) + beta
        return h

    def _L0_attn_ref(encodings, attn_W, attn_b, out_W, out_b):
        import jax, jax.numpy as jnp
        import numpy as np
        import math
        B, N, D, H = (1, 1024, 256, 16)
        HS = D // H
        NEG_INF = -10000.0
        b, n, d = encodings.shape
        qkv = encodings @ attn_W + attn_b
        qkv = qkv.reshape(b, n, H, 3 * HS).transpose(0, 2, 1, 3)
        q, k, v = jnp.split(qkv, 3, axis=-1)
        scores = jnp.einsum('bhki,bhqi->bhkq', k, q) / math.sqrt(HS)
        mask = jnp.arange(n)[:, None] <= jnp.arange(n)[None, :]
        scores = jnp.where(mask, scores, jnp.float32(NEG_INF))
        prob = jax.nn.softmax(scores, axis=2)
        combined = jnp.einsum('bhkq,bhkl->bhql', prob, v)
        out = combined.transpose(0, 2, 1, 3).reshape(b, n, d)
        return out @ out_W + out_b

    def _L0_ffn_ref(x, gate_w, w1, w3, w2, sw1, sw3, sw2):
        import jax, jax.numpy as jnp
        import numpy as np
        DIM = 256
        HID = 128
        N_EXPERTS = 16
        TOP_K = 4
        bsz, seq_len, dim = x.shape
        xf = x.reshape(-1, dim)
        T = xf.shape[0]
        probs = jax.nn.softmax(xf @ gate_w.T, axis=-1)
        top_w, top_idx = jax.lax.top_k(probs, TOP_K)
        top_w = top_w / jnp.sum(top_w, axis=-1, keepdims=True)
        rows = jnp.arange(T)[:, None]
        combine = jnp.zeros((T, N_EXPERTS), dtype=xf.dtype).at[rows, top_idx].set(top_w)
        h1 = jnp.einsum('td,ehd->teh', xf, w1)
        h3 = jnp.einsum('td,ehd->teh', xf, w3)
        act = jax.nn.silu(h1) * h3
        eout = jnp.einsum('teh,edh->ted', act, w2)
        moe_out = jnp.einsum('ted,te->td', eout, combine)
        shared = jax.nn.silu(xf @ sw1.T) * (xf @ sw3.T) @ sw2.T
        return (moe_out + shared).reshape(bsz, seq_len, dim)
    h = _L0_tok_ref(x, L0_tok_W, L0_tok_b, L0_tok_gamma, L0_tok_beta, L0_tok_running_mean, L0_tok_running_var)
    h = h + _L0_attn_ref(_layernorm(h, axis=-1), L0_attn_attn_W, L0_attn_attn_b, L0_attn_out_W, L0_attn_out_b)
    h = h + _L0_ffn_ref(_layernorm(h, axis=-1), L0_ffn_gate_w, L0_ffn_w1, L0_ffn_w3, L0_ffn_w2, L0_ffn_sw1, L0_ffn_sw3, L0_ffn_sw2)
    return h

_drawn_inputs = setup_inputs


def setup_inputs(seed=0):
    import zlib

    import numpy as np

    out = dict(_drawn_inputs(seed))
    spreads = {'L0_tok_b': (0.0, 0.1), 'L0_tok_gamma': (1.0, 0.2), 'L0_tok_beta': (0.0, 0.1)}
    factors = {'L0_attn_attn_b': 3.929,
     'L0_ffn_gate_w': 5.222,
     'L0_ffn_w1': 4.656,
     'L0_ffn_w3': 4.6,
     'L0_ffn_w2': 4.614,
     'L0_ffn_sw1': 4.955,
     'L0_ffn_sw3': 4.859,
     'L0_ffn_sw2': 4.836}
    for name, (base, spread) in spreads.items():
        noise = np.random.default_rng([zlib.crc32(name.encode()), seed]).standard_normal(out[name].shape)
        drawn = base * np.exp(spread * noise) if base else spread * noise
        out[name] = jnp.asarray(drawn.astype(out[name].dtype))
    for name, factor in factors.items():
        out[name] = (out[name] * factor).astype(out[name].dtype)
    return out
```

```python
from contextlib import ExitStack

import numpy as np

import concourse.bass as bass
from concourse import mybir

B, T_IN, FEAT = 8, 375, 128
CONTEXT = 5
T = T_IN - (CONTEXT - 1)
D = 256
KC = D // 128
NT = -(-T // 128)
TP = NT * 128
ROWS = [min(128, T - 128 * t) for t in range(NT)]
H, HS = 16, 16
HH = H // 2
GROUPS = H // 4
PARTS = 3
Q_PART = [0, 0, 0, 1, 1, 2]
K_PART = [0, 1, 2, 0, 1, 0]
SROWS = HS * len(Q_PART)
XROWS = SROWS + PARTS
E, HID, TOPK = 16, 128, 4
N_WEIGHTS = 5
NE = E + 1
ORDER = [E] + list(range(E))
EPS = 1e-5
NEG = -1.0e30
VW = 32

F32 = mybir.dt.float32
BF16 = mybir.dt.bfloat16
U32 = mybir.dt.uint32
ALU = mybir.AluOpType
ACT = mybir.ActivationFunctionType
AX = mybir.AxisListType

WORK = ([("conv", t, "F") for t in range(NT)] + [("onorm", 0, "E")] + [("n1t", t, "F") for t in range(NT)]
        + [("mt", 0, "M"), ("onorm", 1, "E"), ("qk", 0, "F"), ("qk", 1, "F"), ("onorm", 2, "E"), ("qk", 2, "F"),
           ("qk", 3, "F"), ("onorm", 3, "E"), ("v", 0, "F"), ("ot", 0, "E"), ("ot", 1, "E"), ("mt", 1, "M")]
        + [("out", t, "E") for t in range(NT)] + [("v", 1, "F"), ("v", 2, "F")])
PER_BATCH = {"conv": NT, "n1t": NT, "qk": 4, "v": NT, "onorm": GROUPS, "ot": KC, "mt": 2, "out": NT}
AHEAD = {"F": 2, "M": 1, "E": 0}


def stages(s):
    return {"F": s + 2 < B, "M": 0 <= s + 1 < B, "E": 0 <= s < B}


def work_plan():
    plan, held = {}, [None, None]
    for s in range(-2, B):
        n = sum(stages(s)[stage] for _, _, stage in WORK) % 2
        for name, k, stage in WORK:
            if stages(s)[stage]:
                was = held[n % 2]
                plan[s, name, k] = (n % 2, was and (was[0], was[1], was[2] - s))
                held[n % 2] = (name, k, s + AHEAD[stage])
                n += 1
    return plan


PLAN = work_plan()
LOOPED = range(0, B - 2)
for _s in LOOPED:
    for _u in WORK:
        assert PLAN[_s, _u[0], _u[1]] == PLAN[0, _u[0], _u[1]]


def build(nc, xT_d, convw_d, vec_d, qkb_d, wqkv_d, wo_d, gate_d, w13_d, w2_d, out_d):
    with ExitStack() as ctx:
        def sb(name, shape, dt=F32):
            return ctx.enter_context(nc.sbuf_tensor(name, shape, dt))

        def ps(name):
            return ctx.enter_context(nc.psum_tensor(name, [128, 2, 512], F32))

        def sem(name):
            return ctx.enter_context(nc.semaphore(name))

        qk_scratch = nc.dram_tensor("qk_scratch", (2, 2, PARTS, 128, T), BF16, kind="Internal").ap()
        n2_scratch = nc.dram_tensor("n2_scratch", (B * T, D), F32, kind="Internal").ap()

        convw = sb("convw", [128, CONTEXT, D])
        vec = sb("vec", [128, 7, D])
        conv_b, gamma, beta, mean, var, out_b, v_b = [vec[:, i, :] for i in range(7)]
        bn_scale = sb("bn_scale", [128, D])
        bn_shift = sb("bn_shift", [128, D])
        neg_half = sb("neg_half", [128, D])
        qkb = sb("qkb", [128, 2, KC])
        wqkv = sb("wqkv", [128, KC, 3, D])
        wo = sb("wo", [128, KC, D])
        gate = sb("gate", [128, KC, E])
        ident = sb("ident", [128, 128])
        ident_bf = sb("ident_bf", [128, 128], BF16)
        mask_bf = sb("mask_bf", [128, 2, 128], BF16)
        iota_e = sb("iota_e", [128, E])

        xT = sb("xT", [128, T_IN])
        u1 = sb("u1", [128, 2, D])
        u2 = sb("u2", [128, 2, D])
        hcur = sb("hcur", [128, NT, D])
        stats = sb("stats", [128, NT, 6])
        mv = sb("mv", [128, NT, 2])
        rstd = sb("rstd", [128, NT])
        n1 = sb("n1", [128, NT, D])
        n1T = sb("n1T", [128, KC, TP])
        resid = sb("resid", [128, B * NT, D])
        qkp = sb("qkp", [128, 2, PARTS, KC, T], BF16)
        r1 = sb("r1", [128, 2, T])
        V = [sb(f"V{p}", [128, NT, H, VW]) for p in range(2)]
        nmax = sb("nmax", [128, NT, H])
        nm_res = sb("nm_res", [128, NT, HH])
        nm_parts = sb("nm_parts", [128, NT, PARTS, HH], BF16)
        nmT = sb("nmT", [PARTS * HH, TP], BF16)
        oT_raw = sb("oT_raw", [128, 2, TP])
        rden = sb("rden", [128, NT, 4])
        o = sb("o", [128, NT, D])
        oT = sb("oT", [128, KC, TP])
        stats2 = sb("stats2", [128, NT, 6])
        mv2 = sb("mv2", [128, NT, 2])
        rstd2 = sb("rstd2", [128, NT])
        n2 = sb("n2", [128, NT, D])

        early = ExitStack()

        def sbe(name, shape, dt=F32):
            return early.enter_context(nc.sbuf_tensor(name, shape, dt))

        Qs = [sbe(f"Qs{p}", [XROWS, H, TP], BF16) for p in range(2)]
        Ks = [sbe(f"Ks{p}", [XROWS, H, TP], BF16) for p in range(2)]
        P = sbe("P", [128, 8, 2, T])
        early.close()
        w13 = sb("w13", [128, KC, NE, 2 * HID])
        w2 = sb("w2", [128, NE, D])
        nb = sb("nb", [128, NT, D])
        n2T = sb("n2T", [128, KC, T])
        logit = sb("logit", [128, NT, E])
        top8 = sb("top8", [128, NT, 8])
        idx8 = sb("idx8", [128, NT, 8], U32)
        idxf = sb("idxf", [128, NT, TOPK])
        neg_top = sb("neg_top", [128, NT])
        e4 = sb("e4", [128, NT, TOPK])
        esum = sb("esum", [128, NT])
        w4 = sb("w4", [128, NT, TOPK])
        onehot = sb("onehot", [128, TOPK, E])
        combine = sb("combine", [128, NT, E])
        silu = sb("silu", [128, 2, T])
        hidden = sb("hidden", [128, 2, T])
        acc = sb("acc", [128, NT, D])

        work, ex, mx, pv = ps("work"), ps("ex"), ps("mx"), ps("pv")

        const_in, vec_in, pool_const, prep = sem("const_in"), sem("vec_in"), sem("pool_const"), sem("prep")
        dve_const, x_in = sem("dve_const"), sem("x_in")
        conv_ready, conv_chain, bn_ready, h_ready = sem("conv_ready"), sem("conv_chain"), sem("bn_ready"), sem("h_ready")
        ln_chain, rstd_ready, n1_ready = sem("ln_chain"), sem("rstd_ready"), sem("n1_ready")
        n1t_ready, qk_ready, p1_ready = sem("n1t_ready"), sem("qk_ready"), sem("p1_ready")
        p2_done, parts_ready = sem("p2_done"), sem("parts_ready")
        qk_stored = [sem(f"qk_stored{i}") for i in range(2)]
        stack_in = [sem(f"stack_in{i}") for i in range(2)]
        v_mm_ready = sem("v_mm_ready")
        mxa_ready, mxb_ready, mxa_done, mxb_done = sem("mxa_ready"), sem("mxb_ready"), sem("mxa_done"), sem("mxb_done")
        nm_chain, nmt_ready, = sem("nm_chain"), sem("nmt_ready")
        nmax_in = [sem(f"nmax_in{i}") for i in range(2)]
        ex_ready, exp_done, masked = sem("ex_ready"), sem("exp_done"), sem("masked")
        pv_ready, raw_ready, rawt_ready, rden_ready = sem("pv_ready"), sem("raw_ready"), sem("rawt_ready"), sem("rden_ready")
        ott_ready, out_ready = sem("ott_ready"), sem("out_ready")
        ln2_chain, rstd2_ready, n2_ready, n2_free = sem("ln2_chain"), sem("rstd2_ready"), sem("n2_ready"), sem("n2_free")
        resid_ready, waited = sem("resid_ready"), sem("waited")
        w_in, n2_in, n2t_ready, n2T_copied = sem("w_in"), sem("n2_in"), sem("n2t_ready"), sem("n2T_copied")
        logits_ready, logits_read, rt_chain, top_ready = sem("logits_ready"), sem("logits_read"), sem("rt_chain"), sem("top_ready")
        e4_ready, cmb_chain, hid_ready, silu_ready = sem("e4_ready"), sem("cmb_chain"), sem("hid_ready"), sem("silu_ready")
        act_ready, eo_ready, acc_done, acc_free = sem("act_ready"), sem("eo_ready"), sem("acc_done"), sem("acc_free")
        evac = {name: sem(f"{name}_evacuated") for name in PER_BATCH}

        def wait(eng, s, value):
            if not isinstance(value, int) or value > 0:
                eng.wait_ge(s, value)

        def wait_apart(eng, s, value):
            wait(eng, s, value)
            if not isinstance(value, int):
                eng.sem_inc(waited, 1)

        def plan(s, name, k):
            return PLAN[s if isinstance(s, int) else 0, name, k]

        def steps(eng, step):
            step(-2, 0, True, False, False)
            step(-1, 1, True, True, False)
            with eng.Fori(0, (B - 2) // 2) as pair:
                step(2 * pair, 0, True, True, True)
                step(2 * pair + 1, 1, True, True, True)
            step(B - 2, 0, False, True, True)
            step(B - 1, 1, False, False, True)

        block = ctx.enter_context(nc.Block())

        @block.sync
        def _(sp):
            sp.dma_start(vec[:].rearrange("p a d -> p (a d)"), vec_d.partition_broadcast(128)).then_inc(vec_in, 16)
            for dst, src in ((convw, convw_d), (wqkv, wqkv_d), (qkb, qkb_d), (wo, wo_d), (gate, gate_d)):
                sp.dma_start(dst[:], src).then_inc(const_in, 16)

            def step(s, p, F, M, X):
                f, m = s + 2, s + 1
                if F:
                    wait_apart(sp, conv_ready, NT * f)
                    sp.dma_start(xT[:], xT_d[bass.ds(f, 1)].rearrange("a p t -> (a p) t")).then_inc(x_in, 16)
                for half in range(2):
                    if M:
                        wait_apart(sp, evac["mt"], 2 * m + half + 1)
                        for i in range(PARTS):
                            sp.dma_start(Qs[1 - p][SROWS + i:SROWS + i + 1, half * HH:(half + 1) * HH, 0:T],
                                         nmT[i * HH:(i + 1) * HH, 0:T]).then_inc(nmax_in[half], 16)
                    if F:
                        wait_apart(sp, parts_ready, 4 * f + 2 * half + 2)
                        wait_apart(sp, stack_in[half], 16 * 12 * f)
                        sp.dma_start(qk_scratch[half].rearrange("q a p t -> p q a t"),
                                     qkp[:, :, :, half, :]).then_inc(qk_stored[half], 16)
                        if X:
                            wait_apart(sp, ex_ready, H * s + (half + 1) * HH)
                        wait_apart(sp, qk_stored[half], 16 * (f + 1))
                        for qk, (stack, part) in enumerate(((Qs, Q_PART), (Ks, K_PART))):
                            for c in range(len(part)):
                                sp.dma_start(stack[p][HS * c:HS * (c + 1), half * HH:(half + 1) * HH, 0:T],
                                             qk_scratch[half, qk, part[c]].rearrange("(h d) t -> d h t", d=HS)
                                             ).then_inc(stack_in[half], 16)
                if X:
                    for t in range(NT):
                        wait_apart(sp, n2_ready, NT * s + t + 1)
                        sp.dma_start(n2_scratch[bass.ds(T * s + 128 * t, ROWS[t])], n2[0:ROWS[t], t, :]).then_inc(n2_free, 16)
            steps(sp, step)

            sp.wait_ge(evac["mt"], 2 * B)
            sp.wait_ge(ex_ready, H * B)
            sp.wait_ge(pv_ready, GROUPS * B)
            sp.dma_start(w13[:], w13_d).then_inc(w_in, 16)
            sp.dma_start(w2[:], w2_d).then_inc(w_in, 16)
            sp.wait_ge(n2_free, 16 * NT * B + 1)

            def load(b):
                for t in range(NT):
                    sp.dma_start(nb[0:ROWS[t], t, :], n2_scratch[bass.ds(T * b + 128 * t, ROWS[t])]).then_inc(n2_in, 16)

            def store(b):
                wait_apart(sp, acc_done, NE * (b + 1) + 1)
                for t in range(NT):
                    sp.dma_start(out_d[bass.ds(T * b + 128 * t, ROWS[t])], acc[0:ROWS[t], t, :]).then_inc(acc_free, 16)

            load(0)
            with sp.Fori(0, B - 1) as b:
                wait_apart(sp, n2t_ready, KC * (b + 1))
                load(b + 1)
                store(b)
            store(B - 1)
            sp.wait_ge(acc_free, 16 * NT * B + 1)

        @block.tensor
        def _(pe):
            pe.wait_ge(const_in, 16 * N_WEIGHTS)
            pe.wait_ge(pool_const, 4)
            pe.wait_ge(prep, 1)
            pe.wait_ge(dve_const, 3)

            def step(s, p, F, M, X):
                f, m = s + 2, s + 1

                def bank(name, k):
                    b, was = plan(s, name, k)
                    if was is not None:
                        wait(pe, evac[was[0]], PER_BATCH[was[0]] * (s + was[2]) + was[1] + 1)
                    return work[:, b, :]

                def maxima_scores(h):
                    if h % HH == 0:
                        pe.wait_ge(stack_in[h // HH], 16 * 12 * (m + 1))
                    q, k = Qs[1 - p], Ks[1 - p]
                    wait(pe, mxa_done, H * m + h)
                    pe.matmul(mx[:, 0, 256:T], ident_bf[:], mask_bf[:, 0, 0:T - 256], start=True, stop=False, skip_group_check=True)
                    pe.matmul(mx[:, 0, 0:T], q[0:SROWS, h, 256:TP], k[0:SROWS, h, 0:T], start=False, stop=True,
                              skip_group_check=True).then_inc(mxa_ready, 1)
                    wait(pe, mxb_done, H * m + h)
                    pe.matmul(mx[:, 1, :].rearrange("p (a c) -> p a c", a=2)[:, :, 0:128], ident_bf[:], mask_bf[:], start=True, stop=False, skip_group_check=True)
                    pe.matmul(mx[:, 1, 0:128], q[0:SROWS, h, 0:128], k[0:SROWS, h, 0:128], start=False, stop=False, skip_group_check=True)
                    pe.matmul(mx[:, 1, 128:384], q[0:SROWS, h, 128:256], k[0:SROWS, h, 0:256], start=False, stop=True,
                              skip_group_check=True).then_inc(mxb_ready, 1)

                def exp_scores(h):
                    if h % HH == 0:
                        pe.wait_ge(nmax_in[h // HH], 16 * PARTS * (s + 1))
                    q, k = Qs[p], Ks[p]
                    if h:
                        pe.wait_ge(exp_done, H * s + h)
                    pe.matmul(ex[:, 0, 0:T], k[:, h, 0:128], q[:, h, 0:T], start=True, stop=True)
                    pe.matmul(ex[:, 1, 0:T - 128], k[:, h, 128:256], q[:, h, 128:T], start=True, stop=True)
                    pe.matmul(ex[:, 1, T - 128:T], k[:, h, 256:TP], q[:, h, 256:TP], start=True, stop=True).then_inc(ex_ready, 1)

                def weigh_values(g):
                    pe.wait_ge(masked, H * s + 4 * g + 4)
                    if g == 0:
                        pe.wait_ge(evac["v"], NT * (s + 1))
                    for kt in range(NT):
                        for j in range(4):
                            h = 4 * g + j
                            q0 = 128 * kt
                            probs = P[:, h % 8, 0, :] if kt == 0 else P[:, h % 8, 1, 0:T - 128] if kt == 1 \
                                else P[:, h % 8, 1, T - 128:T - 128 + T - 256]
                            mm = pe.matmul(pv[32 * j:32 * j + VW, g % 2, q0:T], V[p][:, kt, h, :], probs,
                                           start=(kt == 0), stop=(kt == NT - 1))
                    mm.then_inc(pv_ready, 1)

                def transpose_raw(g):
                    w = bank("onorm", g)
                    pe.wait_ge(raw_ready, GROUPS * s + g + 1)
                    for t in range(NT):
                        mm = pe.transpose(w[:, 128 * t:128 * (t + 1)], oT_raw[:, g % 2, 128 * t:128 * (t + 1)], ident[:])
                    mm.then_inc(rawt_ready, 1)

                def conv(t):
                    w = bank("conv", t)
                    if t == 0:
                        pe.wait_ge(x_in, 16 * (f + 1))
                    for c in range(CONTEXT):
                        mm = pe.matmul(w[0:ROWS[t], 0:D], xT[:, 128 * t + c:128 * t + c + ROWS[t]], convw[:, c, :],
                                       start=(c == 0), stop=(c == CONTEXT - 1))
                    mm.then_inc(conv_ready, 1)

                def transpose_n1(t):
                    w = bank("n1t", t)
                    pe.wait_ge(n1_ready, NT * f + t + 1)
                    for c in range(KC):
                        mm = pe.transpose(w[:, 128 * c:128 * c + ROWS[t]], n1[0:ROWS[t], t, 128 * c:128 * (c + 1)],
                                          ident[0:ROWS[t], 0:ROWS[t]])
                    mm.then_inc(n1t_ready, 1)

                def project_qk(u):
                    w = bank("qk", u)
                    half, qk = u // 2, u % 2
                    if u == 0:
                        pe.wait_ge(evac["n1t"], NT * (f + 1))
                    for c in range(KC):
                        mm = pe.matmul(w[:, 0:T], wqkv[:, c, qk, 128 * half:128 * (half + 1)], n1T[:, c, 0:T],
                                       start=(c == 0), stop=(c == KC - 1))
                    mm.then_inc(qk_ready, 1)

                def project_v(t):
                    w = bank("v", t)
                    for c in range(KC):
                        mm = pe.matmul(w[0:ROWS[t], 0:D], n1T[:, c, 128 * t:128 * t + ROWS[t]], wqkv[:, c, 2, :],
                                       start=(c == 0), stop=(c == KC - 1))
                    mm.then_inc(v_mm_ready, 1)

                def transpose_maxima(half):
                    w = bank("mt", half)
                    pe.wait_ge(nm_chain, 8 * m + 4 * half + 4)
                    for t in range(NT):
                        mm = pe.transpose(w.bitcast(BF16)[0:PARTS * HH, 128 * t:128 * (t + 1)],
                                          nm_parts[:, t, :, :].rearrange("p a h -> p (a h)"), ident_bf[:])
                    mm.then_inc(nmt_ready, 1)

                def transpose_o(c):
                    w = bank("ot", c)
                    if c == 0:
                        pe.wait_ge(evac["onorm"], GROUPS * (s + 1))
                    for t in range(NT):
                        mm = pe.transpose(w[:, 128 * t:128 * (t + 1)], o[:, t, 128 * c:128 * (c + 1)], ident[:])
                    mm.then_inc(ott_ready, 1)

                def project_out(t):
                    w = bank("out", t)
                    if t == 0:
                        pe.wait_ge(evac["ot"], KC * (s + 1))
                    for c in range(KC):
                        mm = pe.matmul(w[0:ROWS[t], 0:D], oT[:, c, 128 * t:128 * t + ROWS[t]], wo[:, c, :],
                                       start=(c == 0), stop=(c == KC - 1))
                    mm.then_inc(out_ready, 1)

                for h in range(H):
                    if M:
                        maxima_scores(h)
                    if X:
                        exp_scores(h)
                    if F and 2 <= h < 5:
                        conv(h - 2)
                    if X and h == 5:
                        transpose_raw(0)
                    if F and 6 <= h < 9:
                        transpose_n1(h - 6)
                    if M and h == 9:
                        transpose_maxima(0)
                    if X and h == 9:
                        transpose_raw(1)
                    if F and h in (10, 11):
                        project_qk(h - 10)
                    if X and h in (4, 8, 12):
                        weigh_values(h // 4 - 1)
                    if X and h == 13:
                        transpose_raw(2)
                    if F and h == 14:
                        project_qk(2)
                if F:
                    project_qk(3)
                if X:
                    weigh_values(3)
                    transpose_raw(3)
                if F:
                    project_v(0)
                if X:
                    transpose_o(0)
                    transpose_o(1)
                if M:
                    transpose_maxima(1)
                if X:
                    for t in range(NT):
                        project_out(t)
                if F:
                    project_v(1)
                    project_v(2)
            steps(pe, step)

            pe.wait_ge(w_in, 16 * 2)
            with pe.Fori(0, B) as b:
                pe.wait_ge(acc_done, NE * b + 1)
                pe.wait_ge(n2_in, 16 * NT * (b + 1))
                for c in range(KC):
                    for t in range(NT):
                        mm = pe.transpose(work[:, c, 128 * t:128 * t + ROWS[t]], nb[0:ROWS[t], t, 128 * c:128 * (c + 1)],
                                          ident[0:ROWS[t], 0:ROWS[t]])
                    mm.then_inc(n2t_ready, 1)
                pe.wait_ge(n2T_copied, KC * (b + 1))
                for t in range(NT):
                    for c in range(KC):
                        mm = pe.matmul(work[0:ROWS[t], 0, E * t:E * (t + 1)], n2T[:, c, 128 * t:128 * t + ROWS[t]],
                                       gate[:, c, :], start=(c == 0), stop=(c == KC - 1))
                mm.then_inc(logits_ready, 1)

                def expert_out(i):
                    pe.wait_ge(act_ready, NE * b + i + 1)
                    pe.wait_ge(acc_done, NE * b + max(i - 1, 0) + 1)
                    eo = (pv, work)[i % 2]
                    if i == 1:
                        pe.wait_ge(logits_read, b + 1)
                    for t in range(NT):
                        mm = pe.matmul(eo[0:ROWS[t], t // 2, 256 * (t % 2):256 * (t % 2) + D],
                                       hidden[:, i % 2, 128 * t:128 * t + ROWS[t]], w2[:, ORDER[i], :], start=True, stop=True)
                    mm.then_inc(eo_ready, 1)

                for i in range(NE):
                    hb = (ex, mx)[i % 2]
                    if i >= 2:
                        pe.wait_ge(act_ready, NE * b + i - 1)
                    for j in range(2):
                        for c in range(KC):
                            mm = pe.matmul(hb[:, j, 0:T], w13[:, c, ORDER[i], HID * j:HID * (j + 1)], n2T[:, c, 0:T],
                                           start=(c == 0), stop=(c == KC - 1))
                    mm.then_inc(hid_ready, 1)
                    if i:
                        expert_out(i - 1)
                expert_out(NE - 1)

        @block.scalar
        def _(act):
            act.wait_ge(prep, 1)

            def step(s, p, F, M, X):
                f, m = s + 2, s + 1

                def bank(name, k):
                    return work[:, plan(s, name, k)[0], :]

                def exponentials(h):
                    act.wait_ge(ex_ready, H * s + h + 1)
                    if h >= 8:
                        act.wait_ge(pv_ready, GROUPS * s + h // 4 - 1)
                    nc.scalar.activation(P[:, h % 8, :, :], ex[:, :, 0:T], ACT.Exp).then_inc(exp_done, 1)

                def copy_raw(g):
                    act.wait_ge(pv_ready, GROUPS * s + g + 1)
                    nc.scalar.activation(oT_raw[:, g % 2, 0:T], pv[:, g % 2, 0:T], ACT.Copy).then_inc(raw_ready, 1)

                def copy_n1T(t):
                    act.wait_ge(n1t_ready, NT * f + t + 1)
                    w = bank("n1t", t).rearrange("p (c n) -> p c n", n=128)
                    nc.scalar.activation(n1T[:, :, 128 * t:128 * t + ROWS[t]], w[:, 0:KC, 0:ROWS[t]],
                                         ACT.Copy).then_inc(evac["n1t"], 1)

                def first_part(u):
                    half, qk = u // 2, u % 2
                    act.wait_ge(qk_ready, 4 * f + u + 1)
                    wait(act, qk_stored[half], 16 * f)
                    nc.scalar.activation(qkp[:, qk, 0, half, :], bank("qk", u)[:, 0:T], ACT.Identity,
                                         bias=qkb[:, qk, half:half + 1]).then_inc(p1_ready, 1)

                def copy_maxima(half):
                    act.wait_ge(nmt_ready, 2 * m + half + 1)
                    wait(act, nmax_in[1 - half], 16 * PARTS * (m + half))
                    nc.scalar.activation(nmT[:, 0:T], bank("mt", half).bitcast(BF16)[0:PARTS * HH, 0:T],
                                         ACT.Copy).then_inc(evac["mt"], 1)

                def copy_oT(c):
                    act.wait_ge(ott_ready, KC * s + c + 1)
                    nc.scalar.activation(oT[:, c, :], bank("ot", c)[:, 0:TP], ACT.Copy).then_inc(evac["ot"], 1)

                for h in range(H):
                    if X:
                        exponentials(h)
                    if F and 6 <= h < 9:
                        copy_n1T(h - 6)
                    if M and h == 9:
                        copy_maxima(0)
                    if F and h in (10, 11):
                        first_part(h - 10)
                    if X and h in (4, 8, 12):
                        copy_raw(h // 4 - 1)
                    if F and h == 14:
                        first_part(2)
                if F:
                    first_part(3)
                if X:
                    copy_raw(3)
                    copy_oT(0)
                    copy_oT(1)
                if M:
                    copy_maxima(1)
            steps(act, step)

            with act.Fori(0, B) as b:
                for c in range(KC):
                    act.wait_ge(n2t_ready, KC * b + c + 1)
                    nc.scalar.activation(n2T[:, c, 0:T], work[:, c, 0:T], ACT.Copy).then_inc(n2T_copied, 1)
                for t in range(NT):
                    act.wait_ge(top_ready, NT * b + t + 1)
                    r = ROWS[t]
                    nc.scalar.activation(e4[0:r, t, :], top8[0:r, t, 0:TOPK], ACT.Exp, bias=neg_top[0:r, t:t + 1],
                                         accum_out=esum[0:r, t:t + 1]).then_inc(e4_ready, 1)
                for i in range(NE):
                    hb = (ex, mx)[i % 2]
                    act.wait_ge(hid_ready, NE * b + i + 1)
                    if i >= 2:
                        act.wait_ge(act_ready, NE * b + i - 1)
                    nc.scalar.activation(silu[:, i % 2, :], hb[:, 0, 0:T], ACT.Silu).then_inc(silu_ready, 1)

        @block.vector
        def _(dve):
            nc.vector.memset(oT_raw[:, :, T:TP], 1.0)
            nc.vector.memset(n2[:, 0, 0:1], 0.0).then_inc(n2_free, 1)
            for stack in (*Qs, *Ks):
                nc.vector.memset(stack[:, :, T:TP], 0.0)
            nc.vector.memset(V[0][:], 0.0).then_inc(dve_const, 1)
            nc.vector.memset(V[1][:], 0.0).then_inc(dve_const, 1)
            dve.wait_ge(dve_const, 2)
            for p in range(2):
                nc.vector.memset(V[p][:, :, :, HS:HS + 1], 1.0)
                nc.vector.memset(Ks[p][SROWS:XROWS, :, :], 1.0)
            dve.wait_ge(const_in, 16 * N_WEIGHTS)
            nc.vector.tensor_scalar(wqkv[:, :, 0, :], wqkv[:, :, 0, :], HS ** -0.5, None, ALU.mult)
            nc.vector.tensor_scalar(qkb[:, 0, :], qkb[:, 0, :], HS ** -0.5, None, ALU.mult).then_inc(prep, 1)
            dve.wait_ge(pool_const, 8)
            nc.vector.tensor_copy(ident_bf[:], ident[:]).then_inc(dve_const, 1)
            nc.vector.tensor_tensor(bn_scale[:], gamma, bn_scale[:], ALU.mult).then_inc(dve_const, 1)
            dve.wait_ge(dve_const, 4)
            nc.vector.tensor_tensor(bn_shift[:], mean, bn_scale[:], ALU.mult).then_inc(dve_const, 1)
            dve.wait_ge(dve_const, 5)
            nc.vector.tensor_tensor(bn_shift[:], beta, bn_shift[:], ALU.subtract).then_inc(dve_const, 1)

            def step(s, p, F, M, X):
                f, m = s + 2, s + 1

                def bank(name, k):
                    return work[:, plan(s, name, k)[0], :]

                def maxima(h):
                    dve.wait_ge(mxa_ready, H * m + h + 1)
                    nc.vector.tensor_reduce(nmax[:, 2, h:h + 1], mx[:, 0, 0:T], AX.X, ALU.max, negate=True).then_inc(mxa_done, 1)
                    dve.wait_ge(mxb_ready, H * m + h + 1)
                    nc.vector.tensor_reduce(nmax[:, 0, h:h + 1], mx[:, 1, 0:128], AX.X, ALU.max, negate=True)
                    nc.vector.tensor_reduce(nmax[:, 1, h:h + 1], mx[:, 1, 128:384], AX.X, ALU.max, negate=True).then_inc(mxb_done, 1)

                def conv_evac(t):
                    n = NT * f + t
                    dve.wait_ge(conv_ready, n + 1)
                    nc.vector.tensor_tensor(u1[0:ROWS[t], t % 2, :], bank("conv", t)[0:ROWS[t], 0:D], conv_b[0:ROWS[t]],
                                            ALU.add).then_inc(evac["conv"], 1)
                    dve.wait_ge(evac["conv"], n + 1)
                    wait(dve, h_ready, n - 1)
                    nc.vector.scalar_tensor_tensor(out=u2[0:ROWS[t], t % 2, :], in0=u1[0:ROWS[t], t % 2, :], scalar=0.0,
                                                   in1=bn_scale[0:ROWS[t]], op0=ALU.max, op1=ALU.mult).then_inc(bn_ready, 1)

                def ln1_stats(t):
                    n = NT * f + t
                    wait_apart(dve, h_ready, n + 1)
                    nc.vector.bn_stats(stats[0:ROWS[t], t, :], hcur[0:ROWS[t], t, :]).then_inc(ln_chain, 1)
                    wait_apart(dve, ln_chain, 3 * n + 1)
                    nc.vector.bn_aggr(mv[0:ROWS[t], t, :], stats[0:ROWS[t], t, :]).then_inc(ln_chain, 1)
                    dve.wait_ge(ln_chain, 3 * n + 2)
                    nc.vector.tensor_scalar(mv[0:ROWS[t], t, 1:2], mv[0:ROWS[t], t, 1:2], EPS, None, ALU.add).then_inc(ln_chain, 1)

                def ln1_norm(t):
                    n = NT * f + t
                    dve.wait_ge(rstd_ready, n + 1)
                    nc.vector.tensor_scalar(n1[0:ROWS[t], t, :], hcur[0:ROWS[t], t, :], mv[0:ROWS[t], t, 0:1],
                                            rstd[0:ROWS[t], t:t + 1], ALU.subtract, ALU.mult).then_inc(n1_ready, 1)

                def residue(u):
                    half, qk = u // 2, u % 2
                    dve.wait_ge(p1_ready, 4 * f + u + 1)
                    wait(dve, parts_ready, 4 * f + u - 1)
                    nc.vector.scalar_tensor_tensor(out=r1[:, u % 2, :], in0=bank("qk", u)[:, 0:T], scalar=qkb[:, qk, half:half + 1],
                                                   in1=qkp[:, qk, 0, half, :], op0=ALU.add, op1=ALU.subtract
                                                   ).then_inc(evac["qk"], 1)

                def values(t):
                    dve.wait_ge(v_mm_ready, NT * f + t + 1)
                    if X and t == 0:
                        dve.wait_ge(pv_ready, GROUPS * (s + 1))
                    r = ROWS[t]
                    nc.vector.tensor_tensor(V[p][0:r, t, :, 0:HS], bank("v", t)[0:r, 0:D].rearrange("p (h d) -> p h d", h=H),
                                            v_b[0:r].rearrange("p (h d) -> p h d", h=H), ALU.add).then_inc(evac["v"], 1)

                def split_maxima(half):
                    n = 8 * m + 4 * half
                    src = nmax[:, :, half * HH:(half + 1) * HH]
                    dve.wait_ge(mxa_done, H * m + (half + 1) * HH)
                    dve.wait_ge(mxb_done, H * m + (half + 1) * HH)
                    wait(dve, nmt_ready, 2 * m + half)
                    nc.vector.tensor_copy(nm_parts[:, :, 0, :], src).then_inc(nm_chain, 1)
                    dve.wait_ge(nm_chain, n + 1)
                    nc.vector.tensor_tensor(nm_res[:], src, nm_parts[:, :, 0, :], ALU.subtract).then_inc(nm_chain, 1)
                    dve.wait_ge(nm_chain, n + 2)
                    nc.vector.tensor_copy(nm_parts[:, :, 1, :], nm_res[:]).then_inc(nm_chain, 1)
                    dve.wait_ge(nm_chain, n + 3)
                    nc.vector.tensor_tensor(nm_parts[:, :, 2, :], nm_res[:], nm_parts[:, :, 1, :], ALU.subtract).then_inc(nm_chain, 1)

                def normalise(g):
                    dve.wait_ge(rawt_ready, GROUPS * s + g + 1)
                    if g:
                        dve.wait_ge(evac["onorm"], GROUPS * s + g)
                    w = bank("onorm", g)[:, 0:TP].rearrange("p (t j e) -> p t j e", t=NT, j=4)
                    nc.vector.reciprocal(rden[:], w[:, :, :, HS]).then_inc(rden_ready, 1)
                    dve.wait_ge(rden_ready, GROUPS * s + g + 1)
                    for t in range(NT):
                        last = nc.vector.tensor_tensor(
                            o[:, t, 64 * g:64 * (g + 1)].rearrange("p (j d) -> p j d", j=4), w[:, t, :, 0:HS],
                            rden[:, t, :].unsqueeze(2).to_broadcast([128, 4, HS]), ALU.mult)
                    last.then_inc(evac["onorm"], 1)

                def residual(t):
                    r, n = ROWS[t], NT * s + t
                    row = resid[0:r, bass.ds(n, 1), :].rearrange("p a d -> p (a d)")
                    dve.wait_ge(out_ready, n + 1)
                    nc.vector.tensor_tensor(row, bank("out", t)[0:r, 0:D], row, ALU.add).then_inc(evac["out"], 1)
                    wait_apart(dve, evac["out"], n + 1)
                    nc.vector.bn_stats(stats2[0:r, t, :], row).then_inc(ln2_chain, 1)
                    wait_apart(dve, ln2_chain, 3 * n + 1)
                    nc.vector.bn_aggr(mv2[0:r, t, :], stats2[0:r, t, :]).then_inc(ln2_chain, 1)
                    dve.wait_ge(ln2_chain, 3 * n + 2)
                    nc.vector.tensor_scalar(mv2[0:r, t, 1:2], mv2[0:r, t, 1:2], EPS, None, ALU.add).then_inc(ln2_chain, 1)

                def ln2_norm(t):
                    r, n = ROWS[t], NT * s + t
                    dve.wait_ge(rstd2_ready, n + 1)
                    if t == 0:
                        dve.wait_ge(n2_free, 16 * NT * s + 1)
                    nc.vector.tensor_scalar(n2[0:r, t, :], resid[0:r, bass.ds(n, 1), :].rearrange("p a d -> p (a d)"),
                                            mv2[0:r, t, 0:1], rstd2[0:r, t:t + 1],
                                            ALU.subtract, ALU.mult).then_inc(n2_ready, 1)

                for h in range(H):
                    if M:
                        maxima(h)
                    if F and 2 <= h < 5:
                        conv_evac(h - 2)
                    if F and 3 <= h < 6:
                        ln1_stats(h - 3)
                    if F and 4 <= h < 7:
                        ln1_norm(h - 4)
                    if X and h == 5:
                        normalise(0)
                    if M and h == 8:
                        split_maxima(0)
                    if X and h == 9:
                        normalise(1)
                    if F and h in (10, 11):
                        residue(h - 10)
                    if X and h == 13:
                        normalise(2)
                    if F and h == 14:
                        residue(2)
                if F:
                    residue(3)
                if M:
                    split_maxima(1)
                if X:
                    normalise(3)
                if F:
                    values(0)
                if X:
                    for t in range(NT):
                        residual(t)
                if F:
                    values(1)
                    values(2)
                if X:
                    for t in range(NT):
                        ln2_norm(t)
            steps(dve, step)

            nc.vector.memset(esum[:], 0.0).then_inc(acc_done, 1)
            nc.vector.memset(acc[:], 0.0).then_inc(acc_free, 1)
            with dve.Fori(0, B) as b:
                for t in range(NT):
                    r, n = ROWS[t], NT * b + t
                    lg = work[0:r, 0, E * t:E * (t + 1)]
                    if t == 0:
                        dve.wait_ge(logits_ready, b + 1)
                    nc.vector.tensor_copy(logit[0:r, t, :], lg).then_inc(rt_chain, 1)
                    wait_apart(dve, rt_chain, 6 * n + 1)
                    nc.vector.max(top8[0:r, t, :], logit[0:r, t, :]).then_inc(rt_chain, 1)
                    dve.wait_ge(rt_chain, 6 * n + 2)
                    nc.vector.tensor_scalar(neg_top[0:r, t:t + 1], top8[0:r, t, 0:1], -1.0, None, ALU.mult).then_inc(top_ready, 1)
                    nc.vector.max_index(idx8[0:r, t, :], top8[0:r, t, :], logit[0:r, t, :]).then_inc(rt_chain, 1)
                    dve.wait_ge(rt_chain, 6 * n + 3)
                    nc.vector.tensor_copy(idxf[0:r, t, :], idx8[0:r, t, 0:TOPK]).then_inc(rt_chain, 1)
                    dve.wait_ge(e4_ready, n + 1)
                    nc.vector.reciprocal(esum[0:r, t:t + 1], esum[0:r, t:t + 1]).then_inc(rt_chain, 1)
                    dve.wait_ge(rt_chain, 6 * n + 5)
                    nc.vector.tensor_scalar(w4[0:r, t, :], e4[0:r, t, :], esum[0:r, t:t + 1], None, ALU.mult).then_inc(rt_chain, 1)
                    dve.wait_ge(rt_chain, 6 * n + 6)
                    for k in range(TOPK):
                        nc.vector.tensor_scalar(onehot[0:r, k, :], iota_e[0:r], idxf[0:r, t, k:k + 1], w4[0:r, t, k:k + 1],
                                                ALU.is_equal, ALU.mult).then_inc(cmb_chain, 1)
                    dve.wait_ge(cmb_chain, 7 * n + 4)
                    nc.vector.tensor_tensor(onehot[0:r, 0, :], onehot[0:r, 0, :], onehot[0:r, 1, :], ALU.add).then_inc(cmb_chain, 1)
                    nc.vector.tensor_tensor(onehot[0:r, 2, :], onehot[0:r, 2, :], onehot[0:r, 3, :], ALU.add).then_inc(cmb_chain, 1)
                    dve.wait_ge(cmb_chain, 7 * n + 6)
                    nc.vector.tensor_tensor(combine[0:r, t, :], onehot[0:r, 0, :], onehot[0:r, 2, :], ALU.add).then_inc(cmb_chain, 1)
                dve.wait_ge(cmb_chain, 7 * NT * (b + 1))
                nc.vector.tensor_copy(esum[:, 0:1], esum[:, 0:1]).then_inc(logits_read, 1)

                def add_up(i):
                    eo = (pv, work)[i % 2]
                    dve.wait_ge(eo_ready, NE * b + i + 1)
                    if i == 0:
                        dve.wait_ge(acc_free, 16 * NT * b + 1)
                    else:
                        dve.wait_ge(acc_done, NE * b + i + 1)
                    for t in range(NT):
                        r = ROWS[t]
                        part = eo[0:r, t // 2, 256 * (t % 2):256 * (t % 2) + D]
                        if i == 0:
                            last = nc.vector.tensor_tensor(acc[0:r, t, :], part,
                                                           resid[0:r, bass.ds(NT * b + t, 1), :].rearrange("p a d -> p (a d)"), ALU.add)
                        else:
                            last = nc.vector.scalar_tensor_tensor(out=acc[0:r, t, :], in0=part, scalar=combine[0:r, t, ORDER[i]:ORDER[i] + 1],
                                                                  in1=acc[0:r, t, :], op0=ALU.mult, op1=ALU.add)
                    last.then_inc(acc_done, 1)

                for i in range(NE):
                    hb = (ex, mx)[i % 2]
                    dve.wait_ge(silu_ready, NE * b + i + 1)
                    if i >= 2:
                        dve.wait_ge(eo_ready, NE * b + i - 1)
                    nc.vector.tensor_tensor(hidden[:, i % 2, :], silu[:, i % 2, :], hb[:, 1, 0:T], ALU.mult).then_inc(act_ready, 1)
                    if i:
                        add_up(i - 1)
                add_up(NE - 1)

        @block.gpsimd
        def _(pool):
            nc.gpsimd.memset(ident[:], 0.0).then_inc(pool_const, 1)
            nc.gpsimd.memset(mask_bf[:], 0.0).then_inc(pool_const, 1)
            pool.wait_ge(pool_const, 2)
            nc.gpsimd.affine_select(out=ident[:], in_=ident[:], pattern=[[-1, 128]], compare_op=ALU.not_equal, fill=1.0,
                                    base=0, channel_multiplier=1).then_inc(pool_const, 1)
            nc.gpsimd.affine_select(out=mask_bf[:], in_=mask_bf[:], pattern=[[0, 2], [-1, 128]], compare_op=ALU.is_ge,
                                    fill=NEG, base=0, channel_multiplier=1).then_inc(pool_const, 1)
            nc.gpsimd.iota(iota_e[:], pattern=[[1, E]], base=0, channel_multiplier=0,
                           allow_small_or_imprecise_dtypes=True).then_inc(pool_const, 1)
            pool.wait_ge(vec_in, 16)
            nc.gpsimd.memset(neg_half[:], -0.5).then_inc(pool_const, 1)
            nc.gpsimd.tensor_scalar(bn_shift[:], var, EPS, None, ALU.add).then_inc(pool_const, 1)
            pool.wait_ge(pool_const, 7)
            nc.gpsimd.tensor_tensor(bn_scale[:], bn_shift[:], neg_half[:], ALU.pow).then_inc(pool_const, 1)
            pool.wait_ge(dve_const, 6)

            def step(s, p, F, M, X):
                f = s + 2

                def mask(h):
                    wait_apart(pool, exp_done, H * s + h + 1)
                    blocks = P[:, h % 8, :, 0:128]
                    nc.gpsimd.affine_select(out=blocks, in_=blocks, pattern=[[0, 2], [1, 128]], compare_op=ALU.is_ge,
                                            fill=0.0, base=0, channel_multiplier=-1)
                    block = P[:, h % 8, 1, T - 128:T]
                    nc.gpsimd.affine_select(out=block, in_=block, pattern=[[1, 128]], compare_op=ALU.is_ge,
                                            fill=0.0, base=0, channel_multiplier=-1).then_inc(masked, 1)

                def shift(t):
                    r, n = ROWS[t], NT * f + t
                    pool.wait_ge(bn_ready, n + 1)
                    nc.gpsimd.tensor_tensor(hcur[0:r, t, :], u2[0:r, t % 2, :], bn_shift[0:r], ALU.add).then_inc(h_ready, 1)
                    pool.wait_ge(h_ready, n + 1)
                    nc.gpsimd.tensor_tensor(resid[0:r, bass.ds(n, 1), :].rearrange("p a d -> p (a d)"), hcur[0:r, t, :],
                                            out_b[0:r], ALU.add).then_inc(resid_ready, 1)

                def inverse_deviation(t, chain, moments, out, n, ready):
                    pool.wait_ge(chain, 3 * n + 3)
                    nc.gpsimd.tensor_tensor(out[0:ROWS[t], t:t + 1], moments[0:ROWS[t], t, 1:2], neg_half[0:ROWS[t], 0:1],
                                            ALU.pow).then_inc(ready, 1)

                def parts(u):
                    half, qk, n = u // 2, u % 2, 4 * f + u
                    wait_apart(pool, evac["qk"], n + 1)
                    nc.gpsimd.tensor_copy(qkp[:, qk, 1, half, :], r1[:, u % 2, :]).then_inc(p2_done, 1)
                    pool.wait_ge(p2_done, n + 1)
                    nc.gpsimd.tensor_tensor(qkp[:, qk, 2, half, :], r1[:, u % 2, :], qkp[:, qk, 1, half, :],
                                            ALU.subtract).then_inc(parts_ready, 1)

                for h in range(H):
                    if X:
                        mask(h)
                    if F and 2 <= h < 5:
                        shift(h - 2)
                    if F and 3 <= h < 6:
                        inverse_deviation(h - 3, ln_chain, mv, rstd, NT * f + h - 3, rstd_ready)
                    if F and h in (10, 11):
                        parts(h - 10)
                    if F and h == 14:
                        parts(2)
                if F:
                    parts(3)
                if X:
                    for t in range(NT):
                        inverse_deviation(t, ln2_chain, mv2, rstd2, NT * s + t, rstd2_ready)
            steps(pool, step)


def kernel(x, L0_tok_W, L0_tok_b, L0_tok_gamma, L0_tok_beta, L0_tok_running_mean, L0_tok_running_var,
           L0_attn_attn_W, L0_attn_attn_b, L0_attn_out_W, L0_attn_out_b,
           L0_ffn_gate_w, L0_ffn_w1, L0_ffn_w3, L0_ffn_w2, L0_ffn_sw1, L0_ffn_sw3, L0_ffn_sw2):
    import concourse.bacc as _bacc
    from concourse.bass_utils import run_bass_kernel_spmd as _run

    qkv_w = np.asarray(L0_attn_attn_W).reshape(D, H, 3, HS)
    qkv_b = np.asarray(L0_attn_attn_b).reshape(H, 3, HS)
    w13 = np.concatenate([np.concatenate([np.asarray(L0_ffn_w1), np.asarray(L0_ffn_w3)], 1),
                          np.concatenate([np.asarray(L0_ffn_sw1), np.asarray(L0_ffn_sw3)], 0)[None]], 0)
    w2 = np.concatenate([np.asarray(L0_ffn_w2), np.asarray(L0_ffn_sw2)[None]], 0)
    arrays = {
        "xT": np.asarray(x).transpose(0, 2, 1),
        "convw": np.asarray(L0_tok_W).reshape(D, CONTEXT, FEAT).transpose(2, 1, 0),
        "vec": np.concatenate([np.asarray(a).ravel() for a in (
            L0_tok_b, L0_tok_gamma, L0_tok_beta, L0_tok_running_mean, L0_tok_running_var, L0_attn_out_b, qkv_b[:, 2, :])]),
        "qkb": qkv_b[:, 0:2, :].transpose(1, 0, 2).reshape(2, KC, 128).transpose(2, 0, 1),
        "wqkv": qkv_w.transpose(0, 2, 1, 3).reshape(KC, 128, 3, D).transpose(1, 0, 2, 3),
        "wo": np.asarray(L0_attn_out_W).reshape(KC, 128, D).transpose(1, 0, 2),
        "gate": np.asarray(L0_ffn_gate_w).T.reshape(KC, 128, E).transpose(1, 0, 2),
        "w13": w13.transpose(2, 0, 1).reshape(KC, 128, NE, 2 * HID).transpose(1, 0, 2, 3),
        "w2": w2.transpose(2, 0, 1),
    }
    arrays = {k + "_in": np.ascontiguousarray(v) for k, v in arrays.items()}
    nc = _bacc.Bacc("TRN2", target_bir_lowering=False, num_devices=1)
    args = [nc.dram_tensor(n, a.shape, F32, kind="ExternalInput").ap() for n, a in arrays.items()]
    out = nc.dram_tensor("out", (B * T, D), F32, kind="ExternalOutput").ap()
    build(nc, *args, out)
    r = _run(nc, [arrays], core_ids=[0])
    return r.results[0]["out"].reshape(B, T, D)
```

```python
from contextlib import ExitStack

import numpy as np

import concourse.bass as bass
from concourse import mybir

B, T_IN, FEAT = 8, 375, 128
CONTEXT = 5
T = T_IN - (CONTEXT - 1)
D = 256
KC = D // 128
NT = -(-T // 128)
TP = NT * 128
ROWS = [min(128, T - 128 * t) for t in range(NT)]
H, HS = 16, 16
HH = H // 2
GROUPS = H // 4
PARTS = 3
Q_PART = [0, 0, 0, 1, 1, 2]
K_PART = [0, 1, 2, 0, 1, 0]
SROWS = HS * len(Q_PART)
XROWS = SROWS + PARTS
E, HID, TOPK = 16, 128, 4
N_WEIGHTS = 5
NE = E + 1
PICKS = TOPK + 1
C_EXPERT, C_WEIGHT, C_PLACE, C_OUTSIDE = D, D + PICKS, D + 2 * PICKS, D + 3 * PICKS
ROW = D + 3 * PICKS + 1
REGION = B * T + 128
MAX_TILES = (B * T * TOPK + E * 127) // 128
TILES_OF_ONE = -(-B * T // 128)
SLOTS = MAX_TILES + TILES_OF_ONE
DEEP = 8
OCTETS = -(-SLOTS // DEEP)
EPS = 1e-5
NEG = -1.0e30
ROUTE_OPS = 13
VW = 32

F32 = mybir.dt.float32
BF16 = mybir.dt.bfloat16
U32 = mybir.dt.uint32
I32 = mybir.dt.int32
ALU = mybir.AluOpType
ACT = mybir.ActivationFunctionType
AX = mybir.AxisListType

WORK = ([("rt", 0, "R"), ("rt", 1, "R"), ("conv", 0, "F"), ("conv", 1, "F"), ("lg", 0, "R"), ("conv", 2, "F"), ("onorm", 0, "E")] + [("n1t", t, "F") for t in range(NT)]
        + [("mt", 0, "M"), ("onorm", 1, "E"), ("qk", 0, "F"), ("qk", 1, "F"), ("rk", 0, "R"), ("onorm", 2, "E"), ("qk", 2, "F"),
           ("qk", 3, "F"), ("onorm", 3, "E"), ("v", 0, "F"), ("ot", 0, "E"), ("ot", 1, "E"), ("mt", 1, "M")]
        + [("out", t, "E") for t in range(NT)] + [("v", 1, "F"), ("v", 2, "F")])
PER_BATCH = {"conv": NT, "n1t": NT, "qk": 4, "v": NT, "onorm": GROUPS, "ot": KC, "mt": 2, "out": NT,
             "rt": KC, "lg": 1, "rk": 1}
AHEAD = {"F": 2, "M": 1, "E": 0, "R": -1}


def stages(s):
    return {"F": s + 2 < B, "M": 0 <= s + 1 < B, "E": 0 <= s < B, "R": 0 <= s - 1 < B}


def work_plan():
    plan, held = {}, [None, None]
    for s in range(-2, B + 1):
        n = sum(stages(s)[stage] for _, _, stage in WORK) % 2
        for name, k, stage in WORK:
            if stages(s)[stage]:
                was = held[n % 2]
                plan[s, name, k] = (n % 2, was and (was[0], was[1], was[2] - s))
                held[n % 2] = (name, k, s + AHEAD[stage])
                n += 1
    return plan


PLAN = work_plan()
for _s in range(1, B - 2):
    for _u in WORK:
        assert PLAN[_s, _u[0], _u[1]] == PLAN[1, _u[0], _u[1]]


def build(nc, xT_d, convw_d, vec_d, qkb_d, wqkv_d, wo_d, gate_d, w13_d, w2_d, out_d):
    with ExitStack() as ctx:
        def sb(name, shape, dt=F32):
            return ctx.enter_context(nc.sbuf_tensor(name, shape, dt))

        def ps(name):
            return ctx.enter_context(nc.psum_tensor(name, [128, 2, 512], F32))

        def sem(name):
            return ctx.enter_context(nc.semaphore(name))

        qk_scratch = nc.dram_tensor("qk_scratch", (2, 2, PARTS, 128, T), BF16, kind="Internal").ap()
        expert_rows = nc.dram_tensor("expert_rows", (NE * REGION + 128, ROW), F32, kind="Internal").ap()
        results = nc.dram_tensor("results", (B * T * PICKS, D), F32, kind="Internal").ap()

        convw = sb("convw", [128, CONTEXT, D])
        vec = sb("vec", [128, 7, D])
        conv_b, gamma, beta, mean, var, out_b, v_b = [vec[:, i, :] for i in range(7)]
        bn_scale = sb("bn_scale", [128, D])
        bn_shift = sb("bn_shift", [128, D])
        neg_half = sb("neg_half", [128, D])
        qkb = sb("qkb", [128, 2, KC])
        wqkv = sb("wqkv", [128, KC, 3, D])
        wo = sb("wo", [128, KC, D])
        gate = sb("gate", [128, KC, E])
        ident = sb("ident", [128, 128])
        ident_bf = sb("ident_bf", [128, 128], BF16)
        mask_bf = sb("mask_bf", [128, 2, 128], BF16)
        iota_e = sb("iota_e", [128, E])

        xT = sb("xT", [128, T_IN])
        u1 = sb("u1", [128, 2, D])
        u2 = sb("u2", [128, 2, D])
        hcur = sb("hcur", [128, NT, D])
        stats = sb("stats", [128, NT, 6])
        mv = sb("mv", [128, NT, 2])
        rstd = sb("rstd", [128, NT])
        n1 = sb("n1", [128, NT, D])
        n1T = sb("n1T", [128, KC, TP])
        resid = sb("resid", [128, B * NT, D])
        qkp = sb("qkp", [128, 2, PARTS, KC, T], BF16)
        r1 = sb("r1", [128, 2, T])
        V = [sb(f"V{p}", [128, NT, H, VW]) for p in range(2)]
        nmax = sb("nmax", [128, NT, H])
        nm_res = sb("nm_res", [128, NT, HH])
        nm_parts = sb("nm_parts", [128, NT, PARTS, HH], BF16)
        nmT = sb("nmT", [PARTS * HH, TP], BF16)
        oT_raw = sb("oT_raw", [128, 2, TP])
        rden = sb("rden", [128, NT, 4])
        o = sb("o", [128, NT, D])
        oT = sb("oT", [128, KC, TP])
        stats2 = sb("stats2", [128, NT, 6])
        mv2 = sb("mv2", [128, NT, 2])
        rstd2 = sb("rstd2", [128, NT])
        n2 = sb("n2", [128, NT, ROW])

        tri_bf = sb("tri_bf", [128, 128], BF16)
        ones_bf = sb("ones_bf", [128, 128], BF16)
        padding = sb("padding", [128, ROW])
        slot_no = sb("slot_no", [128, SLOTS])
        tile_start = sb("tile_start", [128, TILES_OF_ONE])
        up_to = sb("up_to", [128, NE, NE])
        region_start = sb("region_start", [128, NE])
        next_row = sb("next_row", [128, NE])
        n2T = sb("n2T", [128, KC, TP])
        logit = sb("logit", [128, NT, E])
        top8 = sb("top8", [128, NT, 8])
        idx8 = sb("idx8", [128, NT, 8], U32)
        idxf = sb("idxf", [128, NT, TOPK])
        e4 = sb("e4", [128, NT, TOPK])
        esum = sb("esum", [128, NT])
        onehot = sb("onehot", [128, NT * TOPK, E])
        chosen = sb("chosen", [128, NT, E], BF16)
        position = sb("position", [128, NT, E])
        picked = sb("picked", [128, NT * TOPK, E])
        row_f = sb("row_f", [128, NT * TOPK])
        row_i = sb("row_i", [128, NT * TOPK], I32)

        early = ExitStack()

        def sbe(name, shape, dt=F32):
            return early.enter_context(nc.sbuf_tensor(name, shape, dt))

        Qs = [sbe(f"Qs{p}", [XROWS, H, TP], BF16) for p in range(2)]
        Ks = [sbe(f"Ks{p}", [XROWS, H, TP], BF16) for p in range(2)]
        P = sbe("P", [128, 8, 2, T])
        early.close()
        w13 = sb("w13", [128, KC, NE, 2 * HID])
        w2 = sb("w2", [128, NE, D])
        slot_expert = sb("slot_expert", [128, SLOTS])
        slot_first = sb("slot_first", [128, SLOTS])
        slot_row = sb("slot_row", [128, SLOTS])
        slot_expert_i = sb("slot_expert_i", [1, DEEP * OCTETS + 2], I32)
        slot_row_i = sb("slot_row_i", [1, SLOTS], I32)
        next_row_i = sb("next_row_i", [1, NE], I32)
        rows = sb("rows", [128, DEEP, ROW])
        rowsT = sb("rowsT", [128, 2, D])
        silu = sb("silu", [128, 2, HID])
        hidden = sb("hidden", [128, 2, HID])
        hiddenT = sb("hiddenT", [128, 2, 128])
        hits = sb("hits", [128, 2, PICKS])
        factor = sb("factor", [128, DEEP, 2])
        place_i = sb("place_i", [128, DEEP], I32)
        scaled = sb("scaled", [128, DEEP, D])
        table = ExitStack()

        def sbt(name, shape):
            return table.enter_context(nc.sbuf_tensor(name, shape, F32))

        counts = sbt("counts", [128, NE])
        needs = sbt("needs", [128, NE, TILES_OF_ONE])
        tiles = sbt("tiles", [128, NE])
        sums = sbt("sums", [128, NE, NE])
        last_slot = sbt("last_slot", [128, NE])
        past = sbt("past", [128, SLOTS, NE])
        past_slots = sbt("past_slots", [128, SLOTS, NE])
        table.close()
        yc = sb("yc", [128, NT, PICKS * D])
        total = sb("total", [128, NT, D])

        work, ex, mx, pv = ps("work"), ps("ex"), ps("mx"), ps("pv")

        const_in, vec_in, pool_const, prep = sem("const_in"), sem("vec_in"), sem("pool_const"), sem("prep")
        dve_const, x_in = sem("dve_const"), sem("x_in")
        route_const, route_init = sem("route_const"), sem("route_init")
        conv_ready, conv_chain, bn_ready, h_ready = sem("conv_ready"), sem("conv_chain"), sem("bn_ready"), sem("h_ready")
        ln_chain, rstd_ready, n1_ready = sem("ln_chain"), sem("rstd_ready"), sem("n1_ready")
        n1t_ready, qk_ready, p1_ready = sem("n1t_ready"), sem("qk_ready"), sem("p1_ready")
        p2_done, parts_ready = sem("p2_done"), sem("parts_ready")
        qk_stored = [sem(f"qk_stored{i}") for i in range(2)]
        stack_in = [sem(f"stack_in{i}") for i in range(2)]
        v_mm_ready = sem("v_mm_ready")
        mxa_ready, mxb_ready, mxa_done, mxb_done = sem("mxa_ready"), sem("mxb_ready"), sem("mxa_done"), sem("mxb_done")
        nm_chain, nmt_ready, = sem("nm_chain"), sem("nmt_ready")
        nmax_in = [sem(f"nmax_in{i}") for i in range(2)]
        ex_ready, exp_done, masked = sem("ex_ready"), sem("exp_done"), sem("masked")
        pv_ready, raw_ready, rawt_ready, rden_ready = sem("pv_ready"), sem("raw_ready"), sem("rawt_ready"), sem("rden_ready")
        ott_ready, out_ready = sem("ott_ready"), sem("out_ready")
        ln2_chain, rstd2_ready, n2_ready, shared_sent = sem("ln2_chain"), sem("rstd2_ready"), sem("n2_ready"), sem("shared_sent")
        resid_ready, waited = sem("resid_ready"), sem("waited")
        w_in = sem("w_in")
        n2t_ready, logits_ready, ranks_ready = sem("n2t_ready"), sem("logits_ready"), sem("ranks_ready")
        rt_chain, chosen_ready, margin_ready, e4_ready = sem("rt_chain"), sem("chosen_ready"), sem("margin_ready"), sem("e4_ready")
        position_ready, rows_sent, pad_const, pad_sent = sem("position_ready"), sem("rows_sent"), sem("pad_const"), sem("pad_sent")
        tb_chain, counted, table_ready = sem("tb_chain"), sem("counted"), sem("table_ready")
        rows_in = [sem(f"rows_in{u}") for u in range(DEEP)]
        result_sent = [sem(f"result_sent{u}") for u in range(DEEP)]
        rowt_ready, rowT_copied, hid_ready, silu_ready = sem("rowt_ready"), sem("rowT_copied"), sem("hid_ready"), sem("silu_ready")
        hidden_ready, hiddent_ready, hiddenT_copied = sem("hidden_ready"), sem("hiddent_ready"), sem("hiddenT_copied")
        y_ready, y_scaled, place_chain, place_ready = sem("y_ready"), sem("y_scaled"), sem("place_chain"), sem("place_ready")
        yc_in = [sem(f"yc_in{t}") for t in range(NT)]
        half_ready, shared_ready, total_chain, total_ready = sem("half_ready"), sem("shared_ready"), sem("total_chain"), sem("total_ready")
        out_sent = [sem(f"out_sent{t}") for t in range(NT)]
        evac = {name: sem(f"{name}_evacuated") for name in PER_BATCH}

        def wait(eng, s, value):
            if not isinstance(value, int) or value > 0:
                eng.wait_ge(s, value)

        def wait_apart(eng, s, value):
            wait(eng, s, value)
            if not isinstance(value, int):
                eng.sem_inc(waited, 1)

        def plan(s, name, k):
            return PLAN[s if isinstance(s, int) else 1, name, k]

        def steps(eng, step):
            step(-2, 0, True, False, False, False)
            step(-1, 1, True, True, False, False)
            step(0, 0, True, True, True, False)
            with eng.Fori(0, (B - 4) // 2) as pair:
                step(2 * pair + 1, 1, True, True, True, True)
                step(2 * pair + 2, 0, True, True, True, True)
            step(B - 3, 1, True, True, True, True)
            step(B - 2, 0, False, True, True, True)
            step(B - 1, 1, False, False, True, True)
            step(B, 0, False, False, False, True)

        def octets(eng, octet):
            octet(0, DEEP, True, False)
            with eng.Fori(1, OCTETS - 1) as q:
                octet(q, DEEP, False, False)
            octet(OCTETS - 1, SLOTS - DEEP * (OCTETS - 1), False, True)

        block = ctx.enter_context(nc.Block())

        @block.sync
        def _(sp):
            sp.dma_start(vec[:].rearrange("p a d -> p (a d)"), vec_d.partition_broadcast(128)).then_inc(vec_in, 16)
            for dst, src in ((convw, convw_d), (wqkv, wqkv_d), (qkb, qkb_d), (wo, wo_d), (gate, gate_d)):
                sp.dma_start(dst[:], src).then_inc(const_in, 16)

            def step(s, p, F, M, X, R):
                f, m = s + 2, s + 1
                if F:
                    wait_apart(sp, conv_ready, NT * f)
                    sp.dma_start(xT[:], xT_d[bass.ds(f, 1)].rearrange("a p t -> (a p) t")).then_inc(x_in, 16)
                for half in range(2):
                    if M:
                        wait_apart(sp, evac["mt"], 2 * m + half + 1)
                        for i in range(PARTS):
                            sp.dma_start(Qs[1 - p][SROWS + i:SROWS + i + 1, half * HH:(half + 1) * HH, 0:T],
                                         nmT[i * HH:(i + 1) * HH, 0:T]).then_inc(nmax_in[half], 16)
                    if F:
                        wait_apart(sp, parts_ready, 4 * f + 2 * half + 2)
                        wait_apart(sp, stack_in[half], 16 * 12 * f)
                        sp.dma_start(qk_scratch[half].rearrange("q a p t -> p q a t"),
                                     qkp[:, :, :, half, :]).then_inc(qk_stored[half], 16)
                        if X:
                            wait_apart(sp, ex_ready, H * s + (half + 1) * HH)
                        wait_apart(sp, qk_stored[half], 16 * (f + 1))
                        for qk, (stack, part) in enumerate(((Qs, Q_PART), (Ks, K_PART))):
                            for c in range(len(part)):
                                sp.dma_start(stack[p][HS * c:HS * (c + 1), half * HH:(half + 1) * HH, 0:T],
                                             qk_scratch[half, qk, part[c]].rearrange("(h d) t -> d h t", d=HS)
                                             ).then_inc(stack_in[half], 16)
                if R:
                    wait_apart(sp, position_ready, s)
                    for t in range(NT):
                        sp.dma_start(expert_rows[bass.ds(E * REGION + T * (s - 1) + 128 * t, ROWS[t])], n2[0:ROWS[t], t, :]
                                     ).then_inc(shared_sent, 16)
            sp.wait_ge(pad_const, 4)
            for row in (E * REGION + B * T, NE * REGION):
                sp.dma_start(expert_rows[row:row + 128], padding[:]).then_inc(pad_sent, 16)
            steps(sp, step)

            sp.wait_ge(evac["mt"], 2 * B)
            sp.wait_ge(ex_ready, H * B)
            sp.wait_ge(pv_ready, GROUPS * B)
            sp.dma_start(w13[:], w13_d).then_inc(w_in, 16)
            sp.dma_start(w2[:], w2_d).then_inc(w_in, 16)
            sp.wait_ge(counted, 1)
            for e in range(E):
                row = sp.value_load(next_row_i[0:1, e:e + 1], min_val=0, max_val=NE * REGION)
                sp.dma_start(expert_rows[bass.ds(row, 128)], padding[:]).then_inc(pad_sent, 16)
            sp.wait_ge(pad_sent, 16 * (E + 2))
            sp.wait_ge(rows_sent, 16 * NT * TOPK * B)
            sp.wait_ge(shared_sent, 16 * NT * B)
            sp.wait_ge(table_ready, 2)

            slot_regs = [sp.alloc_register(f"row{u}") for u in range(DEEP)]

            def octet(q, n, first, last):
                sp.load(slot_regs[0:n], slot_row_i[0:1, bass.ds(DEEP * q, n)])
                for u in range(n):
                    j = DEEP * q + u
                    row = sp.snap(slot_regs[u], min_val=0, max_val=NE * REGION)
                    if not first:
                        wait_apart(sp, rowt_ready, j - DEEP + 1)
                        wait_apart(sp, place_ready, j - DEEP + 1)
                    sp.dma_start(rows[:, u, :], expert_rows[bass.ds(row, 128)]).then_inc(rows_in[u], 16)
            octets(sp, octet)

            for u in range(DEEP):
                sp.wait_ge(result_sent[u], 16 * ((SLOTS - 1 - u) // DEEP + 1))

            def load(b, t):
                sp.dma_start(yc[0:ROWS[t], t, :], results[bass.ds(PICKS * (T * b + 128 * t), PICKS * ROWS[t])]
                             .rearrange("(p k) d -> p (k d)", k=PICKS)).then_inc(yc_in[t], 16)

            def store(b, t):
                wait_apart(sp, total_ready, NT * b + t + 1)
                sp.dma_start(out_d[bass.ds(T * b + 128 * t, ROWS[t])], total[0:ROWS[t], t, :]).then_inc(out_sent[t], 16)

            for t in range(NT):
                load(0, t)
            with sp.Fori(0, B - 1) as b:
                for t in range(NT):
                    store(b, t)
                    load(b + 1, t)
            for t in range(NT):
                store(B - 1, t)
            for t in range(NT):
                sp.wait_ge(out_sent[t], 16 * B)

        @block.tensor
        def _(pe):
            pe.wait_ge(const_in, 16 * N_WEIGHTS)
            pe.wait_ge(pool_const, 4)
            pe.wait_ge(route_const, 3)
            pe.wait_ge(prep, 1)
            pe.wait_ge(dve_const, 3)

            def step(s, p, F, M, X, R):
                f, m = s + 2, s + 1

                def bank(name, k):
                    b, was = plan(s, name, k)
                    if was is not None:
                        wait(pe, evac[was[0]], PER_BATCH[was[0]] * (s + was[2]) + was[1] + 1)
                    return work[:, b, :]

                def maxima_scores(h):
                    if h % HH == 0:
                        pe.wait_ge(stack_in[h // HH], 16 * 12 * (m + 1))
                    q, k = Qs[1 - p], Ks[1 - p]
                    wait(pe, mxa_done, H * m + h)
                    pe.matmul(mx[:, 0, 256:T], ident_bf[:], mask_bf[:, 0, 0:T - 256], start=True, stop=False, skip_group_check=True)
                    pe.matmul(mx[:, 0, 0:T], q[0:SROWS, h, 256:TP], k[0:SROWS, h, 0:T], start=False, stop=True,
                              skip_group_check=True).then_inc(mxa_ready, 1)
                    wait(pe, mxb_done, H * m + h)
                    pe.matmul(mx[:, 1, :].rearrange("p (a c) -> p a c", a=2)[:, :, 0:128], ident_bf[:], mask_bf[:], start=True, stop=False, skip_group_check=True)
                    pe.matmul(mx[:, 1, 0:128], q[0:SROWS, h, 0:128], k[0:SROWS, h, 0:128], start=False, stop=False, skip_group_check=True)
                    pe.matmul(mx[:, 1, 128:384], q[0:SROWS, h, 128:256], k[0:SROWS, h, 0:256], start=False, stop=True,
                              skip_group_check=True).then_inc(mxb_ready, 1)

                def exp_scores(h):
                    if h % HH == 0:
                        pe.wait_ge(nmax_in[h // HH], 16 * PARTS * (s + 1))
                    q, k = Qs[p], Ks[p]
                    if h:
                        pe.wait_ge(exp_done, H * s + h)
                    pe.matmul(ex[:, 0, 0:T], k[:, h, 0:128], q[:, h, 0:T], start=True, stop=True)
                    pe.matmul(ex[:, 1, 0:T - 128], k[:, h, 128:256], q[:, h, 128:T], start=True, stop=True)
                    pe.matmul(ex[:, 1, T - 128:T], k[:, h, 256:TP], q[:, h, 256:TP], start=True, stop=True).then_inc(ex_ready, 1)

                def weigh_values(g):
                    pe.wait_ge(masked, H * s + 4 * g + 4)
                    if g == 0:
                        pe.wait_ge(evac["v"], NT * (s + 1))
                    for kt in range(NT):
                        for j in range(4):
                            h = 4 * g + j
                            q0 = 128 * kt
                            probs = P[:, h % 8, 0, :] if kt == 0 else P[:, h % 8, 1, 0:T - 128] if kt == 1 \
                                else P[:, h % 8, 1, T - 128:T - 128 + T - 256]
                            mm = pe.matmul(pv[32 * j:32 * j + VW, g % 2, q0:T], V[p][:, kt, h, :], probs,
                                           start=(kt == 0), stop=(kt == NT - 1))
                    mm.then_inc(pv_ready, 1)

                def transpose_raw(g):
                    w = bank("onorm", g)
                    pe.wait_ge(raw_ready, GROUPS * s + g + 1)
                    for t in range(NT):
                        mm = pe.transpose(w[:, 128 * t:128 * (t + 1)], oT_raw[:, g % 2, 128 * t:128 * (t + 1)], ident[:])
                    mm.then_inc(rawt_ready, 1)

                def conv(t):
                    w = bank("conv", t)
                    if t == 0:
                        pe.wait_ge(x_in, 16 * (f + 1))
                    for c in range(CONTEXT):
                        mm = pe.matmul(w[0:ROWS[t], 0:D], xT[:, 128 * t + c:128 * t + c + ROWS[t]], convw[:, c, :],
                                       start=(c == 0), stop=(c == CONTEXT - 1))
                    mm.then_inc(conv_ready, 1)

                def transpose_n1(t):
                    w = bank("n1t", t)
                    pe.wait_ge(n1_ready, NT * f + t + 1)
                    for c in range(KC):
                        mm = pe.transpose(w[:, 128 * c:128 * c + ROWS[t]], n1[0:ROWS[t], t, 128 * c:128 * (c + 1)],
                                          ident[0:ROWS[t], 0:ROWS[t]])
                    mm.then_inc(n1t_ready, 1)

                def project_qk(u):
                    w = bank("qk", u)
                    half, qk = u // 2, u % 2
                    if u == 0:
                        pe.wait_ge(evac["n1t"], NT * (f + 1))
                    for c in range(KC):
                        mm = pe.matmul(w[:, 0:T], wqkv[:, c, qk, 128 * half:128 * (half + 1)], n1T[:, c, 0:T],
                                       start=(c == 0), stop=(c == KC - 1))
                    mm.then_inc(qk_ready, 1)

                def project_v(t):
                    w = bank("v", t)
                    for c in range(KC):
                        mm = pe.matmul(w[0:ROWS[t], 0:D], n1T[:, c, 128 * t:128 * t + ROWS[t]], wqkv[:, c, 2, :],
                                       start=(c == 0), stop=(c == KC - 1))
                    mm.then_inc(v_mm_ready, 1)

                def transpose_maxima(half):
                    w = bank("mt", half)
                    pe.wait_ge(nm_chain, 8 * m + 4 * half + 4)
                    for t in range(NT):
                        mm = pe.transpose(w.bitcast(BF16)[0:PARTS * HH, 128 * t:128 * (t + 1)],
                                          nm_parts[:, t, :, :].rearrange("p a h -> p (a h)"), ident_bf[:])
                    mm.then_inc(nmt_ready, 1)

                def transpose_o(c):
                    w = bank("ot", c)
                    if c == 0:
                        pe.wait_ge(evac["onorm"], GROUPS * (s + 1))
                    for t in range(NT):
                        mm = pe.transpose(w[:, 128 * t:128 * (t + 1)], o[:, t, 128 * c:128 * (c + 1)], ident[:])
                    mm.then_inc(ott_ready, 1)

                def project_out(t):
                    w = bank("out", t)
                    if t == 0:
                        pe.wait_ge(evac["ot"], KC * (s + 1))
                    for c in range(KC):
                        mm = pe.matmul(w[0:ROWS[t], 0:D], oT[:, c, 128 * t:128 * t + ROWS[t]], wo[:, c, :],
                                       start=(c == 0), stop=(c == KC - 1))
                    mm.then_inc(out_ready, 1)

                def transpose_n2(c):
                    w = bank("rt", c)
                    pe.wait_ge(n2_ready, NT * s)
                    for t in range(NT):
                        mm = pe.transpose(w[:, 128 * t:128 * t + ROWS[t]], n2[0:ROWS[t], t, 128 * c:128 * (c + 1)],
                                          ident[0:ROWS[t], 0:ROWS[t]])
                    mm.then_inc(n2t_ready, 1)

                def gate_logits():
                    w = bank("lg", 0)
                    pe.wait_ge(evac["rt"], KC * s)
                    for t in range(NT):
                        for c in range(KC):
                            mm = pe.matmul(w[:, E * t:E * (t + 1)], n2T[:, c, 128 * t:128 * (t + 1)], gate[:, c, :],
                                           start=(c == 0), stop=(c == KC - 1))
                    mm.then_inc(logits_ready, 1)

                def ranks():
                    w = bank("rk", 0)
                    pe.wait_ge(chosen_ready, s)
                    for t in range(NT + 1):
                        for before in range(min(t, NT - 1) + 1):
                            rows_before = tri_bf if before == t else ones_bf
                            last = before == min(t, NT - 1)
                            mm = pe.matmul(w[:, E * t:E * (t + 1)], rows_before[0:ROWS[before], :],
                                           chosen[0:ROWS[before], before, :], start=(before == 0), stop=last)
                    mm.then_inc(ranks_ready, 1)

                for h in range(H):
                    if M:
                        maxima_scores(h)
                    if X:
                        exp_scores(h)
                    if R and h < KC:
                        transpose_n2(h)
                    if F and 2 <= h < 5:
                        conv(h - 2)
                    if R and h == 3:
                        gate_logits()
                    if X and h == 5:
                        transpose_raw(0)
                    if F and 6 <= h < 9:
                        transpose_n1(h - 6)
                    if M and h == 9:
                        transpose_maxima(0)
                    if X and h == 9:
                        transpose_raw(1)
                    if F and h in (10, 11):
                        project_qk(h - 10)
                    if R and h == 12:
                        ranks()
                    if X and h in (4, 8, 12):
                        weigh_values(h // 4 - 1)
                    if X and h == 13:
                        transpose_raw(2)
                    if F and h == 14:
                        project_qk(2)
                if F:
                    project_qk(3)
                if X:
                    weigh_values(3)
                    transpose_raw(3)
                if F:
                    project_v(0)
                if X:
                    transpose_o(0)
                    transpose_o(1)
                if M:
                    transpose_maxima(1)
                if X:
                    for t in range(NT):
                        project_out(t)
                if F:
                    project_v(1)
                    project_v(2)
            steps(pe, step)

            pe.wait_ge(w_in, 16 * 2)
            pe.wait_ge(table_ready, 2)

            expert_regs = [pe.alloc_register(f"expert{u}") for u in range(DEEP + 2)]

            def transpose_rows(q, u):
                j = DEEP * q + u
                pe.wait_ge(rows_in[u], 16 * (q + 1))
                wait(pe, rowT_copied, j - 1)
                for c in range(KC):
                    mm = pe.transpose(work[:, u % 2, 128 * c:128 * (c + 1)], rows[:, u, 128 * c:128 * (c + 1)], ident[:])
                mm.then_inc(rowt_ready, 1)

            def hidden_units(j, u, e):
                pe.wait_ge(rowT_copied, j + 1)
                wait(pe, hidden_ready, j - 1)
                for c in range(KC):
                    mm = pe.matmul(ex[:, u % 2, 0:2 * HID], rowsT[:, u % 2, 128 * c:128 * (c + 1)],
                                   w13[:, c, bass.ds(e, 1), :].rearrange("p a h -> p (a h)"), start=(c == 0), stop=(c == KC - 1))
                mm.then_inc(hid_ready, 1)

            def transpose_hidden(j, u):
                pe.wait_ge(hidden_ready, j + 1)
                wait(pe, hiddenT_copied, j - 1)
                pe.transpose(mx[:, u % 2, 0:128], hidden[:, u % 2, :], ident[:]).then_inc(hiddent_ready, 1)

            def expert_out(j, u, e):
                pe.wait_ge(hiddenT_copied, j + 1)
                wait(pe, y_scaled, j - 1)
                pe.matmul(pv[:, u % 2, 0:D], hiddenT[:, u % 2, :], w2[:, bass.ds(e, 1), :].rearrange("p a d -> p (a d)"),
                          start=True, stop=True).then_inc(y_ready, 1)

            def octet(q, n, first, last):
                pe.load(expert_regs, slot_expert_i[0:1, bass.ds(DEEP * q, DEEP + 2)])
                expert = [pe.snap(reg, min_val=0, max_val=NE - 1) for reg in expert_regs]
                for u in range(n):
                    j = DEEP * q + u
                    if not (last and u == n - 1):
                        transpose_rows(q + (u + 1) // DEEP, (u + 1) % DEEP)
                    hidden_units(j, u, expert[u + 2])
                    if not (first and u < 1):
                        transpose_hidden(j - 1, u - 1)
                    if not (first and u < 2):
                        expert_out(j - 2, u - 2, expert[u])
                if last:
                    transpose_hidden(SLOTS - 1, n - 1)
                    expert_out(SLOTS - 2, n - 2, expert[n])
                    expert_out(SLOTS - 1, n - 1, expert[n + 1])
            transpose_rows(0, 0)
            octets(pe, octet)

        @block.scalar
        def _(act):
            act.wait_ge(prep, 1)

            def step(s, p, F, M, X, R):
                f, m = s + 2, s + 1

                def bank(name, k):
                    return work[:, plan(s, name, k)[0], :]

                def exponentials(h):
                    act.wait_ge(ex_ready, H * s + h + 1)
                    if h >= 8:
                        act.wait_ge(pv_ready, GROUPS * s + h // 4 - 1)
                    nc.scalar.activation(P[:, h % 8, :, :], ex[:, :, 0:T], ACT.Exp).then_inc(exp_done, 1)

                def copy_raw(g):
                    act.wait_ge(pv_ready, GROUPS * s + g + 1)
                    nc.scalar.activation(oT_raw[:, g % 2, 0:T], pv[:, g % 2, 0:T], ACT.Copy).then_inc(raw_ready, 1)

                def copy_n1T(t):
                    act.wait_ge(n1t_ready, NT * f + t + 1)
                    w = bank("n1t", t).rearrange("p (c n) -> p c n", n=128)
                    nc.scalar.activation(n1T[:, :, 128 * t:128 * t + ROWS[t]], w[:, 0:KC, 0:ROWS[t]],
                                         ACT.Copy).then_inc(evac["n1t"], 1)

                def first_part(u):
                    half, qk = u // 2, u % 2
                    act.wait_ge(qk_ready, 4 * f + u + 1)
                    wait(act, qk_stored[half], 16 * f)
                    nc.scalar.activation(qkp[:, qk, 0, half, :], bank("qk", u)[:, 0:T], ACT.Identity,
                                         bias=qkb[:, qk, half:half + 1]).then_inc(p1_ready, 1)

                def copy_maxima(half):
                    act.wait_ge(nmt_ready, 2 * m + half + 1)
                    wait(act, nmax_in[1 - half], 16 * PARTS * (m + half))
                    nc.scalar.activation(nmT[:, 0:T], bank("mt", half).bitcast(BF16)[0:PARTS * HH, 0:T],
                                         ACT.Copy).then_inc(evac["mt"], 1)

                def copy_oT(c):
                    act.wait_ge(ott_ready, KC * s + c + 1)
                    nc.scalar.activation(oT[:, c, :], bank("ot", c)[:, 0:TP], ACT.Copy).then_inc(evac["ot"], 1)

                def copy_n2T(c):
                    act.wait_ge(n2t_ready, KC * (s - 1) + c + 1)
                    nc.scalar.activation(n2T[:, c, 0:T], bank("rt", c)[:, 0:T], ACT.Copy).then_inc(evac["rt"], 1)

                def choice_exponentials():
                    act.wait_ge(margin_ready, s)
                    nc.scalar.activation(e4[:], e4[:], ACT.Exp).then_inc(e4_ready, 1)

                for h in range(H):
                    if X:
                        exponentials(h)
                    if R and h < KC:
                        copy_n2T(h)
                    if R and h == 8:
                        choice_exponentials()
                    if F and 6 <= h < 9:
                        copy_n1T(h - 6)
                    if M and h == 9:
                        copy_maxima(0)
                    if F and h in (10, 11):
                        first_part(h - 10)
                    if X and h in (4, 8, 12):
                        copy_raw(h // 4 - 1)
                    if F and h == 14:
                        first_part(2)
                if F:
                    first_part(3)
                if X:
                    copy_raw(3)
                    copy_oT(0)
                    copy_oT(1)
                if M:
                    copy_maxima(1)
            steps(act, step)

            act.wait_ge(table_ready, 2)

            def copy_rowsT(j, u):
                act.wait_ge(rowt_ready, j + 1)
                wait(act, hid_ready, j - 1)
                nc.scalar.activation(rowsT[:, u % 2, :], work[:, u % 2, 0:D], ACT.Copy).then_inc(rowT_copied, 1)

            def octet(q, n, first, last):
                for u in range(n):
                    j = DEEP * q + u
                    if not (last and u == n - 1):
                        copy_rowsT(j + 1, u + 1)
                    act.wait_ge(hid_ready, j + 1)
                    wait(act, hidden_ready, j - 1)
                    nc.scalar.activation(silu[:, u % 2, :], ex[:, u % 2, 0:HID], ACT.Silu).then_inc(silu_ready, 1)
            copy_rowsT(0, 0)
            octets(act, octet)

        @block.vector
        def _(dve):
            nc.vector.memset(oT_raw[:, :, T:TP], 1.0)
            nc.vector.memset(n2T[:, :, T:TP], 0.0)
            for stack in (*Qs, *Ks):
                nc.vector.memset(stack[:, :, T:TP], 0.0)
            nc.vector.memset(V[0][:], 0.0).then_inc(dve_const, 1)
            nc.vector.memset(V[1][:], 0.0).then_inc(dve_const, 1)
            dve.wait_ge(dve_const, 2)
            for p in range(2):
                nc.vector.memset(V[p][:, :, :, HS:HS + 1], 1.0)
                nc.vector.memset(Ks[p][SROWS:XROWS, :, :], 1.0)
            dve.wait_ge(const_in, 16 * N_WEIGHTS)
            nc.vector.tensor_scalar(wqkv[:, :, 0, :], wqkv[:, :, 0, :], HS ** -0.5, None, ALU.mult)
            nc.vector.tensor_scalar(qkb[:, 0, :], qkb[:, 0, :], HS ** -0.5, None, ALU.mult).then_inc(prep, 1)
            dve.wait_ge(pool_const, 8)
            dve.wait_ge(route_init, 10)
            nc.vector.tensor_copy(ident_bf[:], ident[:]).then_inc(dve_const, 1)
            nc.vector.tensor_tensor(bn_scale[:], gamma, bn_scale[:], ALU.mult).then_inc(dve_const, 1)
            dve.wait_ge(dve_const, 4)
            nc.vector.tensor_tensor(bn_shift[:], mean, bn_scale[:], ALU.mult).then_inc(dve_const, 1)
            dve.wait_ge(dve_const, 5)
            nc.vector.tensor_tensor(bn_shift[:], beta, bn_shift[:], ALU.subtract).then_inc(dve_const, 1)

            def step(s, p, F, M, X, R):
                f, m = s + 2, s + 1

                def bank(name, k):
                    return work[:, plan(s, name, k)[0], :]

                def maxima(h):
                    dve.wait_ge(mxa_ready, H * m + h + 1)
                    nc.vector.tensor_reduce(nmax[:, 2, h:h + 1], mx[:, 0, 0:T], AX.X, ALU.max, negate=True).then_inc(mxa_done, 1)
                    dve.wait_ge(mxb_ready, H * m + h + 1)
                    nc.vector.tensor_reduce(nmax[:, 0, h:h + 1], mx[:, 1, 0:128], AX.X, ALU.max, negate=True)
                    nc.vector.tensor_reduce(nmax[:, 1, h:h + 1], mx[:, 1, 128:384], AX.X, ALU.max, negate=True).then_inc(mxb_done, 1)

                def conv_evac(t):
                    n = NT * f + t
                    dve.wait_ge(conv_ready, n + 1)
                    nc.vector.tensor_tensor(u1[0:ROWS[t], t % 2, :], bank("conv", t)[0:ROWS[t], 0:D], conv_b[0:ROWS[t]],
                                            ALU.add).then_inc(evac["conv"], 1)
                    dve.wait_ge(evac["conv"], n + 1)
                    wait(dve, h_ready, n - 1)
                    nc.vector.scalar_tensor_tensor(out=u2[0:ROWS[t], t % 2, :], in0=u1[0:ROWS[t], t % 2, :], scalar=0.0,
                                                   in1=bn_scale[0:ROWS[t]], op0=ALU.max, op1=ALU.mult).then_inc(bn_ready, 1)

                def ln1_stats(t):
                    n = NT * f + t
                    wait_apart(dve, h_ready, n + 1)
                    nc.vector.bn_stats(stats[0:ROWS[t], t, :], hcur[0:ROWS[t], t, :]).then_inc(ln_chain, 1)
                    wait_apart(dve, ln_chain, 3 * n + 1)
                    nc.vector.bn_aggr(mv[0:ROWS[t], t, :], stats[0:ROWS[t], t, :]).then_inc(ln_chain, 1)
                    dve.wait_ge(ln_chain, 3 * n + 2)
                    nc.vector.tensor_scalar(mv[0:ROWS[t], t, 1:2], mv[0:ROWS[t], t, 1:2], EPS, None, ALU.add).then_inc(ln_chain, 1)

                def ln1_norm(t):
                    n = NT * f + t
                    dve.wait_ge(rstd_ready, n + 1)
                    nc.vector.tensor_scalar(n1[0:ROWS[t], t, :], hcur[0:ROWS[t], t, :], mv[0:ROWS[t], t, 0:1],
                                            rstd[0:ROWS[t], t:t + 1], ALU.subtract, ALU.mult).then_inc(n1_ready, 1)

                def residue(u):
                    half, qk = u // 2, u % 2
                    dve.wait_ge(p1_ready, 4 * f + u + 1)
                    wait(dve, parts_ready, 4 * f + u - 1)
                    nc.vector.scalar_tensor_tensor(out=r1[:, u % 2, :], in0=bank("qk", u)[:, 0:T], scalar=qkb[:, qk, half:half + 1],
                                                   in1=qkp[:, qk, 0, half, :], op0=ALU.add, op1=ALU.subtract
                                                   ).then_inc(evac["qk"], 1)

                def values(t):
                    dve.wait_ge(v_mm_ready, NT * f + t + 1)
                    if X and t == 0:
                        dve.wait_ge(pv_ready, GROUPS * (s + 1))
                    r = ROWS[t]
                    nc.vector.tensor_tensor(V[p][0:r, t, :, 0:HS], bank("v", t)[0:r, 0:D].rearrange("p (h d) -> p h d", h=H),
                                            v_b[0:r].rearrange("p (h d) -> p h d", h=H), ALU.add).then_inc(evac["v"], 1)

                def split_maxima(half):
                    n = 8 * m + 4 * half
                    src = nmax[:, :, half * HH:(half + 1) * HH]
                    dve.wait_ge(mxa_done, H * m + (half + 1) * HH)
                    dve.wait_ge(mxb_done, H * m + (half + 1) * HH)
                    wait(dve, nmt_ready, 2 * m + half)
                    nc.vector.tensor_copy(nm_parts[:, :, 0, :], src).then_inc(nm_chain, 1)
                    dve.wait_ge(nm_chain, n + 1)
                    nc.vector.tensor_tensor(nm_res[:], src, nm_parts[:, :, 0, :], ALU.subtract).then_inc(nm_chain, 1)
                    dve.wait_ge(nm_chain, n + 2)
                    nc.vector.tensor_copy(nm_parts[:, :, 1, :], nm_res[:]).then_inc(nm_chain, 1)
                    dve.wait_ge(nm_chain, n + 3)
                    nc.vector.tensor_tensor(nm_parts[:, :, 2, :], nm_res[:], nm_parts[:, :, 1, :], ALU.subtract).then_inc(nm_chain, 1)

                def normalise(g):
                    dve.wait_ge(rawt_ready, GROUPS * s + g + 1)
                    if g:
                        dve.wait_ge(evac["onorm"], GROUPS * s + g)
                    w = bank("onorm", g)[:, 0:TP].rearrange("p (t j e) -> p t j e", t=NT, j=4)
                    nc.vector.reciprocal(rden[:], w[:, :, :, HS]).then_inc(rden_ready, 1)
                    dve.wait_ge(rden_ready, GROUPS * s + g + 1)
                    for t in range(NT):
                        last = nc.vector.tensor_tensor(
                            o[:, t, 64 * g:64 * (g + 1)].rearrange("p (j d) -> p j d", j=4), w[:, t, :, 0:HS],
                            rden[:, t, :].unsqueeze(2).to_broadcast([128, 4, HS]), ALU.mult)
                    last.then_inc(evac["onorm"], 1)

                def residual(t):
                    r, n = ROWS[t], NT * s + t
                    row = resid[0:r, bass.ds(n, 1), :].rearrange("p a d -> p (a d)")
                    dve.wait_ge(out_ready, n + 1)
                    nc.vector.tensor_tensor(row, bank("out", t)[0:r, 0:D], row, ALU.add).then_inc(evac["out"], 1)
                    wait_apart(dve, evac["out"], n + 1)
                    nc.vector.bn_stats(stats2[0:r, t, :], row).then_inc(ln2_chain, 1)
                    wait_apart(dve, ln2_chain, 3 * n + 1)
                    nc.vector.bn_aggr(mv2[0:r, t, :], stats2[0:r, t, :]).then_inc(ln2_chain, 1)
                    dve.wait_ge(ln2_chain, 3 * n + 2)
                    nc.vector.tensor_scalar(mv2[0:r, t, 1:2], mv2[0:r, t, 1:2], EPS, None, ALU.add).then_inc(ln2_chain, 1)

                def ln2_norm(t):
                    r, n = ROWS[t], NT * s + t
                    dve.wait_ge(rstd2_ready, n + 1)
                    if t == 0:
                        wait(dve, rows_sent, 16 * NT * TOPK * s)
                        wait(dve, shared_sent, 16 * NT * s)
                    nc.vector.tensor_scalar(n2[0:r, t, 0:D], resid[0:r, bass.ds(n, 1), :].rearrange("p a d -> p (a d)"),
                                            mv2[0:r, t, 0:1], rstd2[0:r, t:t + 1],
                                            ALU.subtract, ALU.mult).then_inc(n2_ready, 1)

                def after(k):
                    dve.wait_ge(rt_chain, ROUTE_OPS * (s - 1) + k)

                def route_logits():
                    nc.vector.tensor_scalar(n2[:, :, C_PLACE:C_PLACE + PICKS], n2[:, :, C_PLACE:C_PLACE + PICKS], float(PICKS * T), None,
                                            ALU.add).then_inc(rt_chain, 1)
                    dve.wait_ge(logits_ready, s)
                    nc.vector.tensor_copy(logit[:].rearrange("p t e -> p (t e)"), bank("lg", 0)[:, 0:NT * E]).then_inc(evac["lg"], 1)

                def route_top():
                    wait_apart(dve, evac["lg"], s)
                    for t in range(NT):
                        last = nc.vector.max(top8[:, t, :], logit[:, t, :])
                    last.then_inc(rt_chain, 1)

                def route_index():
                    wait_apart(dve, rt_chain, ROUTE_OPS * (s - 1) + 2)
                    for t in range(NT):
                        last = nc.vector.max_index(idx8[:, t, :], top8[:, t, :], logit[:, t, :])
                    last.then_inc(rt_chain, 1)
                    wait(dve, e4_ready, s - 1)
                    nc.vector.tensor_tensor(e4[:], top8[:, :, 0:TOPK], top8[:, :, 0:1].to_broadcast([128, NT, TOPK]),
                                            ALU.subtract).then_inc(margin_ready, 1)

                def route_onehot():
                    after(3)
                    nc.vector.tensor_copy(idxf[:], idx8[:, :, 0:TOPK]).then_inc(rt_chain, 1)
                    nc.vector.tensor_copy(n2[:, :, C_EXPERT:C_EXPERT + TOPK], idx8[:, :, 0:TOPK]).then_inc(rt_chain, 1)
                    after(5)
                    nc.vector.tensor_tensor(onehot[:], iota_e[:].unsqueeze(1).to_broadcast([128, NT * TOPK, E]),
                                            idxf[:].rearrange("p t k -> p (t k)").unsqueeze(2).to_broadcast([128, NT * TOPK, E]),
                                            ALU.is_equal).then_inc(rt_chain, 1)

                def route_chosen():
                    after(6)
                    wait(dve, ranks_ready, s - 1)
                    nc.vector.tensor_reduce(position[:], onehot[:].rearrange("p (t k) e -> p t e k", k=TOPK),
                                            AX.X, ALU.add).then_inc(rt_chain, 1)
                    after(7)
                    nc.vector.tensor_copy(chosen[:], position[:]).then_inc(chosen_ready, 1)

                def route_weights():
                    dve.wait_ge(e4_ready, s)
                    nc.vector.tensor_reduce(esum[:], e4[:], AX.X, ALU.add).then_inc(rt_chain, 1)
                    after(8)
                    nc.vector.reciprocal(esum[:], esum[:]).then_inc(rt_chain, 1)
                    after(9)
                    nc.vector.tensor_tensor(n2[:, :, C_WEIGHT:C_WEIGHT + TOPK], e4[:], esum[:].unsqueeze(2).to_broadcast([128, NT, TOPK]),
                                            ALU.mult).then_inc(rt_chain, 1)

                def route_positions():
                    w = bank("rk", 0)
                    dve.wait_ge(ranks_ready, s)
                    dve.wait_ge(chosen_ready, s)
                    nc.vector.tensor_tensor(position[:], w[:, 0:NT * E].rearrange("p (t e) -> p t e", t=NT),
                                            next_row[:, 0:E].unsqueeze(1).to_broadcast([128, NT, E]), ALU.add).then_inc(rt_chain, 1)
                    after(11)
                    nc.vector.tensor_tensor(next_row[:, 0:E], next_row[:, 0:E], w[:, NT * E:(NT + 1) * E],
                                            ALU.add).then_inc(evac["rk"], 1)
                    nc.vector.tensor_tensor(picked[:].rearrange("p (t k) e -> p t k e", k=TOPK),
                                            onehot[:].rearrange("p (t k) e -> p t k e", k=TOPK),
                                            position[:].unsqueeze(2).to_broadcast([128, NT, TOPK, E]), ALU.mult).then_inc(rt_chain, 1)
                    after(12)
                    nc.vector.tensor_reduce(row_f[:], picked[:], AX.X, ALU.add).then_inc(rt_chain, 1)
                    after(13)
                    nc.vector.tensor_copy(row_i[:], row_f[:]).then_inc(position_ready, 1)

                ROUTE = {4: route_logits, 5: route_top, 6: route_index, 7: route_onehot, 8: route_chosen, 10: route_weights,
                         13: route_positions}
                for h in range(H):
                    if M:
                        maxima(h)
                    if R and h in ROUTE:
                        ROUTE[h]()
                    if F and 2 <= h < 5:
                        conv_evac(h - 2)
                    if F and 3 <= h < 6:
                        ln1_stats(h - 3)
                    if F and 4 <= h < 7:
                        ln1_norm(h - 4)
                    if X and h == 5:
                        normalise(0)
                    if M and h == 8:
                        split_maxima(0)
                    if X and h == 9:
                        normalise(1)
                    if F and h in (10, 11):
                        residue(h - 10)
                    if X and h == 13:
                        normalise(2)
                    if F and h == 14:
                        residue(2)
                if F:
                    residue(3)
                if M:
                    split_maxima(1)
                if X:
                    normalise(3)
                if F:
                    values(0)
                if X:
                    for t in range(NT):
                        residual(t)
                if F:
                    values(1)
                    values(2)
                if X:
                    for t in range(NT):
                        ln2_norm(t)
            steps(dve, step)

            dve.wait_ge(position_ready, B)
            dve.wait_ge(evac["rk"], B)
            dve.wait_ge(pv_ready, GROUPS * B)
            dve.wait_ge(ex_ready, H * B)
            dve.wait_ge(masked, H * B)
            nc.vector.tensor_copy(next_row_i[:], next_row[0:1, :]).then_inc(counted, 1)
            nc.vector.tensor_tensor(counts[:], next_row[:], region_start[:], ALU.subtract).then_inc(tb_chain, 1)
            dve.wait_ge(tb_chain, 1)
            nc.vector.tensor_tensor(needs[:], counts[:].unsqueeze(2).to_broadcast([128, NE, TILES_OF_ONE]),
                                    tile_start[:].unsqueeze(1).to_broadcast([128, NE, TILES_OF_ONE]), ALU.is_gt).then_inc(tb_chain, 1)
            dve.wait_ge(tb_chain, 2)
            nc.vector.tensor_reduce(tiles[:], needs[:], AX.X, ALU.add).then_inc(tb_chain, 1)
            dve.wait_ge(tb_chain, 3)
            nc.vector.tensor_tensor(sums[:], up_to[:], tiles[:].unsqueeze(1).to_broadcast([128, NE, NE]), ALU.mult).then_inc(tb_chain, 1)
            dve.wait_ge(tb_chain, 4)
            nc.vector.tensor_reduce(last_slot[:], sums[:], AX.X, ALU.add).then_inc(tb_chain, 1)
            dve.wait_ge(tb_chain, 5)
            nc.vector.tensor_tensor(past[:], last_slot[:].unsqueeze(1).to_broadcast([128, SLOTS, NE]),
                                    slot_no[:].unsqueeze(2).to_broadcast([128, SLOTS, NE]), ALU.is_le).then_inc(tb_chain, 1)
            dve.wait_ge(tb_chain, 6)
            nc.vector.tensor_reduce(slot_expert[:], past[:], AX.X, ALU.add).then_inc(tb_chain, 1)
            nc.vector.tensor_tensor(past_slots[:], past[:], last_slot[:].unsqueeze(1).to_broadcast([128, SLOTS, NE]),
                                    ALU.mult).then_inc(tb_chain, 1)
            dve.wait_ge(tb_chain, 8)
            nc.vector.tensor_reduce(slot_first[:], past_slots[:], AX.X, ALU.max).then_inc(tb_chain, 1)
            dve.wait_ge(tb_chain, 9)
            nc.vector.tensor_tensor(slot_first[:], slot_no[:], slot_first[:], ALU.subtract).then_inc(tb_chain, 1)
            nc.vector.tensor_scalar(slot_row[:], slot_expert[:], float(REGION), None, ALU.mult).then_inc(tb_chain, 1)
            dve.wait_ge(tb_chain, 11)
            nc.vector.scalar_tensor_tensor(out=slot_row[:], in0=slot_first[:], scalar=128.0, in1=slot_row[:],
                                           op0=ALU.mult, op1=ALU.add).then_inc(tb_chain, 1)
            dve.wait_ge(tb_chain, 12)
            nc.vector.tensor_scalar(slot_row_i[:], slot_row[0:1, :], float(NE * REGION), None, ALU.min).then_inc(table_ready, 1)
            nc.vector.memset(slot_expert_i[:, 0:2], 0.0)
            nc.vector.memset(slot_expert_i[:, SLOTS + 2:], 0.0)
            nc.vector.tensor_scalar(slot_expert_i[:, 2:SLOTS + 2], slot_expert[0:1, :], float(NE - 1), None, ALU.min).then_inc(table_ready, 1)

            def copy_hiddenT(j, u):
                dve.wait_ge(hiddent_ready, j + 1)
                wait(dve, y_ready, j - 1)
                nc.vector.tensor_copy(hiddenT[:, u % 2, :], mx[:, u % 2, 0:128]).then_inc(hiddenT_copied, 1)

            def gated(j, u):
                dve.wait_ge(silu_ready, j + 1)
                wait(dve, hiddent_ready, j - 1)
                nc.vector.tensor_tensor(hidden[:, u % 2, :], silu[:, u % 2, :], ex[:, u % 2, HID:2 * HID],
                                        ALU.mult).then_inc(hidden_ready, 1)

            def places(q, u, first):
                j = DEEP * q + u
                dve.wait_ge(rows_in[u], 16 * (q + 1))
                wait(dve, place_chain, 2 * j)
                nc.vector.scalar_tensor_tensor(
                    out=hits[:], in0=rows[:, u, C_EXPERT:C_EXPERT + PICKS].unsqueeze(1).to_broadcast([128, 2, PICKS]),
                    scalar=slot_expert[:, bass.ds(j, 1)], in1=rows[:, u, C_WEIGHT:C_WEIGHT + 2 * PICKS].rearrange("p (a k) -> p a k", a=2),
                    op0=ALU.is_equal, op1=ALU.mult).then_inc(place_chain, 1)
                dve.wait_ge(place_chain, 2 * j + 1)
                if not first:
                    dve.wait_ge(result_sent[u], 16 * q)
                nc.vector.tensor_reduce(factor[:, u, :], hits[:], AX.X, ALU.add).then_inc(place_chain, 1)
                dve.wait_ge(place_chain, 2 * j + 2)
                nc.vector.tensor_tensor(place_i[:, u:u + 1], factor[:, u, 1:2], rows[:, u, C_OUTSIDE:C_OUTSIDE + 1],
                                        ALU.add).then_inc(place_ready, 1)

            def scale(j, u):
                dve.wait_ge(y_ready, j + 1)
                nc.vector.tensor_scalar(scaled[:, u % DEEP, :], pv[:, u % 2, 0:D], factor[:, u % DEEP, 0:1], None, ALU.mult).then_inc(y_scaled, 1)

            def octet(q, n, first, last):
                for u in range(n):
                    j = DEEP * q + u
                    if not (first and u < 1):
                        copy_hiddenT(j - 1, u - 1)
                    gated(j, u)
                    if not (first and u < 2):
                        scale(j - 2, u - 2)
                    if not (last and u == n - 1):
                        places(q + (u + 1) // DEEP, (u + 1) % DEEP, first and u + 1 < DEEP)
                if last:
                    copy_hiddenT(SLOTS - 1, n - 1)
                    scale(SLOTS - 2, n - 2)
                    scale(SLOTS - 1, n - 1)
            places(0, 0, True)
            octets(dve, octet)

            def combine(b, t, first):
                r, n = ROWS[t], NT * b + t
                dve.wait_ge(yc_in[t], 16 * (b + 1))
                nc.vector.tensor_tensor(yc[0:r, t, 0:2 * D], yc[0:r, t, 0:2 * D], yc[0:r, t, 2 * D:4 * D], ALU.add).then_inc(half_ready, 1)
                dve.wait_ge(half_ready, n + 1)
                nc.vector.tensor_tensor(yc[0:r, t, 0:D], yc[0:r, t, 0:D], yc[0:r, t, D:2 * D], ALU.add).then_inc(total_chain, 1)
                dve.wait_ge(total_chain, n + 1)
                dve.wait_ge(shared_ready, n + 1)
                nc.vector.tensor_tensor(total[0:r, t, :], total[0:r, t, :], yc[0:r, t, 0:D], ALU.add).then_inc(total_ready, 1)

            for t in range(NT):
                combine(0, t, True)
            with dve.Fori(1, B) as b:
                for t in range(NT):
                    combine(b, t, False)

        @block.gpsimd
        def _(pool):
            nc.gpsimd.memset(ident[:], 0.0).then_inc(pool_const, 1)
            nc.gpsimd.memset(mask_bf[:], 0.0).then_inc(pool_const, 1)
            pool.wait_ge(pool_const, 2)
            nc.gpsimd.affine_select(out=ident[:], in_=ident[:], pattern=[[-1, 128]], compare_op=ALU.not_equal, fill=1.0,
                                    base=0, channel_multiplier=1).then_inc(pool_const, 1)
            nc.gpsimd.affine_select(out=mask_bf[:], in_=mask_bf[:], pattern=[[0, 2], [-1, 128]], compare_op=ALU.is_ge,
                                    fill=NEG, base=0, channel_multiplier=1).then_inc(pool_const, 1)
            nc.gpsimd.iota(iota_e[:], pattern=[[1, E]], base=0, channel_multiplier=0,
                           allow_small_or_imprecise_dtypes=True).then_inc(pool_const, 1)
            nc.gpsimd.memset(tri_bf[:], 1.0).then_inc(route_const, 1)
            nc.gpsimd.memset(ones_bf[:], 1.0).then_inc(route_const, 1)
            pool.wait_ge(route_const, 1)
            nc.gpsimd.affine_select(out=tri_bf[:], in_=tri_bf[:], pattern=[[1, 128]], compare_op=ALU.is_gt,
                                    fill=0.0, base=0, channel_multiplier=-1).then_inc(route_const, 1)
            nc.gpsimd.memset(padding[:], 0.0).then_inc(pad_const, 1)
            pool.wait_ge(pad_const, 1)
            nc.gpsimd.memset(padding[:, C_EXPERT:C_EXPERT + PICKS], -1.0).then_inc(pad_const, 1)
            nc.gpsimd.memset(padding[:, C_OUTSIDE:C_OUTSIDE + 1], float(B * T * PICKS)).then_inc(pad_const, 1)
            nc.gpsimd.memset(n2[:], 0.0).then_inc(pad_const, 1)
            pool.wait_ge(pad_const, 4)
            nc.gpsimd.memset(n2[:, :, C_EXPERT + TOPK:C_EXPERT + PICKS], float(E)).then_inc(route_init, 1)
            nc.gpsimd.memset(n2[:, :, C_WEIGHT + TOPK:C_WEIGHT + PICKS], 1.0).then_inc(route_init, 1)
            nc.gpsimd.iota(n2[:, :, C_PLACE:C_PLACE + PICKS], pattern=[[PICKS * 128, NT], [1, PICKS]], base=-PICKS * T,
                           channel_multiplier=PICKS, allow_small_or_imprecise_dtypes=True).then_inc(route_init, 1)
            for dst, pattern, base in ((slot_no[:], [[1, SLOTS]], 0), (tile_start[:], [[128, TILES_OF_ONE]], 0),
                                       (region_start[:], [[REGION, NE]], 0), (next_row[:], [[REGION, NE]], 0),
                                       (up_to[:], [[-1, NE], [1, NE]], 0)):
                nc.gpsimd.iota(dst, pattern=pattern, base=base, channel_multiplier=0,
                               allow_small_or_imprecise_dtypes=True).then_inc(route_init, 1)
            pool.wait_ge(route_init, 8)
            nc.gpsimd.tensor_scalar(up_to[:], up_to[:], 0.0, None, ALU.is_le).then_inc(route_init, 1)
            nc.gpsimd.tensor_scalar(next_row[:, E:NE], next_row[:, E:NE], float(B * T), None, ALU.add).then_inc(route_init, 1)
            pool.wait_ge(vec_in, 16)
            nc.gpsimd.memset(neg_half[:], -0.5).then_inc(pool_const, 1)
            nc.gpsimd.tensor_scalar(bn_shift[:], var, EPS, None, ALU.add).then_inc(pool_const, 1)
            pool.wait_ge(pool_const, 7)
            nc.gpsimd.tensor_tensor(bn_scale[:], bn_shift[:], neg_half[:], ALU.pow).then_inc(pool_const, 1)
            pool.wait_ge(dve_const, 6)

            def step(s, p, F, M, X, R):
                f = s + 2

                def mask(h):
                    wait_apart(pool, exp_done, H * s + h + 1)
                    blocks = P[:, h % 8, :, 0:128]
                    nc.gpsimd.affine_select(out=blocks, in_=blocks, pattern=[[0, 2], [1, 128]], compare_op=ALU.is_ge,
                                            fill=0.0, base=0, channel_multiplier=-1)
                    block = P[:, h % 8, 1, T - 128:T]
                    nc.gpsimd.affine_select(out=block, in_=block, pattern=[[1, 128]], compare_op=ALU.is_ge,
                                            fill=0.0, base=0, channel_multiplier=-1).then_inc(masked, 1)

                def shift(t):
                    r, n = ROWS[t], NT * f + t
                    pool.wait_ge(bn_ready, n + 1)
                    nc.gpsimd.tensor_tensor(hcur[0:r, t, :], u2[0:r, t % 2, :], bn_shift[0:r], ALU.add).then_inc(h_ready, 1)
                    pool.wait_ge(h_ready, n + 1)
                    nc.gpsimd.tensor_tensor(resid[0:r, bass.ds(n, 1), :].rearrange("p a d -> p (a d)"), hcur[0:r, t, :],
                                            out_b[0:r], ALU.add).then_inc(resid_ready, 1)

                def inverse_deviation(t, chain, moments, out, n, ready):
                    pool.wait_ge(chain, 3 * n + 3)
                    nc.gpsimd.tensor_tensor(out[0:ROWS[t], t:t + 1], moments[0:ROWS[t], t, 1:2], neg_half[0:ROWS[t], 0:1],
                                            ALU.pow).then_inc(ready, 1)

                def parts(u):
                    half, qk, n = u // 2, u % 2, 4 * f + u
                    wait_apart(pool, evac["qk"], n + 1)
                    nc.gpsimd.tensor_copy(qkp[:, qk, 1, half, :], r1[:, u % 2, :]).then_inc(p2_done, 1)
                    pool.wait_ge(p2_done, n + 1)
                    nc.gpsimd.tensor_tensor(qkp[:, qk, 2, half, :], r1[:, u % 2, :], qkp[:, qk, 1, half, :],
                                            ALU.subtract).then_inc(parts_ready, 1)

                for h in range(H):
                    if X:
                        mask(h)
                    if F and 2 <= h < 5:
                        shift(h - 2)
                    if F and 3 <= h < 6:
                        inverse_deviation(h - 3, ln_chain, mv, rstd, NT * f + h - 3, rstd_ready)
                    if F and h in (10, 11):
                        parts(h - 10)
                    if F and h == 14:
                        parts(2)
                if F:
                    parts(3)
                if R:
                    wait_apart(pool, position_ready, s)
                    for t in range(NT):
                        for k in range(TOPK):
                            n = TOPK * t + k
                            nc.gpsimd.indirect_dma_start(
                                out=expert_rows, out_offset=bass.IndirectOffsetOnAxis(ap=row_i[0:ROWS[t], n:n + 1], axis=0),
                                in_=n2[0:ROWS[t], t, :], in_offset=None).then_inc(rows_sent, 16)
                if X:
                    for t in range(NT):
                        inverse_deviation(t, ln2_chain, mv2, rstd2, NT * s + t, rstd2_ready)
            steps(pool, step)

            def octet(q, n, first, last):
                for u in range(n):
                    wait_apart(pool, y_scaled, DEEP * q + u + 1)
                    nc.gpsimd.indirect_dma_start(
                        out=results, out_offset=bass.IndirectOffsetOnAxis(ap=place_i[:, u:u + 1], axis=0),
                        in_=scaled[:, u, :], in_offset=None, bounds_check=B * T * PICKS - 1, oob_is_err=False
                    ).then_inc(result_sent[u], 16)
            octets(pool, octet)

            def shared(b, t, first):
                r, n = ROWS[t], NT * b + t
                pool.wait_ge(yc_in[t], 16 * (b + 1))
                if not first:
                    pool.wait_ge(out_sent[t], 16 * b)
                nc.gpsimd.tensor_tensor(total[0:r, t, :], yc[0:r, t, TOPK * D:PICKS * D],
                                        resid[0:r, bass.ds(n, 1), :].rearrange("p a d -> p (a d)"), ALU.add).then_inc(shared_ready, 1)

            for t in range(NT):
                shared(0, t, True)
            with pool.Fori(1, B) as b:
                for t in range(NT):
                    shared(b, t, False)


def kernel(x, L0_tok_W, L0_tok_b, L0_tok_gamma, L0_tok_beta, L0_tok_running_mean, L0_tok_running_var,
           L0_attn_attn_W, L0_attn_attn_b, L0_attn_out_W, L0_attn_out_b,
           L0_ffn_gate_w, L0_ffn_w1, L0_ffn_w3, L0_ffn_w2, L0_ffn_sw1, L0_ffn_sw3, L0_ffn_sw2):
    import concourse.bacc as _bacc
    from concourse.bass_utils import run_bass_kernel_spmd as _run

    qkv_w = np.asarray(L0_attn_attn_W).reshape(D, H, 3, HS)
    qkv_b = np.asarray(L0_attn_attn_b).reshape(H, 3, HS)
    w13 = np.concatenate([np.concatenate([np.asarray(L0_ffn_w1), np.asarray(L0_ffn_w3)], 1),
                          np.concatenate([np.asarray(L0_ffn_sw1), np.asarray(L0_ffn_sw3)], 0)[None]], 0)
    w2 = np.concatenate([np.asarray(L0_ffn_w2), np.asarray(L0_ffn_sw2)[None]], 0)
    arrays = {
        "xT": np.asarray(x).transpose(0, 2, 1),
        "convw": np.asarray(L0_tok_W).reshape(D, CONTEXT, FEAT).transpose(2, 1, 0),
        "vec": np.concatenate([np.asarray(a).ravel() for a in (
            L0_tok_b, L0_tok_gamma, L0_tok_beta, L0_tok_running_mean, L0_tok_running_var, L0_attn_out_b, qkv_b[:, 2, :])]),
        "qkb": qkv_b[:, 0:2, :].transpose(1, 0, 2).reshape(2, KC, 128).transpose(2, 0, 1),
        "wqkv": qkv_w.transpose(0, 2, 1, 3).reshape(KC, 128, 3, D).transpose(1, 0, 2, 3),
        "wo": np.asarray(L0_attn_out_W).reshape(KC, 128, D).transpose(1, 0, 2),
        "gate": np.asarray(L0_ffn_gate_w).T.reshape(KC, 128, E).transpose(1, 0, 2),
        "w13": w13.transpose(2, 0, 1).reshape(KC, 128, NE, 2 * HID).transpose(1, 0, 2, 3),
        "w2": w2.transpose(2, 0, 1),
    }
    arrays = {k + "_in": np.ascontiguousarray(v) for k, v in arrays.items()}
    nc = _bacc.Bacc("TRN2", target_bir_lowering=False, num_devices=1)
    args = [nc.dram_tensor(n, a.shape, F32, kind="ExternalInput").ap() for n, a in arrays.items()]
    out = nc.dram_tensor("out", (B * T, D), F32, kind="ExternalOutput").ap()
    build(nc, *args, out)
    r = _run(nc, [arrays], core_ids=[0])
    return r.results[0]["out"].reshape(B, T, D)
```

```python
from contextlib import ExitStack

import numpy as np

import concourse.bass as bass
from concourse import mybir

B, T_IN, FEAT = 8, 375, 128
CONTEXT = 5
T = T_IN - (CONTEXT - 1)
D = 256
KC = D // 128
NT = -(-T // 128)
TP = NT * 128
ROWS = [min(128, T - 128 * t) for t in range(NT)]
H, HS = 16, 16
HH = H // 2
GROUPS = H // 4
PARTS = 3
Q_PART = [0, 0, 0, 1, 1, 2]
K_PART = [0, 1, 2, 0, 1, 0]
SROWS = HS * len(Q_PART)
XROWS = SROWS + PARTS
E, HID, TOPK = 16, 128, 4
N_WEIGHTS = 4
NE = E + 1
C_EXPERT, C_WEIGHT, C_PLACE, C_OUTSIDE = D, D + TOPK, D + 2 * TOPK, D + 3 * TOPK
ROW = D + 3 * TOPK + 1
REGION = B * T + 128
MAX_TILES = (B * T * TOPK + E * 127) // 128
TILES_OF_ONE = -(-B * T // 128)
SLOTS = MAX_TILES + TILES_OF_ONE
DEEP = 8
OCTETS = -(-SLOTS // DEEP)
SHARED = NT * B
SHARED_OCTETS = SHARED // DEEP
assert SHARED == TILES_OF_ONE and SHARED % DEEP == 0
EPS = 1e-5
NEG = -1.0e30
ROUTE_OPS = 13
VW = 32

F32 = mybir.dt.float32
BF16 = mybir.dt.bfloat16
U32 = mybir.dt.uint32
I32 = mybir.dt.int32
ALU = mybir.AluOpType
ACT = mybir.ActivationFunctionType
AX = mybir.AxisListType

WORK = ([("conv", 0, "F"), ("rt", 0, "R"), ("conv", 1, "F"), ("rt", 1, "R"), ("conv", 2, "F"), ("onorm", 0, "E"), ("lg", 0, "R")]
        + [("n1t", t, "F") for t in range(NT)] + [("mt", 0, "M"), ("onorm", 1, "E"), ("qk", 0, "F"), ("qk", 1, "F"), ("rk", 0, "R"), ("onorm", 2, "E"), ("qk", 2, "F"),
           ("qk", 3, "F"), ("onorm", 3, "E"), ("v", 0, "F"), ("ot", 0, "E"), ("ot", 1, "E"), ("mt", 1, "M")]
        + [("out", t, "E") for t in range(NT)] + [("v", 1, "F"), ("v", 2, "F")])
PER_BATCH = {"conv": NT, "n1t": NT, "qk": 4, "v": NT, "onorm": GROUPS, "ot": KC, "mt": 2, "out": NT,
             "rt": KC, "lg": 1, "rk": 1}
AHEAD = {"F": 2, "M": 1, "E": 0, "R": -1}


def stages(s):
    return {"F": s + 2 < B, "M": 0 <= s + 1 < B, "E": 0 <= s < B, "R": 0 <= s - 1 < B}


def work_plan():
    plan, held = {}, [None, None]
    for s in range(-2, B):
        n = sum(stages(s)[stage] for _, _, stage in WORK) % 2
        for name, k, stage in WORK:
            if stages(s)[stage]:
                was = held[n % 2]
                plan[s, name, k] = (n % 2, was and (was[0], was[1], was[2] - s))
                held[n % 2] = (name, k, s + AHEAD[stage])
                n += 1
    return plan


PLAN = work_plan()
for _s in range(1, B - 2):
    for _u in WORK:
        assert PLAN[_s, _u[0], _u[1]] == PLAN[1, _u[0], _u[1]]


def build(nc, xT_d, convw_d, vec_d, cols_d, qkb_d, wqkv_d, wo_d, gate_d, w13_d, w2_d, out_d):
    with ExitStack() as ctx:
        def sb(name, shape, dt=F32):
            return ctx.enter_context(nc.sbuf_tensor(name, shape, dt))

        def ps(name):
            return ctx.enter_context(nc.psum_tensor(name, [128, 2, 512], F32))

        def sem(name):
            return ctx.enter_context(nc.semaphore(name))

        qk_scratch = nc.dram_tensor("qk_scratch", (2, 2, PARTS, 128, T), BF16, kind="Internal").ap()
        expert_rows = nc.dram_tensor("expert_rows", (NE * REGION + 128, ROW), F32, kind="Internal").ap()
        results = nc.dram_tensor("results", (B * T * TOPK, D), F32, kind="Internal").ap()

        vec = sb("vec", [128, 6, D])
        conv_b, gamma, beta, mean, var, out_b = [vec[:, i, :] for i in range(6)]
        bn_scale = sb("bn_scale", [128, D])
        bn_shift = sb("bn_shift", [128, D])
        neg_half = sb("neg_half", [128, 1])
        cols = sb("cols", [128, 2, KC])
        var_col, vb_col = cols[:, 0, :], cols[:, 1, :]
        qkb = sb("qkb", [128, 2, KC])
        wo = sb("wo", [128, KC, D])
        gate = sb("gate", [128, KC, E])
        ident = sb("ident", [128, 128])
        ident_bf = sb("ident_bf", [128, 128], BF16)
        mask_bf = sb("mask_bf", [128, 2, 128], BF16)
        iota_e = sb("iota_e", [128, E])

        stats = sb("stats", [128, NT, 6])
        mv = sb("mv", [128, NT, 2])
        rstd = sb("rstd", [128, NT])
        resid = sb("resid", [128, B * NT, D])
        V = [sb(f"V{p}", [128, NT, H, VW]) for p in range(2)]
        nmax = sb("nmax", [128, NT, H])
        nm_res = sb("nm_res", [128, NT, HH])
        nm_parts = sb("nm_parts", [128, NT, PARTS, HH], BF16)
        nmT = sb("nmT", [PARTS * HH, TP], BF16)
        oT_raw = sb("oT_raw", [128, 2, TP])
        rden = sb("rden", [128, NT, 4])
        o = sb("o", [128, NT, D])
        oT = sb("oT", [128, KC, TP])
        stats2 = sb("stats2", [128, NT, 6])
        mv2 = sb("mv2", [128, NT, 2])
        rstd2 = sb("rstd2", [128, NT])
        n2s = [sb(f"n2_{p}", [128, NT, ROW]) for p in range(2)]

        tri_bf = sb("tri_bf", [128, 128], BF16)
        ones_bf = sb("ones_bf", [128, 128], BF16)
        padding = sb("padding", [128, ROW])
        slot_no = sb("slot_no", [NE, SLOTS])
        tile_start = sb("tile_start", [NE, TILES_OF_ONE])
        up_to = sb("up_to", [NE, NE])
        ones_f = sb("ones_f", [NE, 128])
        region_start = sb("region_start", [NE, 1])
        slot_offset = sb("slot_offset", [1, SLOTS])
        count = sb("count", [NE, 1])
        needs = sb("needs", [NE, TILES_OF_ONE])
        tiles = sb("tiles", [NE, 1])
        last_slot = sb("last_slot", [NE, 1])
        step_row = sb("step_row", [NE, 128])
        past = sb("past", [NE, SLOTS])
        slot_pick = sb("slot_pick", [128, SLOTS])
        slot_row = sb("slot_row", [1, SLOTS])
        next_row = sb("next_row", [128, NE])
        n2T = sb("n2T", [128, KC, TP])
        logit = sb("logit", [128, NT, E])
        top8 = sb("top8", [128, NT, 8])
        idx8 = sb("idx8", [128, NT, 8], U32)
        idxf = sb("idxf", [128, NT, TOPK])
        e4 = sb("e4", [128, NT, TOPK])
        esum = sb("esum", [128, NT])
        onehot = sb("onehot", [128, NT * TOPK, E])
        chosen = sb("chosen", [128, NT, E], BF16)
        position = sb("position", [128, NT, E])
        picked = sb("picked", [128, NT * TOPK, E])
        row_f = sb("row_f", [128, NT * TOPK])
        row_i = sb("row_i", [128, NT * TOPK], I32)

        early = ExitStack()

        def sbe(name, shape, dt=F32):
            return early.enter_context(nc.sbuf_tensor(name, shape, dt))

        convw = sbe("convw", [128, CONTEXT, D])
        wqkv = sbe("wqkv", [128, KC, 3, D])
        xT = sbe("xT", [128, T_IN])
        u1 = sbe("u1", [128, 2, D])
        u2 = sbe("u2", [128, 2, D])
        hcur = sbe("hcur", [128, NT, D])
        n1 = sbe("n1", [128, NT, D])
        n1T = sbe("n1T", [128, KC, TP])
        qkp = sbe("qkp", [128, 2, PARTS, KC, T], BF16)
        r1 = sbe("r1", [128, 2, T])
        Qs, Ks = [], []
        for p in range(2):
            Qs.append(sbe(f"Qs{p}", [XROWS, H, TP], BF16))
            Ks.append(sbe(f"Ks{p}", [XROWS, H, TP], BF16))
        P = sbe("P", [128, 8, 2, T])
        early.close()
        w13 = sb("w13", [128, KC, NE, 2 * HID])
        w2 = sb("w2", [128, NE, D])
        slot_expert_i = sb("slot_expert_i", [1, DEEP * OCTETS + 2], I32)
        slot_row_i = sb("slot_row_i", [1, SLOTS], I32)
        next_row_i = sb("next_row_i", [1, NE], I32)
        rows = sb("rows", [128, DEEP, ROW])
        rowsT = sb("rowsT", [128, 2, D])
        silu = sb("silu", [128, 2, HID])
        hidden = sb("hidden", [128, 2, HID])
        hiddenT = sb("hiddenT", [128, 2, 128])
        hits = sb("hits", [128, 2, TOPK])
        factor = sb("factor", [128, DEEP, 2])
        place_i = sb("place_i", [128, DEEP], I32)
        scaled = sb("scaled", [128, DEEP, D])
        yc = sb("yc", [128, NT, TOPK * D])
        total = sb("total", [128, NT, D])

        work, ex, mx, pv = ps("work"), ps("ex"), ps("mx"), ps("pv")

        const_in, vec_in, pool_const, prep = sem("const_in"), sem("vec_in"), sem("pool_const"), sem("prep")
        v_const, fold_ready, bias_ready, convw_in, pads_ready, var_in, deviation_ready, scale_ready, ones_in = sem("v_const"), sem("fold_ready"), sem("bias_ready"), sem("convw_in"), sem("pads_ready"), sem("var_in"), sem("deviation_ready"), sem("scale_ready"), sem("ones_in")
        dve_const, x_in = sem("dve_const"), sem("x_in")
        route_const, route_init = sem("route_const"), sem("route_init")
        conv_ready, conv_chain, bn_ready, h_ready = sem("conv_ready"), sem("conv_chain"), sem("bn_ready"), sem("h_ready")
        ln_chain, rstd_ready, n1_ready = sem("ln_chain"), sem("rstd_ready"), sem("n1_ready")
        n1t_ready, qk_ready, p1_ready = sem("n1t_ready"), sem("qk_ready"), sem("p1_ready")
        p2_done, parts_ready = sem("p2_done"), sem("parts_ready")
        qk_stored = [sem(f"qk_stored{i}") for i in range(2)]
        stack_in = [sem(f"stack_in{i}") for i in range(2)]
        v_mm_ready = sem("v_mm_ready")
        mxa_ready, mxb_ready, mxa_done, mxb_done = sem("mxa_ready"), sem("mxb_ready"), sem("mxa_done"), sem("mxb_done")
        nm_chain, nmt_ready, = sem("nm_chain"), sem("nmt_ready")
        nmax_in = [sem(f"nmax_in{i}") for i in range(2)]
        ex_ready, exp_done, masked = sem("ex_ready"), sem("exp_done"), sem("masked")
        pv_ready, raw_ready, rawt_ready, rden_ready = sem("pv_ready"), sem("raw_ready"), sem("rawt_ready"), sem("rden_ready")
        ott_ready, out_ready = sem("ott_ready"), sem("out_ready")
        ln2_chain, rstd2_ready, n2_ready, shared_sent = sem("ln2_chain"), sem("rstd2_ready"), sem("n2_ready"), sem("shared_sent")
        resid_ready, waited = sem("resid_ready"), sem("waited")
        w_in = sem("w_in")
        n2t_ready, logits_ready, ranks_ready = sem("n2t_ready"), sem("logits_ready"), sem("ranks_ready")
        rt_chain, chosen_ready, margin_ready, e4_ready = sem("rt_chain"), sem("chosen_ready"), sem("margin_ready"), sem("e4_ready")
        position_ready, rows_sent, pad_const, pad_sent = sem("position_ready"), sem("rows_sent"), sem("pad_const"), sem("pad_sent")
        tb_chain, counted, table_ready = sem("tb_chain"), sem("counted"), sem("table_ready")
        rows_no_ready, last_ready, slots_ready = sem("rows_no_ready"), sem("last_ready"), sem("slots_ready")
        rows_in = [sem(f"rows_in{u}") for u in range(DEEP)]
        result_sent = [sem(f"result_sent{u}") for u in range(DEEP)]
        rowt_ready, rowT_copied, hid_ready, silu_ready = sem("rowt_ready"), sem("rowT_copied"), sem("hid_ready"), sem("silu_ready")
        hidden_ready, hiddent_ready, hiddenT_copied = sem("hidden_ready"), sem("hiddent_ready"), sem("hiddenT_copied")
        y_ready, y_scaled, place_chain, place_ready = sem("y_ready"), sem("y_scaled"), sem("place_chain"), sem("place_ready")
        yc_in = [sem(f"yc_in{t}") for t in range(NT)]
        half_ready, shared_ready, total_chain, total_ready = sem("half_ready"), sem("shared_ready"), sem("total_chain"), sem("total_ready")
        out_sent = [sem(f"out_sent{t}") for t in range(NT)]
        evac = {name: sem(f"{name}_evacuated") for name in PER_BATCH}

        def wait(eng, s, value):
            if not isinstance(value, int) or value > 0:
                eng.wait_ge(s, value)

        def wait_apart(eng, s, value):
            wait(eng, s, value)
            if not isinstance(value, int):
                eng.sem_inc(waited, 1)

        def plan(s, name, k):
            return PLAN[s if isinstance(s, int) else 1, name, k]

        def scores_bank(h, M):
            return ex if M or h % 2 == 0 else mx

        def route_place(s, name, k):
            if isinstance(s, int) and s == B:
                return mx[:, 1, :]
            return work[:, plan(s, name, k)[0], :]

        def steps(eng, step):
            step(-2, 0, True, False, False, False)
            step(-1, 1, True, True, False, False)
            step(0, 0, True, True, True, False)
            step(1, 1, True, True, True, True)
            with eng.Fori(1, (B - 2) // 2) as pair:
                step(2 * pair, 0, True, True, True, True)
                step(2 * pair + 1, 1, True, True, True, True)
            step(B - 2, 0, False, True, True, True)
            step(B - 1, 1, False, False, True, True)

        def octets(eng, octet):
            for q in range(SHARED_OCTETS + 1):
                octet(q, DEEP, q == 0, False)
            with eng.Fori(SHARED_OCTETS + 1, OCTETS - 1) as q:
                octet(q, DEEP, False, False)
            octet(OCTETS - 1, SLOTS - DEEP * (OCTETS - 1), False, True)

        block = ctx.enter_context(nc.Block())

        @block.sync
        def _(sp):
            sp.dma_start(cols[:], cols_d).then_inc(var_in, 16)
            sp.dma_start(convw[:], convw_d).then_inc(convw_in, 16)
            for dst, src in ((wqkv, wqkv_d), (qkb, qkb_d)):
                sp.dma_start(dst[:], src).then_inc(const_in, 16)
            sp.dma_start(vec[:].rearrange("p a d -> p (a d)"), vec_d.partition_broadcast(128)).then_inc(vec_in, 16)
            for dst, src in ((wo, wo_d), (gate, gate_d)):
                sp.dma_start(dst[:], src).then_inc(const_in, 16)

            def step(s, p, F, M, X, R):
                f, m = s + 2, s + 1
                for half in range(2):
                    if M:
                        wait_apart(sp, evac["mt"], 2 * m + half + 1)
                        for i in range(PARTS):
                            sp.dma_start(Qs[1 - p][SROWS + i:SROWS + i + 1, half * HH:(half + 1) * HH, 0:T],
                                         nmT[i * HH:(i + 1) * HH, 0:T]).then_inc(nmax_in[half], 16)
                    if F:
                        wait_apart(sp, parts_ready, 4 * f + 2 * half + 2)
                        wait_apart(sp, stack_in[half], 16 * 12 * f)
                        sp.dma_start(qk_scratch[half].rearrange("q a p t -> p q a t"),
                                     qkp[:, :, :, half, :]).then_inc(qk_stored[half], 16)
                        if X:
                            wait_apart(sp, ex_ready, H * s + (half + 1) * HH)
                        wait_apart(sp, qk_stored[half], 16 * (f + 1))
                        for qk, (stack, part) in enumerate(((Qs, Q_PART), (Ks, K_PART))):
                            for c in range(len(part)):
                                sp.dma_start(stack[p][HS * c:HS * (c + 1), half * HH:(half + 1) * HH, 0:T],
                                             qk_scratch[half, qk, part[c]].rearrange("(h d) t -> d h t", d=HS)
                                             ).then_inc(stack_in[half], 16)
                if X and not M:
                    sp.wait_ge(v_mm_ready, NT * B)
                    sp.wait_ge(parts_ready, 4 * B)
                    sp.wait_ge(resid_ready, NT * B)
                    for half in range(2):
                        sp.wait_ge(qk_stored[half], 16 * B)
                    sp.wait_ge(n2_ready, NT * (B - 1))
                    for c in range(KC):
                        sp.dma_start(w13[:, c], w13_d[:, c]).then_inc(w_in, 16)
                    sp.wait_ge(ex_ready, H * (B - 1))
                    sp.dma_start(w2[:], w2_d).then_inc(w_in, 16)
                if R:
                    wait_apart(sp, position_ready, s)
                    for t in range(NT):
                        sp.dma_start(expert_rows[bass.ds(128 * (NT * (s - 1) + t), 128)], n2s[1 - p][:, t, :]
                                     ).then_inc(shared_sent, 16)
            sp.wait_ge(pad_const, 5)
            sp.dma_start(expert_rows[NE * REGION:NE * REGION + 128], padding[:]).then_inc(pad_sent, 16)
            steps(sp, step)

            slot_regs = [sp.alloc_register(f"row{u}") for u in range(DEEP)]
            region_regs = [sp.alloc_register(f"region{e}") for e in range(E)]
            sp.wait_ge(shared_sent, 16 * NT * (B - 1))
            sp.wait_ge(pad_sent, 16)
            sp.wait_ge(pv_ready, GROUPS * B)
            sp.wait_ge(masked, H * B)

            def load_slot(q, u, row):
                j = DEEP * q + u
                if not isinstance(q, int) or q > 0:
                    wait_apart(sp, rowt_ready, j - DEEP + 1)
                if not isinstance(q, int) or q > SHARED_OCTETS:
                    wait_apart(sp, place_ready, j - DEEP + 1 - SHARED)
                sp.dma_start(rows[:, u, :], expert_rows[bass.ds(row, 128)]).then_inc(rows_in[u], 16)

            def octet(q, n):
                sp.load(slot_regs[0:n], slot_row_i[0:1, bass.ds(DEEP * q, n)])
                for u in range(n):
                    load_slot(q, u, sp.snap(slot_regs[u], min_val=0, max_val=NE * REGION))

            def load_shared(j):
                load_slot(j // DEEP, j % DEEP, 128 * j)

            for j in range(13):
                load_shared(j)
            sp.wait_ge(position_ready, B)
            for t in range(NT):
                row = 128 * (NT * (B - 1) + t)
                sp.dma_start(expert_rows[row:row + 128], n2s[1][:, t, :]).then_inc(shared_sent, 16)
            sp.wait_ge(counted, 1)
            sp.load(region_regs, next_row_i[0:1, 1:NE])
            for e in range(E):
                row = sp.snap(region_regs[e], min_val=0, max_val=NE * REGION)
                sp.dma_start(expert_rows[bass.ds(row, 128)], padding[:]).then_inc(pad_sent, 16)
                if e % 2:
                    load_shared(13 + e // 2)
            sp.wait_ge(shared_sent, 16 * NT * B)
            for j in range(21, SHARED):
                load_shared(j)
            sp.wait_ge(table_ready, 2)
            sp.wait_ge(pad_sent, 16 * (E + 1))
            sp.wait_ge(rows_sent, 16 * NT * TOPK * B)
            octet(SHARED_OCTETS, DEEP)
            with sp.Fori(SHARED_OCTETS + 1, OCTETS - 1) as q:
                octet(q, DEEP)
            octet(OCTETS - 1, SLOTS - DEEP * (OCTETS - 1))

            for u in range(DEEP):
                sp.wait_ge(result_sent[u], 16 * ((SLOTS - SHARED - 1 - u) // DEEP + 1))

            def load(b, t):
                sp.dma_start(yc[0:ROWS[t], t, :], results[bass.ds(TOPK * (T * b + 128 * t), TOPK * ROWS[t])]
                             .rearrange("(p k) d -> p (k d)", k=TOPK)).then_inc(yc_in[t], 16)

            def store(b, t):
                wait_apart(sp, total_ready, NT * b + t + 1)
                sp.dma_start(out_d[bass.ds(T * b + 128 * t, ROWS[t])], total[0:ROWS[t], t, :]).then_inc(out_sent[t], 16)

            for t in range(NT):
                load(0, t)
            with sp.Fori(0, B - 1) as b:
                for t in range(NT):
                    store(b, t)
                    load(b + 1, t)
            for t in range(NT):
                store(B - 1, t)
            for t in range(NT):
                sp.wait_ge(out_sent[t], 16 * B)

        @block.tensor
        def _(pe):
            pe.wait_ge(convw_in, 16)
            pe.wait_ge(pool_const, 4)
            pe.wait_ge(deviation_ready, 1)
            for c in range(KC):
                mm = pe.matmul(pv[:, 0, 128 * c:128 * (c + 1)], var_col[:, c:c + 1].to_broadcast([128, 128]), ident[:],
                               start=True, stop=True)
            mm.then_inc(scale_ready, 1)
            pe.wait_ge(dve_const, 1)

            def route_bank(s, name, k):
                if isinstance(s, int) and s == B:
                    if name == "rt" and k == 1:
                        pe.wait_ge(evac["rt"], KC * (B - 1) + 1)
                    if name == "rk":
                        pe.wait_ge(evac["lg"], B)
                    return route_place(s, name, k)
                was = plan(s, name, k)[1]
                pe.wait_ge(evac[was[0]], PER_BATCH[was[0]] * (s + was[2]) + was[1] + 1)
                return route_place(s, name, k)

            def transpose_n2(s, p, c):
                w = route_bank(s, "rt", c)
                pe.wait_ge(n2_ready, NT * s)
                for t in range(NT):
                    mm = pe.transpose(w[:, 128 * t:128 * t + ROWS[t]], n2s[1 - p][0:ROWS[t], t, 128 * c:128 * (c + 1)],
                                      ident[0:ROWS[t], 0:ROWS[t]])
                mm.then_inc(n2t_ready, 1)

            def gate_logits(s):
                w = route_bank(s, "lg", 0)
                pe.wait_ge(evac["rt"], KC * s)
                for t in range(NT):
                    for c in range(KC):
                        mm = pe.matmul(w[:, E * t:E * (t + 1)], n2T[:, c, 128 * t:128 * (t + 1)], gate[:, c, :],
                                       start=(c == 0), stop=(c == KC - 1))
                mm.then_inc(logits_ready, 1)

            def ranks(s):
                w = route_bank(s, "rk", 0)
                pe.wait_ge(chosen_ready, s)
                pe.wait_ge(route_const, 3)
                for t in range(NT + 1):
                    for before in range(min(t, NT - 1) + 1):
                        rows_before = tri_bf if before == t else ones_bf
                        last = before == min(t, NT - 1)
                        mm = pe.matmul(w[:, E * t:E * (t + 1)], rows_before[0:ROWS[before], :],
                                       chosen[0:ROWS[before], before, :], start=(before == 0), stop=last)
                mm.then_inc(ranks_ready, 1)

            def step(s, p, F, M, X, R):
                f, m = s + 2, s + 1

                def bank(name, k):
                    b, was = plan(s, name, k)
                    if was is not None:
                        wait(pe, evac[was[0]], PER_BATCH[was[0]] * (s + was[2]) + was[1] + 1)
                    return work[:, b, :]

                def maxima_scores_a(h):
                    if h % HH == 0:
                        pe.wait_ge(stack_in[h // HH], 16 * 12 * (m + 1))
                    q, k = Qs[1 - p], Ks[1 - p]
                    wait(pe, mxa_done, H * m + h)
                    pe.matmul(mx[:, 0, 256:T], ident_bf[:], mask_bf[:, 0, 0:T - 256], start=True, stop=False, skip_group_check=True)
                    pe.matmul(mx[:, 0, 0:T], q[0:SROWS, h, 256:TP], k[0:SROWS, h, 0:T], start=False, stop=True,
                              skip_group_check=True).then_inc(mxa_ready, 1)

                def maxima_scores_b(h):
                    q, k = Qs[1 - p], Ks[1 - p]
                    wait(pe, mxb_done, H * m + h)
                    pe.matmul(mx[:, 1, :].rearrange("p (a c) -> p a c", a=2)[:, :, 0:128], ident_bf[:], mask_bf[:], start=True, stop=False, skip_group_check=True)
                    pe.matmul(mx[:, 1, 0:128], q[0:SROWS, h, 0:128], k[0:SROWS, h, 0:128], start=False, stop=False, skip_group_check=True)
                    pe.matmul(mx[:, 1, 128:384], q[0:SROWS, h, 128:256], k[0:SROWS, h, 0:256], start=False, stop=True,
                              skip_group_check=True).then_inc(mxb_ready, 1)

                def exp_scores(h):
                    if h % HH == 0:
                        pe.wait_ge(nmax_in[h // HH], 16 * PARTS * (s + 1))
                    if h == 0:
                        pe.wait_ge(ones_in, 16 * 2 * PARTS)
                    q, k = Qs[p], Ks[p]
                    ex = scores_bank(h, M)
                    if not M and h < 2:
                        pe.wait_ge(exp_done, H * s)
                        pe.wait_ge(mxb_done, H * B)
                    elif not M:
                        pe.wait_ge(exp_done, H * s + h - 1)
                    elif h:
                        pe.wait_ge(exp_done, H * s + h)
                    pe.matmul(ex[:, 0, 0:T], k[:, h, 0:128], q[:, h, 0:T], start=True, stop=True)
                    pe.matmul(ex[:, 1, 0:T - 128], k[:, h, 128:256], q[:, h, 128:T], start=True, stop=True)
                    pe.matmul(ex[:, 1, T - 128:T], k[:, h, 256:TP], q[:, h, 256:TP], start=True, stop=True).then_inc(ex_ready, 1)

                def weigh_values(g):
                    pe.wait_ge(masked, H * s + 4 * g + 4)
                    if g == 0:
                        pe.wait_ge(evac["v"], NT * (s + 1))
                    for kt in range(NT):
                        for j in range(4):
                            h = 4 * g + j
                            q0 = 128 * kt
                            probs = P[:, h % 8, 0, :] if kt == 0 else P[:, h % 8, 1, 0:T - 128] if kt == 1 \
                                else P[:, h % 8, 1, T - 128:T - 128 + T - 256]
                            mm = pe.matmul(pv[32 * j:32 * j + VW, g % 2, q0:T], V[p][:, kt, h, :], probs,
                                           start=(kt == 0), stop=(kt == NT - 1))
                    mm.then_inc(pv_ready, 1)

                def transpose_raw(g):
                    w = bank("onorm", g)
                    pe.wait_ge(raw_ready, GROUPS * s + g + 1)
                    for t in range(NT):
                        mm = pe.transpose(w[:, 128 * t:128 * (t + 1)], oT_raw[:, g % 2, 128 * t:128 * (t + 1)], ident[:])
                    mm.then_inc(rawt_ready, 1)

                def conv(t):
                    w = bank("conv", t)
                    if t == 0:
                        pe.wait_ge(x_in, 16 * (f + 1))
                    for c in range(CONTEXT):
                        mm = pe.matmul(w[0:ROWS[t], 0:D], xT[:, 128 * t + c:128 * t + c + ROWS[t]], convw[:, c, :],
                                       start=(c == 0), stop=(c == CONTEXT - 1))
                    mm.then_inc(conv_ready, 1)

                def transpose_n1(t):
                    w = bank("n1t", t)
                    pe.wait_ge(n1_ready, NT * f + t + 1)
                    for c in range(KC):
                        mm = pe.transpose(w[:, 128 * c:128 * c + ROWS[t]], n1[0:ROWS[t], t, 128 * c:128 * (c + 1)],
                                          ident[0:ROWS[t], 0:ROWS[t]])
                    mm.then_inc(n1t_ready, 1)

                def project_qk(u):
                    w = bank("qk", u)
                    half, qk = u // 2, u % 2
                    if u == 0:
                        pe.wait_ge(evac["n1t"], NT * (f + 1))
                    if u == 0 and not M:
                        pe.wait_ge(const_in, 16 * N_WEIGHTS)
                        pe.wait_ge(prep, 1)
                    for c in range(KC):
                        mm = pe.matmul(w[:, 0:T], wqkv[:, c, qk, 128 * half:128 * (half + 1)], n1T[:, c, 0:T],
                                       start=(c == 0), stop=(c == KC - 1))
                    mm.then_inc(qk_ready, 1)

                def project_v(t):
                    w = bank("v", t)
                    for c in range(KC):
                        mm = pe.matmul(w[0:ROWS[t], 0:D], n1T[:, c, 128 * t:128 * t + ROWS[t]], wqkv[:, c, 2, :],
                                       start=(c == 0), stop=(c == KC - 1))
                    mm.then_inc(v_mm_ready, 1)

                def transpose_maxima(half):
                    w = bank("mt", half)
                    pe.wait_ge(nm_chain, 8 * m + 4 * half + 4)
                    for t in range(NT):
                        mm = pe.transpose(w.bitcast(BF16)[0:PARTS * HH, 128 * t:128 * (t + 1)],
                                          nm_parts[:, t, :, :].rearrange("p a h -> p (a h)"), ident_bf[:])
                    mm.then_inc(nmt_ready, 1)

                def transpose_o(c):
                    w = bank("ot", c)
                    if c == 0:
                        pe.wait_ge(evac["onorm"], GROUPS * (s + 1))
                    for t in range(NT):
                        mm = pe.transpose(w[:, 128 * t:128 * (t + 1)], o[:, t, 128 * c:128 * (c + 1)], ident[:])
                    mm.then_inc(ott_ready, 1)

                def project_out(t):
                    w = bank("out", t)
                    if t == 0:
                        pe.wait_ge(evac["ot"], KC * (s + 1))
                    for c in range(KC):
                        mm = pe.matmul(w[0:ROWS[t], 0:D], oT[:, c, 128 * t:128 * t + ROWS[t]], wo[:, c, :],
                                       start=(c == 0), stop=(c == KC - 1))
                    mm.then_inc(out_ready, 1)

                def fold_bias():
                    pe.wait_ge(const_in, 16 * N_WEIGHTS)
                    pe.wait_ge(dve_const, 2)
                    for c in range(KC):
                        mm = pe.matmul(pv[:, 0, 0:D], vb_col[:, c:c + 1].to_broadcast([128, 128]), wo[:, c, :],
                                       start=(c == 0), stop=(c == KC - 1))
                    mm.then_inc(fold_ready, 1)

                for h in range(H):
                    if F and not M and h == 5:
                        fold_bias()
                    if M:
                        maxima_scores_a(h)
                    if X:
                        exp_scores(h)
                    if M:
                        maxima_scores_b(h)
                    if F and 2 <= h < 5:
                        conv(h - 2)
                    if R and 2 <= h < 2 + KC:
                        transpose_n2(s, p, h - 2)
                    if X and h == 5:
                        transpose_raw(0)
                    if R and h == 5:
                        gate_logits(s)
                    if F and 6 <= h < 9:
                        transpose_n1(h - 6)
                    if M and h == 9:
                        transpose_maxima(0)
                    if X and h == 9:
                        transpose_raw(1)
                    if F and h in (10, 11):
                        project_qk(h - 10)
                    if R and h == 12:
                        ranks(s)
                    if X and h in (4, 8, 12):
                        weigh_values(h // 4 - 1)
                    if X and h == 13:
                        transpose_raw(2)
                    if F and h == 14:
                        project_qk(2)
                if F:
                    project_qk(3)
                if X:
                    weigh_values(3)
                    transpose_raw(3)
                if F:
                    project_v(0)
                if X:
                    transpose_o(0)
                    transpose_o(1)
                if M:
                    transpose_maxima(1)
                if X:
                    for t in range(NT):
                        project_out(t)
                if F:
                    project_v(1)
                    project_v(2)
            steps(pe, step)

            pe.wait_ge(w_in, 16 * 3)
            pe.wait_ge(exp_done, H * B)
            pe.wait_ge(raw_ready, GROUPS * B)
            pe.wait_ge(evac["out"], NT * B)

            def slots_table(k):
                if k == 0:
                    pe.wait_ge(evac["rk"], B)
                    pe.transpose(mx[0:NE, 1, 0:128], next_row[:], ident[:]).then_inc(rows_no_ready, 1)
                elif k == 1:
                    pe.wait_ge(tb_chain, 3)
                    pe.matmul(mx[0:NE, 1, 0:1], up_to[:], tiles[:], start=True, stop=True).then_inc(last_ready, 1)
                else:
                    pe.wait_ge(tb_chain, 6)
                    pe.matmul(mx[:, 1, 0:SLOTS], ones_f[:], past[:], start=True, stop=True)
                    pe.matmul(mx[:, 1, 256:256 + SLOTS], step_row[:], past[:], start=True, stop=True).then_inc(slots_ready, 1)

            expert_regs = [pe.alloc_register(f"expert{u}") for u in range(DEEP + 2)]

            def transpose_rows(q, u):
                j = DEEP * q + u
                pe.wait_ge(rows_in[u], 16 * (q + 1))
                wait(pe, rowT_copied, j - 1)
                for c in range(KC):
                    mm = pe.transpose(work[:, u % 2, 128 * c:128 * (c + 1)], rows[:, u, 128 * c:128 * (c + 1)], ident[:])
                mm.then_inc(rowt_ready, 1)

            def hidden_units(j, u, e):
                pe.wait_ge(rowT_copied, j + 1)
                wait(pe, hidden_ready, j - 1)
                for c in range(KC):
                    mm = pe.matmul(ex[:, u % 2, 0:2 * HID], rowsT[:, u % 2, 128 * c:128 * (c + 1)],
                                   w13[:, c, bass.ds(e, 1), :].rearrange("p a h -> p (a h)") if e is not None else w13[:, c, 0, :], start=(c == 0), stop=(c == KC - 1))
                mm.then_inc(hid_ready, 1)

            def transpose_hidden(j, u):
                pe.wait_ge(hidden_ready, j + 1)
                wait(pe, hiddenT_copied, j)
                pe.transpose(mx[:, 0, 0:128], hidden[:, u % 2, :], ident[:]).then_inc(hiddent_ready, 1)

            def expert_out(j, u, e):
                pe.wait_ge(hiddenT_copied, j + 1)
                wait(pe, y_scaled, j - 1)
                pe.matmul(pv[:, u % 2, 0:D], hiddenT[:, u % 2, :], w2[:, bass.ds(e, 1), :].rearrange("p a d -> p (a d)") if e is not None else w2[:, 0, :],
                          start=True, stop=True).then_inc(y_ready, 1)

            def octet(q, n, first, last):
                if isinstance(q, int) and q < SHARED_OCTETS:
                    expert = [None] * (DEEP + 2)
                else:
                    pe.wait_ge(table_ready, 2)
                    pe.load(expert_regs, slot_expert_i[0:1, bass.ds(DEEP * q, DEEP + 2)])
                    expert = [pe.snap(reg, min_val=0, max_val=NE - 1) for reg in expert_regs]
                for u in range(n):
                    j = DEEP * q + u
                    if not (last and u == n - 1):
                        transpose_rows(q + (u + 1) // DEEP, (u + 1) % DEEP)
                    hidden_units(j, u, expert[u + 2])
                    if not (first and u < 1):
                        transpose_hidden(j - 1, u - 1)
                    if not (first and u < 2):
                        expert_out(j - 2, u - 2, expert[u])
                    if isinstance(j, int):
                        if j < KC:
                            transpose_n2(B, 0, j)
                        if j == 3:
                            gate_logits(B)
                        if j == 6:
                            ranks(B)
                        if j in (8, 10, 12):
                            slots_table((j - 8) // 2)
                if last:
                    transpose_hidden(SLOTS - 1, n - 1)
                    expert_out(SLOTS - 2, n - 2, expert[n])
                    expert_out(SLOTS - 1, n - 1, expert[n + 1])
            transpose_rows(0, 0)
            octets(pe, octet)

        @block.scalar
        def _(act):
            def copy_n2T(s, c):
                act.wait_ge(n2t_ready, KC * (s - 1) + c + 1)
                nc.scalar.activation(n2T[:, c, 0:T], route_place(s, "rt", c)[:, 0:T], ACT.Copy).then_inc(evac["rt"], 1)

            def choice_exponentials(s):
                act.wait_ge(margin_ready, s)
                nc.scalar.activation(e4[:], e4[:], ACT.Exp).then_inc(e4_ready, 1)

            def step(s, p, F, M, X, R):
                f, m = s + 2, s + 1

                def bank(name, k):
                    return work[:, plan(s, name, k)[0], :]

                def exponentials(h):
                    act.wait_ge(ex_ready, H * s + h + 1)
                    if h >= 8:
                        act.wait_ge(pv_ready, GROUPS * s + h // 4 - 1)
                    nc.scalar.activation(P[:, h % 8, :, :], scores_bank(h, M)[:, :, 0:T], ACT.Exp).then_inc(exp_done, 1)

                def copy_raw(g):
                    act.wait_ge(pv_ready, GROUPS * s + g + 1)
                    nc.scalar.activation(oT_raw[:, g % 2, 0:T], pv[:, g % 2, 0:T], ACT.Copy).then_inc(raw_ready, 1)

                def copy_n1T(t):
                    act.wait_ge(n1t_ready, NT * f + t + 1)
                    w = bank("n1t", t).rearrange("p (c n) -> p c n", n=128)
                    nc.scalar.activation(n1T[:, :, 128 * t:128 * t + ROWS[t]], w[:, 0:KC, 0:ROWS[t]],
                                         ACT.Copy).then_inc(evac["n1t"], 1)

                def first_part(u):
                    half, qk = u // 2, u % 2
                    if not M and u == 0:
                        act.wait_ge(prep, 1)
                    act.wait_ge(qk_ready, 4 * f + u + 1)
                    wait(act, qk_stored[half], 16 * f)
                    nc.scalar.activation(qkp[:, qk, 0, half, :], bank("qk", u)[:, 0:T], ACT.Identity,
                                         bias=qkb[:, qk, half:half + 1]).then_inc(p1_ready, 1)

                def second_part(u):
                    half, qk = u // 2, u % 2
                    act.wait_ge(evac["qk"], 4 * f + u + 1)
                    nc.scalar.activation(qkp[:, qk, 1, half, :], r1[:, u % 2, :], ACT.Copy).then_inc(p2_done, 1)

                def values(t):
                    act.wait_ge(v_mm_ready, NT * f + t + 1)
                    if X and t == 0:
                        act.wait_ge(pv_ready, GROUPS * (s + 1))
                    if not X and t == 0:
                        act.wait_ge(v_const, 2)
                    r = ROWS[t]
                    nc.scalar.activation(V[p][0:r, t, :, 0:HS], bank("v", t)[0:r, 0:D].rearrange("p (h d) -> p h d", h=H),
                                         ACT.Copy).then_inc(evac["v"], 1)

                def copy_maxima(half):
                    act.wait_ge(nmt_ready, 2 * m + half + 1)
                    wait(act, nmax_in[1 - half], 16 * PARTS * (m + half))
                    nc.scalar.activation(nmT[:, 0:T], bank("mt", half).bitcast(BF16)[0:PARTS * HH, 0:T],
                                         ACT.Copy).then_inc(evac["mt"], 1)

                def copy_oT(c):
                    act.wait_ge(ott_ready, KC * s + c + 1)
                    nc.scalar.activation(oT[:, c, :], bank("ot", c)[:, 0:TP], ACT.Copy).then_inc(evac["ot"], 1)

                if F:
                    wait_apart(act, conv_ready, NT * f)
                    act.dma_start(xT[:], xT_d[bass.ds(f, 1)].rearrange("a p t -> (a p) t")).then_inc(x_in, 16)
                if F and not M:
                    act.wait_ge(route_const, 3)
                    act.wait_ge(pads_ready, 4)
                    for stack in Ks:
                        for i in range(SROWS, XROWS):
                            act.dma_start(stack[i:i + 1, :, :].rearrange("p h (c n) -> p (h c) n", n=128),
                                          ones_bf[0:H * NT, :]).then_inc(ones_in, 16)
                for h in range(H):
                    if X:
                        exponentials(h)
                    if R and 2 <= h < 2 + KC:
                        copy_n2T(s, h - 2)
                    if R and h == 9:
                        choice_exponentials(s)
                    if F and 6 <= h < 9:
                        copy_n1T(h - 6)
                    if M and h == 9:
                        copy_maxima(0)
                    if F and h in (10, 11):
                        first_part(h - 10)
                    if F and h in (11, 12):
                        second_part(h - 11)
                    if X and h in (4, 8, 12):
                        copy_raw(h // 4 - 1)
                    if F and h == 14:
                        first_part(2)
                if F:
                    first_part(3)
                    second_part(2)
                    second_part(3)
                if X:
                    copy_raw(3)
                if F:
                    values(0)
                if X:
                    copy_oT(0)
                    copy_oT(1)
                if M:
                    copy_maxima(1)
                if F:
                    values(1)
                    values(2)
            steps(act, step)

            def copy_rowsT(j, u):
                act.wait_ge(rowt_ready, j + 1)
                wait(act, hid_ready, j - 1)
                nc.scalar.activation(rowsT[:, u % 2, :], work[:, u % 2, 0:D], ACT.Copy).then_inc(rowT_copied, 1)

            def octet(q, n, first, last):
                for u in range(n):
                    j = DEEP * q + u
                    if not (last and u == n - 1):
                        copy_rowsT(j + 1, u + 1)
                    act.wait_ge(hid_ready, j + 1)
                    wait(act, hidden_ready, j - 1)
                    nc.scalar.activation(silu[:, u % 2, :], ex[:, u % 2, 0:HID], ACT.Silu).then_inc(silu_ready, 1)
                    if isinstance(j, int):
                        if j < KC:
                            copy_n2T(B, j)
                        if j == 5:
                            choice_exponentials(B)
            copy_rowsT(0, 0)
            octets(act, octet)

        @block.vector
        def _(dve):
            dve.wait_ge(pool_const, 4)
            nc.vector.tensor_copy(ident_bf[:], ident[:]).then_inc(dve_const, 1)
            for stack in (*Qs, *Ks):
                nc.vector.memset(stack[:, :, T:TP], 0.0).then_inc(pads_ready, 1)
            dve.wait_ge(const_in, 16 * N_WEIGHTS)
            nc.vector.tensor_scalar(wqkv[:, :, 0, :], wqkv[:, :, 0, :], HS ** -0.5, None, ALU.mult)
            nc.vector.tensor_scalar(qkb[:, 0, :], qkb[:, 0, :], HS ** -0.5, None, ALU.mult).then_inc(prep, 1)
            dve.wait_ge(scale_ready, 1)
            dve.wait_ge(vec_in, 16)
            nc.vector.tensor_tensor(bn_scale[:], gamma, pv[:, 0, 0:D], ALU.mult).then_inc(dve_const, 1)
            dve.wait_ge(dve_const, 2)
            nc.vector.tensor_tensor(bn_shift[:], mean, bn_scale[:], ALU.mult).then_inc(dve_const, 1)
            dve.wait_ge(dve_const, 3)
            nc.vector.tensor_tensor(bn_shift[:], beta, bn_shift[:], ALU.subtract).then_inc(dve_const, 1)
            nc.vector.memset(oT_raw[:, :, T:TP], 1.0)
            nc.vector.memset(n2T[:, :, T:TP], 0.0)
            for p in range(2):
                nc.vector.memset(V[p][:], 0.0).then_inc(dve_const, 1)
            dve.wait_ge(dve_const, 6)
            for p in range(2):
                nc.vector.memset(V[p][:, :, :, HS:HS + 1], 1.0).then_inc(v_const, 1)
            dve.wait_ge(route_init, 11)

            def after(s, k):
                dve.wait_ge(rt_chain, ROUTE_OPS * (s - 1) + k)

            def route_logits(s, p):
                nc.vector.tensor_scalar(n2s[1 - p][:, :, C_PLACE:C_PLACE + TOPK], n2s[1 - p][:, :, C_PLACE:C_PLACE + TOPK], float(2 * TOPK * T), None,
                                        ALU.add).then_inc(rt_chain, 1)
                dve.wait_ge(logits_ready, s)
                nc.vector.tensor_copy(logit[:].rearrange("p t e -> p (t e)"), route_place(s, "lg", 0)[:, 0:NT * E]).then_inc(evac["lg"], 1)

            def route_top(s, p):
                wait_apart(dve, evac["lg"], s)
                for t in range(NT):
                    last = nc.vector.max(top8[:, t, :], logit[:, t, :])
                last.then_inc(rt_chain, 1)

            def route_index(s, p):
                wait_apart(dve, rt_chain, ROUTE_OPS * (s - 1) + 2)
                for t in range(NT):
                    last = nc.vector.max_index(idx8[:, t, :], top8[:, t, :], logit[:, t, :])
                last.then_inc(rt_chain, 1)
                nc.vector.tensor_tensor(e4[:], top8[:, :, 0:TOPK], top8[:, :, 0:1].to_broadcast([128, NT, TOPK]),
                                        ALU.subtract).then_inc(margin_ready, 1)

            def route_onehot(s, p):
                after(s, 3)
                nc.vector.tensor_copy(idxf[:], idx8[:, :, 0:TOPK]).then_inc(rt_chain, 1)
                nc.vector.tensor_copy(n2s[1 - p][:, :, C_EXPERT:C_EXPERT + TOPK], idx8[:, :, 0:TOPK]).then_inc(rt_chain, 1)
                after(s, 5)
                nc.vector.tensor_tensor(onehot[:], iota_e[:].unsqueeze(1).to_broadcast([128, NT * TOPK, E]),
                                        idxf[:].rearrange("p t k -> p (t k)").unsqueeze(2).to_broadcast([128, NT * TOPK, E]),
                                        ALU.is_equal).then_inc(rt_chain, 1)

            def route_chosen(s, p):
                after(s, 6)
                nc.vector.tensor_reduce(position[:], onehot[:].rearrange("p (t k) e -> p t e k", k=TOPK),
                                        AX.X, ALU.add).then_inc(rt_chain, 1)
                after(s, 7)
                nc.vector.tensor_copy(chosen[:], position[:]).then_inc(chosen_ready, 1)

            def route_weights(s, p):
                dve.wait_ge(e4_ready, s)
                nc.vector.tensor_reduce(esum[:], e4[:], AX.X, ALU.add).then_inc(rt_chain, 1)
                after(s, 8)
                nc.vector.reciprocal(esum[:], esum[:]).then_inc(rt_chain, 1)
                after(s, 9)
                nc.vector.tensor_tensor(n2s[1 - p][:, :, C_WEIGHT:C_WEIGHT + TOPK], e4[:], esum[:].unsqueeze(2).to_broadcast([128, NT, TOPK]),
                                        ALU.mult).then_inc(rt_chain, 1)

            def route_positions(s, p):
                w = route_place(s, "rk", 0)
                dve.wait_ge(ranks_ready, s)
                dve.wait_ge(chosen_ready, s)
                nc.vector.tensor_tensor(position[:], w[:, 0:NT * E].rearrange("p (t e) -> p t e", t=NT),
                                        next_row[:, 1:NE].unsqueeze(1).to_broadcast([128, NT, E]), ALU.add).then_inc(rt_chain, 1)
                after(s, 11)
                nc.vector.tensor_tensor(next_row[:, 1:NE], next_row[:, 1:NE], w[:, NT * E:(NT + 1) * E],
                                        ALU.add).then_inc(evac["rk"], 1)
                nc.vector.tensor_tensor(picked[:].rearrange("p (t k) e -> p t k e", k=TOPK),
                                        onehot[:].rearrange("p (t k) e -> p t k e", k=TOPK),
                                        position[:].unsqueeze(2).to_broadcast([128, NT, TOPK, E]), ALU.mult).then_inc(rt_chain, 1)
                after(s, 12)
                nc.vector.tensor_reduce(row_f[:], picked[:], AX.X, ALU.add).then_inc(rt_chain, 1)
                after(s, 13)
                wait(dve, rows_sent, 16 * NT * TOPK * (s - 1))
                wait(dve, shared_sent, 16 * NT * (s - 1))
                nc.vector.tensor_copy(row_i[:], row_f[:]).then_inc(position_ready, 1)

            def step(s, p, F, M, X, R):
                f, m = s + 2, s + 1

                def bank(name, k):
                    return work[:, plan(s, name, k)[0], :]

                def maxima(h):
                    dve.wait_ge(mxa_ready, H * m + h + 1)
                    nc.vector.tensor_reduce(nmax[:, 2, h:h + 1], mx[:, 0, 0:T], AX.X, ALU.max, negate=True).then_inc(mxa_done, 1)
                    dve.wait_ge(mxb_ready, H * m + h + 1)
                    nc.vector.tensor_reduce(nmax[:, 0, h:h + 1], mx[:, 1, 0:128], AX.X, ALU.max, negate=True)
                    nc.vector.tensor_reduce(nmax[:, 1, h:h + 1], mx[:, 1, 128:384], AX.X, ALU.max, negate=True).then_inc(mxb_done, 1)

                def conv_evac(t):
                    n = NT * f + t
                    dve.wait_ge(conv_ready, n + 1)
                    nc.vector.tensor_tensor(u1[0:ROWS[t], t % 2, :], bank("conv", t)[0:ROWS[t], 0:D], conv_b[0:ROWS[t]],
                                            ALU.add).then_inc(evac["conv"], 1)
                    dve.wait_ge(evac["conv"], n + 1)
                    wait(dve, h_ready, n - 1)
                    nc.vector.scalar_tensor_tensor(out=u2[0:ROWS[t], t % 2, :], in0=u1[0:ROWS[t], t % 2, :], scalar=0.0,
                                                   in1=bn_scale[0:ROWS[t]], op0=ALU.max, op1=ALU.mult).then_inc(bn_ready, 1)

                def ln1_stats(t):
                    n = NT * f + t
                    wait_apart(dve, h_ready, n + 1)
                    nc.vector.bn_stats(stats[0:ROWS[t], t, :], hcur[0:ROWS[t], t, :]).then_inc(ln_chain, 1)
                    wait_apart(dve, ln_chain, 3 * n + 1)
                    nc.vector.bn_aggr(mv[0:ROWS[t], t, :], stats[0:ROWS[t], t, :]).then_inc(ln_chain, 1)
                    dve.wait_ge(ln_chain, 3 * n + 2)
                    nc.vector.tensor_scalar(mv[0:ROWS[t], t, 1:2], mv[0:ROWS[t], t, 1:2], EPS, None, ALU.add).then_inc(ln_chain, 1)

                def ln1_norm(t):
                    n = NT * f + t
                    dve.wait_ge(rstd_ready, n + 1)
                    nc.vector.tensor_scalar(n1[0:ROWS[t], t, :], hcur[0:ROWS[t], t, :], mv[0:ROWS[t], t, 0:1],
                                            rstd[0:ROWS[t], t:t + 1], ALU.subtract, ALU.mult).then_inc(n1_ready, 1)

                def residue(u):
                    half, qk = u // 2, u % 2
                    dve.wait_ge(p1_ready, 4 * f + u + 1)
                    wait(dve, parts_ready, 4 * f + u - 1)
                    nc.vector.scalar_tensor_tensor(out=r1[:, u % 2, :], in0=bank("qk", u)[:, 0:T], scalar=qkb[:, qk, half:half + 1],
                                                   in1=qkp[:, qk, 0, half, :], op0=ALU.add, op1=ALU.subtract
                                                   ).then_inc(evac["qk"], 1)

                def split_maxima(half):
                    n = 8 * m + 4 * half
                    src = nmax[:, :, half * HH:(half + 1) * HH]
                    dve.wait_ge(mxa_done, H * m + (half + 1) * HH)
                    dve.wait_ge(mxb_done, H * m + (half + 1) * HH)
                    wait(dve, nmt_ready, 2 * m + half)
                    nc.vector.tensor_copy(nm_parts[:, :, 0, :], src).then_inc(nm_chain, 1)
                    dve.wait_ge(nm_chain, n + 1)
                    nc.vector.tensor_tensor(nm_res[:], src, nm_parts[:, :, 0, :], ALU.subtract).then_inc(nm_chain, 1)
                    dve.wait_ge(nm_chain, n + 2)
                    nc.vector.tensor_copy(nm_parts[:, :, 1, :], nm_res[:]).then_inc(nm_chain, 1)
                    dve.wait_ge(nm_chain, n + 3)
                    nc.vector.tensor_tensor(nm_parts[:, :, 2, :], nm_res[:], nm_parts[:, :, 1, :], ALU.subtract).then_inc(nm_chain, 1)

                def normalise(g):
                    dve.wait_ge(rawt_ready, GROUPS * s + g + 1)
                    if g:
                        dve.wait_ge(evac["onorm"], GROUPS * s + g)
                    w = bank("onorm", g)[:, 0:TP].rearrange("p (t j e) -> p t j e", t=NT, j=4)
                    nc.vector.reciprocal(rden[:], w[:, :, :, HS]).then_inc(rden_ready, 1)
                    dve.wait_ge(rden_ready, GROUPS * s + g + 1)
                    nc.vector.tensor_tensor(
                        o[:, :, 64 * g:64 * (g + 1)].rearrange("p t (j d) -> p t j d", j=4), w[:, :, :, 0:HS],
                        rden[:].unsqueeze(3).to_broadcast([128, NT, 4, HS]), ALU.mult).then_inc(evac["onorm"], 1)

                def residual(t):
                    r, n = ROWS[t], NT * s + t
                    row = resid[0:r, bass.ds(n, 1), :].rearrange("p a d -> p (a d)")
                    dve.wait_ge(out_ready, n + 1)
                    nc.vector.tensor_tensor(row, bank("out", t)[0:r, 0:D], row, ALU.add).then_inc(evac["out"], 1)
                    wait_apart(dve, evac["out"], n + 1)
                    nc.vector.bn_stats(stats2[0:r, t, :], row).then_inc(ln2_chain, 1)
                    wait_apart(dve, ln2_chain, 3 * n + 1)
                    nc.vector.bn_aggr(mv2[0:r, t, :], stats2[0:r, t, :]).then_inc(ln2_chain, 1)
                    dve.wait_ge(ln2_chain, 3 * n + 2)
                    nc.vector.tensor_scalar(mv2[0:r, t, 1:2], mv2[0:r, t, 1:2], EPS, None, ALU.add).then_inc(ln2_chain, 1)

                def ln2_norm(t):
                    r, n = ROWS[t], NT * s + t
                    dve.wait_ge(rstd2_ready, n + 1)
                    nc.vector.tensor_scalar(n2s[p][0:r, t, 0:D], resid[0:r, bass.ds(n, 1), :].rearrange("p a d -> p (a d)"),
                                            mv2[0:r, t, 0:1], rstd2[0:r, t:t + 1],
                                            ALU.subtract, ALU.mult).then_inc(n2_ready, 1)

                for h in range(H):
                    if F and not M and h == 7:
                        dve.wait_ge(fold_ready, 1)
                        nc.vector.tensor_tensor(out_b, out_b, pv[:, 0, 0:D], ALU.add).then_inc(bias_ready, 1)
                    if M:
                        maxima(h)
                    if R and h == 6:
                        route_logits(s, p)
                    if R and h == 7:
                        route_top(s, p)
                    if R and h == 8:
                        route_index(s, p)
                    if R and h == 9:
                        route_onehot(s, p)
                    if R and h == 10:
                        route_chosen(s, p)
                    if R and h == 11:
                        route_weights(s, p)
                    if R and h == 13:
                        route_positions(s, p)
                    if F and 2 <= h < 5:
                        conv_evac(h - 2)
                    if F and 3 <= h < 6:
                        ln1_stats(h - 3)
                    if F and 4 <= h < 7:
                        ln1_norm(h - 4)
                    if X and h == 5:
                        normalise(0)
                    if M and h == 8:
                        split_maxima(0)
                    if X and h == 9:
                        normalise(1)
                    if F and h in (10, 11):
                        residue(h - 10)
                    if X and h == 13:
                        normalise(2)
                    if F and h == 14:
                        residue(2)
                if F:
                    residue(3)
                if M:
                    split_maxima(1)
                if X:
                    normalise(3)
                if X:
                    for t in range(NT):
                        residual(t)
                if X:
                    for t in range(NT):
                        ln2_norm(t)
            steps(dve, step)

            def slots_table(k):
                if k == 0:
                    dve.wait_ge(rows_no_ready, 1)
                    nc.vector.tensor_tensor(count[:], mx[0:NE, 1, 0:1], region_start[:], ALU.subtract).then_inc(tb_chain, 1)
                    dve.wait_ge(tb_chain, 1)
                    nc.vector.tensor_scalar(needs[:], tile_start[:], count[:, 0:1], None, ALU.is_lt).then_inc(tb_chain, 1)
                    dve.wait_ge(tb_chain, 2)
                    nc.vector.tensor_reduce(tiles[:], needs[:], AX.X, ALU.add).then_inc(tb_chain, 1)
                    dve.wait_ge(tb_chain, 3)
                    nc.vector.tensor_scalar(step_row[:], tiles[:].to_broadcast([NE, 128]), -128.0, float(REGION),
                                            ALU.mult, ALU.add).then_inc(tb_chain, 1)
                elif k == 1:
                    dve.wait_ge(last_ready, 1)
                    nc.vector.tensor_copy(last_slot[:], mx[0:NE, 1, 0:1]).then_inc(tb_chain, 1)
                    dve.wait_ge(tb_chain, 5)
                    nc.vector.tensor_scalar(past[:], slot_no[:], last_slot[:, 0:1], None, ALU.is_ge).then_inc(tb_chain, 1)
                    nc.vector.memset(slot_expert_i[:, 0:2], 0.0)
                    nc.vector.memset(slot_expert_i[:, SLOTS + 2:], 0.0)
                else:
                    dve.wait_ge(slots_ready, 1)
                    nc.vector.tensor_scalar(slot_expert_i[:, 2:SLOTS + 2], mx[0:1, 1, 0:SLOTS], float(NE - 1), None,
                                            ALU.min).then_inc(table_ready, 1)
                    nc.vector.tensor_scalar(slot_pick[:], mx[:, 1, 0:SLOTS], -1.0, None, ALU.add).then_inc(tb_chain, 1)
                    nc.vector.tensor_tensor(slot_row[:], mx[0:1, 1, 256:256 + SLOTS], slot_offset[:], ALU.add).then_inc(tb_chain, 1)
                    dve.wait_ge(tb_chain, 8)
                    nc.vector.tensor_scalar(slot_row_i[:], slot_row[:], float(NE * REGION), None, ALU.min).then_inc(table_ready, 1)

            def copy_hiddenT(j, u):
                dve.wait_ge(hiddent_ready, j + 1)
                wait(dve, y_ready, j - 1)
                nc.vector.tensor_copy(hiddenT[:, u % 2, :], mx[:, 0, 0:128]).then_inc(hiddenT_copied, 1)

            def gated(j, u):
                dve.wait_ge(silu_ready, j + 1)
                wait(dve, hiddent_ready, j - 1)
                nc.vector.tensor_tensor(hidden[:, u % 2, :], silu[:, u % 2, :], ex[:, u % 2, HID:2 * HID],
                                        ALU.mult).then_inc(hidden_ready, 1)

            def places(q, u):
                j = DEEP * q + u
                dve.wait_ge(rows_in[u], 16 * (q + 1))
                wait(dve, place_chain, 2 * (j - SHARED))
                nc.vector.scalar_tensor_tensor(
                    out=hits[:], in0=rows[:, u, C_EXPERT:C_EXPERT + TOPK].unsqueeze(1).to_broadcast([128, 2, TOPK]),
                    scalar=slot_pick[:, bass.ds(j, 1)], in1=rows[:, u, C_WEIGHT:C_WEIGHT + 2 * TOPK].rearrange("p (a k) -> p a k", a=2),
                    op0=ALU.is_equal, op1=ALU.mult).then_inc(place_chain, 1)
                dve.wait_ge(place_chain, 2 * (j - SHARED) + 1)
                if not isinstance(q, int) or q > SHARED_OCTETS:
                    dve.wait_ge(result_sent[u], 16 * (q - SHARED_OCTETS))
                nc.vector.tensor_reduce(factor[:, u, :], hits[:], AX.X, ALU.add).then_inc(place_chain, 1)
                dve.wait_ge(place_chain, 2 * (j - SHARED) + 2)
                nc.vector.tensor_tensor(place_i[:, u:u + 1], factor[:, u, 1:2], rows[:, u, C_OUTSIDE:C_OUTSIDE + 1],
                                        ALU.add).then_inc(place_ready, 1)

            def scale(j, u):
                dve.wait_ge(y_ready, j + 1)
                if isinstance(j, int) and j < SHARED:
                    r = ROWS[j % NT]
                    nc.vector.tensor_tensor(resid[0:r, j, :], pv[0:r, u % 2, 0:D], resid[0:r, j, :], ALU.add).then_inc(y_scaled, 1)
                    return
                nc.vector.tensor_scalar(scaled[:, u % DEEP, :], pv[:, u % 2, 0:D], factor[:, u % DEEP, 0:1], None, ALU.mult).then_inc(y_scaled, 1)

            def octet(q, n, first, last):
                for u in range(n):
                    j = DEEP * q + u
                    if not (first and u < 1):
                        copy_hiddenT(j - 1, u - 1)
                    gated(j, u)
                    if not (first and u < 2):
                        scale(j - 2, u - 2)
                    if not (last and u == n - 1):
                        if not isinstance(j, int) or j + 1 >= SHARED:
                            places(q + (u + 1) // DEEP, (u + 1) % DEEP)
                    if isinstance(j, int):
                        if j == 3:
                            route_logits(B, 0)
                        if j == 4:
                            route_top(B, 0)
                            route_index(B, 0)
                        if j == 5:
                            route_onehot(B, 0)
                            route_chosen(B, 0)
                        if j == 6:
                            route_weights(B, 0)
                        if j == 7:
                            route_positions(B, 0)
                            dve.wait_ge(evac["rk"], B)
                            nc.vector.tensor_copy(next_row_i[:], next_row[0:1, :]).then_inc(counted, 1)
                        if j in (8, 10, 12):
                            slots_table((j - 8) // 2)
                if last:
                    copy_hiddenT(SLOTS - 1, n - 1)
                    scale(SLOTS - 2, n - 2)
                    scale(SLOTS - 1, n - 1)
            octets(dve, octet)

            def combine(b, t, first):
                r, n = ROWS[t], NT * b + t
                dve.wait_ge(yc_in[t], 16 * (b + 1))
                nc.vector.tensor_tensor(yc[0:r, t, 0:D], yc[0:r, t, 0:D], yc[0:r, t, D:2 * D], ALU.add).then_inc(half_ready, 1)
                dve.wait_ge(half_ready, n + 1)
                nc.vector.tensor_tensor(yc[0:r, t, 0:D], yc[0:r, t, 0:D], yc[0:r, t, 2 * D:3 * D], ALU.add).then_inc(total_chain, 1)
                dve.wait_ge(total_chain, n + 1)
                dve.wait_ge(shared_ready, n + 1)
                nc.vector.tensor_tensor(total[0:r, t, :], total[0:r, t, :], yc[0:r, t, 0:D], ALU.add).then_inc(total_ready, 1)

            for t in range(NT):
                combine(0, t, True)
            with dve.Fori(1, B) as b:
                for t in range(NT):
                    combine(b, t, False)

        @block.gpsimd
        def _(pool):
            nc.gpsimd.memset(ident[:], 0.0).then_inc(pool_const, 1)
            nc.gpsimd.memset(mask_bf[:], 0.0).then_inc(pool_const, 1)
            pool.wait_ge(pool_const, 2)
            nc.gpsimd.affine_select(out=ident[:], in_=ident[:], pattern=[[-1, 128]], compare_op=ALU.not_equal, fill=1.0,
                                    base=0, channel_multiplier=1).then_inc(pool_const, 1)
            nc.gpsimd.affine_select(out=mask_bf[:], in_=mask_bf[:], pattern=[[0, 2], [-1, 128]], compare_op=ALU.is_ge,
                                    fill=NEG, base=0, channel_multiplier=1).then_inc(pool_const, 1)
            nc.gpsimd.iota(iota_e[:], pattern=[[1, E]], base=0, channel_multiplier=0,
                           allow_small_or_imprecise_dtypes=True).then_inc(pool_const, 1)
            nc.gpsimd.memset(neg_half[:], -0.5).then_inc(pool_const, 1)
            pool.wait_ge(var_in, 16)
            nc.gpsimd.tensor_scalar(var_col, var_col, EPS, None, ALU.add).then_inc(pool_const, 1)
            pool.wait_ge(pool_const, 7)
            nc.gpsimd.tensor_tensor(var_col, var_col, neg_half[:].to_broadcast([128, KC]), ALU.pow).then_inc(deviation_ready, 1)
            nc.gpsimd.memset(tri_bf[:], 1.0).then_inc(route_const, 1)
            nc.gpsimd.memset(ones_bf[:], 1.0).then_inc(route_const, 1)
            pool.wait_ge(route_const, 1)
            nc.gpsimd.affine_select(out=tri_bf[:], in_=tri_bf[:], pattern=[[1, 128]], compare_op=ALU.is_gt,
                                    fill=0.0, base=0, channel_multiplier=-1).then_inc(route_const, 1)
            nc.gpsimd.memset(padding[:], 0.0).then_inc(pad_const, 1)
            pool.wait_ge(pad_const, 1)
            nc.gpsimd.memset(padding[:, C_EXPERT:C_EXPERT + TOPK], -2.0).then_inc(pad_const, 1)
            nc.gpsimd.memset(padding[:, C_OUTSIDE:C_OUTSIDE + 1], float(B * T * TOPK)).then_inc(pad_const, 1)
            nc.gpsimd.memset(n2s[0][:], 0.0).then_inc(pad_const, 1)
            nc.gpsimd.memset(n2s[1][:], 0.0).then_inc(pad_const, 1)
            pool.wait_ge(pad_const, 5)
            for p, n2 in enumerate(n2s):
                nc.gpsimd.iota(n2[:, :, C_PLACE:C_PLACE + TOPK], pattern=[[TOPK * 128, NT], [1, TOPK]], base=TOPK * T * (p - 2),
                               channel_multiplier=TOPK, allow_small_or_imprecise_dtypes=True).then_inc(route_init, 1)
            for dst, pattern, per_partition in (
                    (slot_no[:], [[1, SLOTS]], 0), (slot_offset[:], [[128, SLOTS]], 0), (tile_start[:], [[128, TILES_OF_ONE]], 0),
                    (region_start[:], [[0, 1]], REGION), (next_row[:], [[REGION, NE]], 0), (up_to[:], [[1, NE]], -1)):
                nc.gpsimd.iota(dst, pattern=pattern, base=0, channel_multiplier=per_partition,
                               allow_small_or_imprecise_dtypes=True).then_inc(route_init, 1)
            nc.gpsimd.memset(ones_f[:], 1.0).then_inc(route_init, 1)
            pool.wait_ge(route_init, 9)
            nc.gpsimd.tensor_scalar(up_to[:], up_to[:], 0.0, None, ALU.is_ge).then_inc(route_init, 1)
            nc.gpsimd.memset(next_row[:, 0:1], float(B * T)).then_inc(route_init, 1)
            pool.wait_ge(dve_const, 4)

            def send(n2, n):
                t = n // TOPK
                nc.gpsimd.indirect_dma_start(
                    out=expert_rows, out_offset=bass.IndirectOffsetOnAxis(ap=row_i[0:ROWS[t], n:n + 1], axis=0),
                    in_=n2[0:ROWS[t], t, :], in_offset=None).then_inc(rows_sent, 16)

            def step(s, p, F, M, X, R):
                f = s + 2

                def mask(h):
                    wait_apart(pool, exp_done, H * s + h + 1)
                    blocks = P[:, h % 8, :, 0:128]
                    nc.gpsimd.affine_select(out=blocks, in_=blocks, pattern=[[0, 2], [1, 128]], compare_op=ALU.is_ge,
                                            fill=0.0, base=0, channel_multiplier=-1)
                    block = P[:, h % 8, 1, T - 128:T]
                    nc.gpsimd.affine_select(out=block, in_=block, pattern=[[1, 128]], compare_op=ALU.is_ge,
                                            fill=0.0, base=0, channel_multiplier=-1).then_inc(masked, 1)

                def shift(t):
                    r, n = ROWS[t], NT * f + t
                    pool.wait_ge(bn_ready, n + 1)
                    nc.gpsimd.tensor_tensor(hcur[0:r, t, :], u2[0:r, t % 2, :], bn_shift[0:r], ALU.add).then_inc(h_ready, 1)
                    if M:
                        add_bias(t)

                def add_bias(t):
                    r, n = ROWS[t], NT * f + t
                    pool.wait_ge(h_ready, n + 1)
                    nc.gpsimd.tensor_tensor(resid[0:r, bass.ds(n, 1), :].rearrange("p a d -> p (a d)"), hcur[0:r, t, :],
                                            out_b[0:r], ALU.add).then_inc(resid_ready, 1)

                def inverse_deviation(t, chain, moments, out, n, ready):
                    pool.wait_ge(chain, 3 * n + 3)
                    nc.gpsimd.tensor_tensor(out[0:ROWS[t], t:t + 1], moments[0:ROWS[t], t, 1:2], neg_half[0:ROWS[t]],
                                            ALU.pow).then_inc(ready, 1)

                def parts(u):
                    half, qk, n = u // 2, u % 2, 4 * f + u
                    pool.wait_ge(p2_done, n + 1)
                    nc.gpsimd.tensor_tensor(qkp[:, qk, 2, half, :], r1[:, u % 2, :], qkp[:, qk, 1, half, :],
                                            ALU.subtract).then_inc(parts_ready, 1)

                late = X and (not isinstance(s, int) or s >= 2)
                now = R and isinstance(s, int) and s >= B - 1
                if late:
                    wait_apart(pool, position_ready, s - 1)
                for h in range(H):
                    if X:
                        mask(h)
                    n = h if M else h - 4
                    if late and 0 <= n < NT * TOPK:
                        send(n2s[p], n)
                    if F and 2 <= h < 5:
                        shift(h - 2)
                    if F and 3 <= h < 6:
                        inverse_deviation(h - 3, ln_chain, mv, rstd, NT * f + h - 3, rstd_ready)
                    if F and h in (11, 12):
                        parts(h - 11)
                if F:
                    parts(2)
                    parts(3)
                if F and not M:
                    pool.wait_ge(bias_ready, 1)
                    for t in range(NT):
                        add_bias(t)
                    pool.wait_ge(resid_ready, NT)

                if now:
                    wait_apart(pool, position_ready, s)
                    for n in range(TOPK):
                        send(n2s[1 - p], n)
                if X:
                    for t in range(NT):
                        inverse_deviation(t, ln2_chain, mv2, rstd2, NT * s + t, rstd2_ready)
                if now:
                    for n in range(TOPK, NT * TOPK):
                        send(n2s[1 - p], n)
            steps(pool, step)

            pool.wait_ge(position_ready, B)
            for n in range(NT * TOPK):
                send(n2s[1], n)

            def octet(q, n):
                for u in range(n):
                    wait_apart(pool, y_scaled, DEEP * q + u + 1)
                    nc.gpsimd.indirect_dma_start(
                        out=results, out_offset=bass.IndirectOffsetOnAxis(ap=place_i[:, u:u + 1], axis=0),
                        in_=scaled[:, u, :], in_offset=None, bounds_check=B * T * TOPK - 1, oob_is_err=False
                    ).then_inc(result_sent[u], 16)
            octet(SHARED_OCTETS, DEEP)
            with pool.Fori(SHARED_OCTETS + 1, OCTETS - 1) as q:
                octet(q, DEEP)
            octet(OCTETS - 1, SLOTS - DEEP * (OCTETS - 1))

            def shared(b, t, first):
                r, n = ROWS[t], NT * b + t
                pool.wait_ge(yc_in[t], 16 * (b + 1))
                if not first:
                    pool.wait_ge(out_sent[t], 16 * b)
                nc.gpsimd.tensor_tensor(total[0:r, t, :], yc[0:r, t, 3 * D:4 * D],
                                        resid[0:r, bass.ds(n, 1), :].rearrange("p a d -> p (a d)"), ALU.add).then_inc(shared_ready, 1)

            for t in range(NT):
                shared(0, t, True)
            with pool.Fori(1, B) as b:
                for t in range(NT):
                    shared(b, t, False)


def kernel(x, L0_tok_W, L0_tok_b, L0_tok_gamma, L0_tok_beta, L0_tok_running_mean, L0_tok_running_var,
           L0_attn_attn_W, L0_attn_attn_b, L0_attn_out_W, L0_attn_out_b,
           L0_ffn_gate_w, L0_ffn_w1, L0_ffn_w3, L0_ffn_w2, L0_ffn_sw1, L0_ffn_sw3, L0_ffn_sw2):
    import concourse.bacc as _bacc
    from concourse.bass_utils import run_bass_kernel_spmd as _run

    qkv_w = np.asarray(L0_attn_attn_W).reshape(D, H, 3, HS)
    qkv_b = np.asarray(L0_attn_attn_b).reshape(H, 3, HS)
    w13 = np.concatenate([np.concatenate([np.asarray(L0_ffn_sw1), np.asarray(L0_ffn_sw3)], 0)[None],
                          np.concatenate([np.asarray(L0_ffn_w1), np.asarray(L0_ffn_w3)], 1)], 0)
    w2 = np.concatenate([np.asarray(L0_ffn_sw2)[None], np.asarray(L0_ffn_w2)], 0)
    arrays = {
        "xT": np.asarray(x).transpose(0, 2, 1),
        "convw": np.asarray(L0_tok_W).reshape(D, CONTEXT, FEAT).transpose(2, 1, 0),
        "vec": np.concatenate([np.asarray(a).ravel() for a in (
            L0_tok_b, L0_tok_gamma, L0_tok_beta, L0_tok_running_mean, L0_tok_running_var, L0_attn_out_b)]),
        "cols": np.stack([np.asarray(L0_tok_running_var), qkv_b[:, 2, :].ravel()]).reshape(2, KC, 128).transpose(2, 0, 1),
        "qkb": qkv_b[:, 0:2, :].transpose(1, 0, 2).reshape(2, KC, 128).transpose(2, 0, 1),
        "wqkv": qkv_w.transpose(0, 2, 1, 3).reshape(KC, 128, 3, D).transpose(1, 0, 2, 3),
        "wo": np.asarray(L0_attn_out_W).reshape(KC, 128, D).transpose(1, 0, 2),
        "gate": np.asarray(L0_ffn_gate_w).T.reshape(KC, 128, E).transpose(1, 0, 2),
        "w13": w13.transpose(2, 0, 1).reshape(KC, 128, NE, 2 * HID).transpose(1, 0, 2, 3),
        "w2": w2.transpose(2, 0, 1),
    }
    arrays = {k + "_in": np.ascontiguousarray(v) for k, v in arrays.items()}
    nc = _bacc.Bacc("TRN2", target_bir_lowering=False, num_devices=1)
    args = [nc.dram_tensor(n, a.shape, F32, kind="ExternalInput").ap() for n, a in arrays.items()]
    out = nc.dram_tensor("out", (B * T, D), F32, kind="ExternalOutput").ap()
    build(nc, *args, out)
    r = _run(nc, [arrays], core_ids=[0])
    return r.results[0]["out"].reshape(B, T, D)
```
